# Optimizing a Trainium2 kernel written in Bass

```python
import numpy as np
import jax
import jax.numpy as jnp

def _softmax(x, axis=-1):
    return jax.nn.softmax(x, axis=axis)

def _gelu(x):
    return jax.nn.gelu(x, approximate=True)

def _silu(x):
    return jax.nn.silu(x)

def _sigmoid(x):
    return jax.nn.sigmoid(x)

def _layernorm(x, axis=-1, eps=1e-05):
    m = jnp.mean(x, axis=axis, keepdims=True)
    v = jnp.var(x, axis=axis, keepdims=True)
    return (x - m) / jnp.sqrt(v + eps)

def _scatter_add(tgt, idx, src, axis=0):
    return tgt.at[idx].add(src)

def _segment_sum(src, seg, n):
    return jax.ops.segment_sum(src, seg, n)
kernel_name = 'mk_macaron_d2_jaxref_r8_21c4e0'

def setup_inputs(seed: int=0):
    np.random.seed(seed)
    _w = jnp.asarray

    def _L0_attn_setup():
        import jax, jax.numpy as jnp
        import numpy as np
        D_MODEL = 256
        N_HEADS = 16
        N_KV_HEADS = 2
        D_HEAD = D_MODEL // N_HEADS
        N_GROUPS = N_HEADS // N_KV_HEADS
        B, T = (2, 256)
        key = jax.random.key(seed)
        ks = jax.random.split(key, 9)
        s = 0.02
        return {'x': jax.random.normal(ks[0], (B, T, D_MODEL), jnp.float32), 'Wq': jax.random.normal(ks[1], (D_MODEL, N_HEADS * D_HEAD), jnp.float32) * s, 'bq': jnp.zeros((N_HEADS * D_HEAD,), jnp.float32), 'Wk': jax.random.normal(ks[2], (D_MODEL, N_KV_HEADS * D_HEAD), jnp.float32) * s, 'bk': jnp.zeros((N_KV_HEADS * D_HEAD,), jnp.float32), 'Wv': jax.random.normal(ks[3], (D_MODEL, N_KV_HEADS * D_HEAD), jnp.float32) * s, 'bv': jnp.zeros((N_KV_HEADS * D_HEAD,), jnp.float32), 'Wo': jax.random.normal(ks[4], (D_MODEL, D_MODEL), jnp.float32) * s, 'bo': jnp.zeros((D_MODEL,), jnp.float32)}
    _L0_attn_in = _L0_attn_setup()

    def _L0_ffn_setup():
        import jax, jax.numpy as jnp
        import numpy as np
        B, T, D = (4, 128, 256)
        N, S, H = (8, 8, 8)
        ETA = 1.0
        key = jax.random.key(seed)
        ks = jax.random.split(key, 9)
        return {'x': jax.random.normal(ks[0], (B, T, D), jnp.float32), 'select_weight': jax.random.normal(ks[1], (N, D, S), jnp.float32) / D, 'select_mean_diff': jax.random.normal(ks[2], (N, D), jnp.float32) / D, 'imp_center': jax.random.normal(ks[3], (N,), jnp.float32), 'imp_slope': jax.random.normal(ks[4], (N,), jnp.float32) * 5.0, 'lora_update': jax.random.normal(ks[5], (N, D, H), jnp.float32) * 0.02, 'lora_degen': jax.random.normal(ks[6], (N, D, H), jnp.float32) * 0.02, 'bias_w': jax.random.normal(ks[7], (N, D), jnp.float32) * 0.02, 'debias_w': jax.random.normal(ks[8], (N, D), jnp.float32) * 0.02}
    _L0_ffn_in = _L0_ffn_setup()

    def _L1_attn_setup():
        import jax, jax.numpy as jnp
        import numpy as np
        HIDDEN = 256
        N_HEADS = 16
        N_KV_HEADS = 4
        HEAD_DIM = 128
        THETA = 10000.0
        MASK_NEG = -2.3819763e+38

        def apply_rotary_emb(x, theta=THETA):
            B, S, H, D = x.shape
            half = D // 2
            freqs = 1.0 / theta ** (jnp.arange(0, D, 2, dtype=jnp.float32) / D)
            ang = jnp.arange(S, dtype=jnp.float32)[:, None] * freqs[None, :]
            cos = jnp.cos(ang)[None, :, None, :]
            sin = jnp.sin(ang)[None, :, None, :]
            xf = x.astype(jnp.float32)
            x1, x2 = (xf[..., :half], xf[..., half:])
            real = x1 * cos - x2 * sin
            imag = x1 * sin + x2 * cos
            return jnp.concatenate([real, imag], axis=-1).astype(x.dtype)
        key = jax.random.key(seed)
        k1, k2, k3 = jax.random.split(key, 3)
        B, S = (2, 256)
        lim_qkv = 1.0 / np.sqrt(HIDDEN)
        lim_o = 1.0 / np.sqrt(N_HEADS * HEAD_DIM)
        x = jax.random.normal(k1, (B, S, HIDDEN), dtype=jnp.float32)
        Wqkv = jax.random.uniform(k2, (HIDDEN, (N_HEADS + 2 * N_KV_HEADS) * HEAD_DIM), minval=-lim_qkv, maxval=lim_qkv, dtype=jnp.float32)
        Wo = jax.random.uniform(k3, (N_HEADS * HEAD_DIM, HIDDEN), minval=-lim_o, maxval=lim_o, dtype=jnp.float32)
        return {'x': x, 'Wqkv': Wqkv, 'Wo': Wo}
    _L1_attn_in = _L1_attn_setup()

    def _L1_ffn_setup():
        import jax, jax.numpy as jnp
        import numpy as np
        TOPK = 2
        key = jax.random.key(seed)
        ks = jax.random.split(key, 10)
        B, S, D = (2, 256, 256)
        E, I = (8, 128)
        ISH = 1 * I
        std = 0.02
        x = jax.random.normal(ks[0], (B, S, D), jnp.float32)
        gate_w = jax.random.normal(ks[1], (E, D), jnp.float32) * std
        gate_b = jnp.zeros((E,), jnp.float32)
        W1 = jax.random.normal(ks[2], (E, I, D), jnp.float32) * std
        W2 = jax.random.normal(ks[3], (E, D, I), jnp.float32) * std
        W3 = jax.random.normal(ks[4], (E, I, D), jnp.float32) * std
        Ws1 = jax.random.normal(ks[5], (ISH, D), jnp.float32) * std
        Ws2 = jax.random.normal(ks[6], (D, ISH), jnp.float32) * std
        Ws3 = jax.random.normal(ks[7], (ISH, D), jnp.float32) * std
        return {'x': x, 'gate_w': gate_w, 'gate_b': gate_b, 'W1': W1, 'W2': W2, 'W3': W3, 'Ws1': Ws1, 'Ws2': Ws2, 'Ws3': Ws3}
    _L1_ffn_in = _L1_ffn_setup()
    _d = {'L0_attn_x': _L0_attn_in['x'], 'L0_attn_Wq': _L0_attn_in['Wq'], 'L0_attn_bq': _L0_attn_in['bq'], 'L0_attn_Wk': _L0_attn_in['Wk'], 'L0_attn_bk': _L0_attn_in['bk'], 'L0_attn_Wv': _L0_attn_in['Wv'], 'L0_attn_bv': _L0_attn_in['bv'], 'L0_attn_Wo': _L0_attn_in['Wo'], 'L0_attn_bo': _L0_attn_in['bo'], 'L0_ffn_select_weight': _L0_ffn_in['select_weight'], 'L0_ffn_select_mean_diff': _L0_ffn_in['select_mean_diff'], 'L0_ffn_imp_center': _L0_ffn_in['imp_center'], 'L0_ffn_imp_slope': _L0_ffn_in['imp_slope'], 'L0_ffn_lora_update': _L0_ffn_in['lora_update'], 'L0_ffn_lora_degen': _L0_ffn_in['lora_degen'], 'L0_ffn_bias_w': _L0_ffn_in['bias_w'], 'L0_ffn_debias_w': _L0_ffn_in['debias_w'], 'L1_attn_Wqkv': _L1_attn_in['Wqkv'], 'L1_attn_Wo': _L1_attn_in['Wo'], 'L1_ffn_gate_w': _L1_ffn_in['gate_w'], 'L1_ffn_gate_b': _L1_ffn_in['gate_b'], 'L1_ffn_W1': _L1_ffn_in['W1'], 'L1_ffn_W2': _L1_ffn_in['W2'], 'L1_ffn_W3': _L1_ffn_in['W3'], 'L1_ffn_Ws1': _L1_ffn_in['Ws1'], 'L1_ffn_Ws2': _L1_ffn_in['Ws2'], 'L1_ffn_Ws3': _L1_ffn_in['Ws3']}
    _x0 = _d['L0_attn_x']
    _d['L0_attn_x'] = jax.random.normal(jax.random.fold_in(jax.random.key(seed), 1), (1, 2048, 256), dtype=_x0.dtype)
    del _x0
    return _d

def reference(L0_attn_x, L0_attn_Wq, L0_attn_bq, L0_attn_Wk, L0_attn_bk, L0_attn_Wv, L0_attn_bv, L0_attn_Wo, L0_attn_bo, L0_ffn_select_weight, L0_ffn_select_mean_diff, L0_ffn_imp_center, L0_ffn_imp_slope, L0_ffn_lora_update, L0_ffn_lora_degen, L0_ffn_bias_w, L0_ffn_debias_w, L1_attn_Wqkv, L1_attn_Wo, L1_ffn_gate_w, L1_ffn_gate_b, L1_ffn_W1, L1_ffn_W2, L1_ffn_W3, L1_ffn_Ws1, L1_ffn_Ws2, L1_ffn_Ws3):

    def _L0_attn_ref(x, Wq, bq, Wk, bk, Wv, bv, Wo, bo):
        import jax, jax.numpy as jnp
        import numpy as np
        D_MODEL = 256
        N_HEADS = 16
        N_KV_HEADS = 2
        D_HEAD = D_MODEL // N_HEADS
        N_GROUPS = N_HEADS // N_KV_HEADS
        B, T = (2, 256)
        Bx, Tx, C = x.shape
        Q = (x @ Wq + bq).reshape(Bx, Tx, N_HEADS, D_HEAD)
        K = (x @ Wk + bk).reshape(Bx, Tx, N_KV_HEADS, D_HEAD)
        V = (x @ Wv + bv).reshape(Bx, Tx, N_KV_HEADS, D_HEAD)
        Qg = Q.reshape(Bx, Tx, N_KV_HEADS, N_GROUPS, D_HEAD)
        scale = jnp.sqrt(jnp.float32(D_HEAD))
        scores = jnp.einsum('bqkgd,bskd->bkgqs', Qg, K) / scale
        causal = jnp.triu(jnp.ones((Tx, Tx), bool), k=1)
        scores = jnp.where(causal, -jnp.inf, scores)
        attn = jax.nn.softmax(scores, axis=-1)
        out = jnp.einsum('bkgqs,bskd->bqkgd', attn, V).reshape(Bx, Tx, C)
        return out @ Wo + bo

    def _L0_ffn_ref(x, select_weight, select_mean_diff, imp_center, imp_slope, lora_update, lora_degen, bias_w, debias_w):
        import jax, jax.numpy as jnp
        import numpy as np
        B, T, D = (4, 128, 256)
        N, S, H = (8, 8, 8)
        ETA = 1.0
        x_diff = x[:, None, :, :] - select_mean_diff[None, :, None, :]
        x_diff = x_diff / jnp.linalg.norm(x_diff, axis=3, keepdims=True)
        cont = jnp.einsum('nds,bntd->bnts', select_weight, x_diff) ** 2
        score = cont.sum(axis=-1)
        gate = jax.nn.sigmoid(imp_slope[None, :, None] * (score - imp_center[None, :, None]))
        sel_scale = gate.max(axis=1)[..., None]
        sel_idx = gate.argmax(axis=1)
        debias = jnp.take(debias_w, sel_idx, axis=0)
        bias = jnp.take(bias_w, sel_idx, axis=0)
        upd = jnp.take(lora_update, sel_idx, axis=0)
        dgn = jnp.take(lora_degen, sel_idx, axis=0)
        x_debias = x - debias
        mod_x = jnp.einsum('btdh,btd->bth', upd, x_debias)
        degen_up = jnp.einsum('btdh,bth->btd', dgn, mod_x)
        mod_x_bias = ETA * (bias + degen_up)
        return (1.0 - sel_scale) * x + sel_scale * mod_x_bias

    def _L1_attn_ref(x, Wqkv, Wo):
        import jax, jax.numpy as jnp
        import numpy as np
        HIDDEN = 256
        N_HEADS = 16
        N_KV_HEADS = 4
        HEAD_DIM = 128
        THETA = 10000.0
        MASK_NEG = -2.3819763e+38

        def apply_rotary_emb(x, theta=THETA):
            B, S, H, D = x.shape
            half = D // 2
            freqs = 1.0 / theta ** (jnp.arange(0, D, 2, dtype=jnp.float32) / D)
            ang = jnp.arange(S, dtype=jnp.float32)[:, None] * freqs[None, :]
            cos = jnp.cos(ang)[None, :, None, :]
            sin = jnp.sin(ang)[None, :, None, :]
            xf = x.astype(jnp.float32)
            x1, x2 = (xf[..., :half], xf[..., half:])
            real = x1 * cos - x2 * sin
            imag = x1 * sin + x2 * cos
            return jnp.concatenate([real, imag], axis=-1).astype(x.dtype)
        B, S, _ = x.shape
        q_size = N_HEADS * HEAD_DIM
        kv_size = N_KV_HEADS * HEAD_DIM
        g = N_HEADS // N_KV_HEADS
        xqkv = x @ Wqkv
        xq = xqkv[..., :q_size].reshape(B, S, N_HEADS, HEAD_DIM)
        xk = xqkv[..., q_size:q_size + kv_size].reshape(B, S, N_KV_HEADS, HEAD_DIM)
        xv = xqkv[..., q_size + kv_size:].reshape(B, S, N_KV_HEADS, HEAD_DIM)
        xq = apply_rotary_emb(xq)
        xk = apply_rotary_emb(xk)
        xk = jnp.repeat(xk, g, axis=2)
        xv = jnp.repeat(xv, g, axis=2)
        scale = HEAD_DIM ** (-0.5)
        scores = jnp.einsum('bqhd,bkhd->bhqk', xq, xk) * scale
        causal_add = jnp.triu(jnp.full((S, S), MASK_NEG, dtype=jnp.float32), k=1)
        scores = scores + causal_add[None, None]
        probs = jax.nn.softmax(scores, axis=-1)
        attn = jnp.einsum('bhqk,bkhd->bqhd', probs, xv).reshape(B, S, q_size)
        return attn @ Wo

    def _L1_ffn_ref(x, gate_w, gate_b, W1, W2, W3, Ws1, Ws2, Ws3):
        import jax, jax.numpy as jnp
        import numpy as np
        TOPK = 2
        B, S, D = x.shape
        xt = x.reshape(-1, D)
        T = xt.shape[0]
        E = gate_w.shape[0]
        logits = xt @ gate_w.T
        scores = jax.nn.softmax(logits.astype(jnp.float32), axis=-1)
        biased = scores + gate_b
        _, idx = jax.lax.top_k(biased, TOPK)
        weights = jnp.take_along_axis(scores, idx, axis=1).astype(x.dtype)
        dw = jnp.zeros((T, E), x.dtype).at[jnp.arange(T)[:, None], idx].add(weights)
        h = jax.nn.silu(jnp.einsum('td,eid->tei', xt, W1)) * jnp.einsum('td,eid->tei', xt, W3)
        y = jnp.einsum('tei,edi,te->td', h, W2, dw)
        z = jax.nn.silu(xt @ Ws1.T) * (xt @ Ws3.T) @ Ws2.T
        return (y + z).reshape(B, S, D)
    x = L0_attn_x
    x = x + 0.5 * _L0_ffn_ref(_layernorm(x, axis=-1), L0_ffn_select_weight, L0_ffn_select_mean_diff, L0_ffn_imp_center, L0_ffn_imp_slope, L0_ffn_lora_update, L0_ffn_lora_degen, L0_ffn_bias_w, L0_ffn_debias_w)
    x = x + _L0_attn_ref(_layernorm(x, axis=-1), L0_attn_Wq, L0_attn_bq, L0_attn_Wk, L0_attn_bk, L0_attn_Wv, L0_attn_bv, L0_attn_Wo, L0_attn_bo)
    x = x + 0.5 * _L0_ffn_ref(_layernorm(x, axis=-1), L0_ffn_select_weight, L0_ffn_select_mean_diff, L0_ffn_imp_center, L0_ffn_imp_slope, L0_ffn_lora_update, L0_ffn_lora_degen, L0_ffn_bias_w, L0_ffn_debias_w)
    x = x + 0.5 * _L1_ffn_ref(_layernorm(x, axis=-1), L1_ffn_gate_w, L1_ffn_gate_b, L1_ffn_W1, L1_ffn_W2, L1_ffn_W3, L1_ffn_Ws1, L1_ffn_Ws2, L1_ffn_Ws3)
    x = x + _L1_attn_ref(_layernorm(x, axis=-1), L1_attn_Wqkv, L1_attn_Wo)
    x = x + 0.5 * _L1_ffn_ref(_layernorm(x, axis=-1), L1_ffn_gate_w, L1_ffn_gate_b, L1_ffn_W1, L1_ffn_W2, L1_ffn_W3, L1_ffn_Ws1, L1_ffn_Ws2, L1_ffn_Ws3)
    return x

_drawn_inputs = setup_inputs


def setup_inputs(seed=0):
    import zlib

    import numpy as np

    out = dict(_drawn_inputs(seed))
    spreads = {'L0_attn_bq': (0.0, 0.8),
     'L0_attn_bk': (0.0, 2.0),
     'L0_attn_bv': (0.0, 0.1),
     'L0_attn_bo': (0.0, 0.1),
     'L1_ffn_gate_b': (0.0, 0.8)}
    factors = {'L0_attn_Wq': 8.0,
     'L0_attn_Wk': 8.0,
     'L0_attn_Wv': 7.69,
     'L0_ffn_select_weight': 64.0,
     'L0_ffn_select_mean_diff': 64.0,
     'L0_ffn_lora_update': 3.139,
     'L0_ffn_lora_degen': 3.11,
     'L0_ffn_bias_w': 2.826,
     'L0_ffn_debias_w': 8.0,
     'L1_ffn_gate_w': 8.0,
     'L1_ffn_W1': 8.0,
     'L1_ffn_W2': 8.0,
     'L1_ffn_W3': 8.0,
     'L1_ffn_Ws1': 4.874,
     'L1_ffn_Ws2': 4.762,
     'L1_ffn_Ws3': 4.745}
    for name, (base, spread) in spreads.items():
        noise = np.random.default_rng([zlib.crc32(name.encode()), seed]).standard_normal(out[name].shape)
        drawn = base * np.exp(spread * noise) if base else spread * noise
        out[name] = jnp.asarray(drawn.astype(out[name].dtype))
    for name, factor in factors.items():
        out[name] = (out[name] * factor).astype(out[name].dtype)
    return out
```

```python
from contextlib import ExitStack

import concourse.bass as bass
from concourse import mybir

F32 = mybir.dt.float32
F16 = mybir.dt.float16
BF16 = mybir.dt.bfloat16
ACT = mybir.ActivationFunctionType
ALU = mybir.AluOpType
AX = mybir.AxisListType

P = 128
T = 2048
D = 256
TILES = T // P
CT = 4
CHUNK = CT * P
CHUNKS = T // CHUNK
KD = D // P
EPS = 1e-5
NEG = -1e30

N0, S0 = 8, 8
C0 = 2 * N0 * S0 + N0
R0 = N0 * S0 + N0

H0, G0, D0 = 16, 2, 16
QUAD = 4
QUADS = H0 // QUAD
VW = 32

E1, I1 = 8, 128
X1 = E1 + 1
H1, G1, D1 = 16, 4, 128
QKV1 = (H1 + 2 * G1) * D1
VO = D1 + 1
VL = D1 + 2


class Steps:

    def __init__(self, eng, sem, base=0):
        self.eng, self.sem, self.base, self.n = eng, sem, base, 0

    def mark(self, ins):
        self.n += 1
        ins.then_inc(self.sem, 1)
        return ins

    def wait(self):
        self.eng.wait_ge(self.sem, self.base + self.n)

    def link(self, ins):
        self.mark(ins)
        self.wait()


class Core:

    def __init__(self, nc, stack, prefix=""):
        self.nc, self.stack, self.prefix, self.sems = nc, stack, prefix, []
        stack.callback(self.clear)

    def clear(self):
        if self.sems:
            self.nc.clear_and_free_semaphores(self.sems)
            self.nc.all_engine_barrier()

    def sb(self, name, shape, dt=F32):
        return self.stack.enter_context(self.nc.sbuf_tensor(self.prefix + name, list(shape), dt))

    def ps(self, name, shape, dt=F32):
        return self.stack.enter_context(self.nc.psum_tensor(self.prefix + name, list(shape), dt))

    def sem(self, name):
        self.sems.append(self.nc.alloc_semaphore(self.prefix + name))
        return self.sems[-1]


def bcast(ap, shape):
    return ap.broadcast_to(list(shape))


def setup(nc, k, a):
    with ExitStack() as stack:
        m = Core(nc, stack, "su_")
        loaded, blank, made = m.sem("loaded"), m.sem("blank"), m.sem("made")
        with nc.Block() as block:

            @block.sync
            def _(sp):
                sp.dma_start(k.x[:, :, :], a["x"].rearrange("o (t p) d -> p (o t) d", p=P)).then_inc(loaded, 16)
                sp.wait_ge(loaded, 16)

            @block.gpsimd
            def _(pool):
                pool.memset(k.ident[:, :], 0.0).then_inc(blank, 1)
                pool.memset(k.identb[:, :], 0.0).then_inc(blank, 1)
                pool.memset(k.minusb[:, :], 0.0).then_inc(blank, 1)
                pool.memset(k.mask_qk[:, :], 0.0).then_inc(blank, 1)
                pool.memset(k.mask_kq[:, :], 0.0).then_inc(blank, 1)
                pool.memset(k.ones[:, :], 1.0).then_inc(made, 1)
                pool.memset(k.onesb[:, :], 1.0).then_inc(made, 1)
                pool.memset(k.eps[:, :], EPS).then_inc(made, 1)
                for n in range(N0):
                    pool.memset(k.rev[:, :, n:n + 1], float(N0 - n)).then_inc(made, 1)
                pool.wait_ge(blank, 5)
                for t, one in ((k.ident, 1.0), (k.identb, 1.0), (k.minusb, -1.0)):
                    pool.affine_select(out=t[:, :], in_=t[:, :], compare_op=ALU.not_equal, fill=one, base=0,
                                       pattern=[[-1, P]], channel_multiplier=1).then_inc(made, 1)
                pool.affine_select(out=k.mask_qk[:, :], in_=k.mask_qk[:, :], compare_op=ALU.is_ge, fill=NEG,
                                   base=0, pattern=[[-1, P]], channel_multiplier=1).then_inc(made, 1)
                pool.affine_select(out=k.mask_kq[:, :], in_=k.mask_kq[:, :], compare_op=ALU.is_ge, fill=NEG,
                                   base=0, pattern=[[1, P]], channel_multiplier=-1).then_inc(made, 1)
                pool.wait_ge(made, 3 + N0 + 5)


def norm_stats(nc, k, name):
    with ExitStack() as stack:
        m = Core(nc, stack, name)
        bn = m.sb("bn", [P, TILES, 6])
        mv = m.sb("mv", [P, TILES, 2])
        std = m.sb("std", [P, TILES])
        r0 = m.sb("r0", [P, TILES])
        vr = m.sb("vr", [P, TILES])
        half = m.sb("half", [P, TILES])
        steps, rooted = m.sem("steps"), m.sem("rooted")
        var_ready = m.sem("var_ready")
        with nc.Block() as block:

            @block.vector
            def _(dve):
                s = Steps(dve, steps)
                for t in range(TILES):
                    s.mark(dve.bn_stats(bn[:, t, :], k.x[:, t, :]))
                s.wait()
                for t in range(TILES):
                    ins = dve.bn_aggr(mv[:, t, :], bn[:, t, :])
                    if t < TILES - 1:
                        s.mark(ins)
                ins.then_inc(var_ready, 1)
                dve.wait_ge(var_ready, 1)
                s.link(dve.tensor_scalar(vr[:, :], mv[:, :, 1], EPS, None, ALU.add))
                dve.wait_ge(rooted, 1)
                s.link(dve.reciprocal(r0[:, :], std[:, :]))
                s.link(dve.tensor_tensor(half[:, :], r0[:, :], r0[:, :], ALU.mult))
                s.link(dve.tensor_tensor(half[:, :], half[:, :], vr[:, :], ALU.mult))
                s.link(dve.tensor_scalar(half[:, :], half[:, :], -0.5, 1.5, ALU.mult, ALU.add))
                s.link(dve.tensor_tensor(k.rstd[:, :], r0[:, :], half[:, :], ALU.mult))
                s.link(dve.scalar_tensor_tensor(out=k.shift[:, :], in0=mv[:, :, 0], scalar=-1.0,
                                                in1=k.rstd[:, :], op0=ALU.mult, op1=ALU.mult))
                s.link(dve.tensor_tensor(half[:, :], k.rstd[:, :], k.rstd[:, :], ALU.mult))
                s.link(dve.scalar_tensor_tensor(out=k.length2[:, :], in0=mv[:, :, 1], scalar=float(D),
                                                in1=half[:, :], op0=ALU.mult, op1=ALU.mult))

            @block.scalar
            def _(act):
                act.wait_ge(var_ready, 1)
                act.activation(std[:, :], mv[:, :, 1], ACT.Sqrt, bias=k.eps[:, 0:1]).then_inc(rooted, 1)


class Normed:

    RING = 2

    def __init__(self, m, k, banks=2):
        self.k, self.banks = k, banks
        self.xn = m.sb("xn", [P, self.RING, CT, D])
        self.xnT = m.sb("xnT", [P, self.RING, KD, CHUNK])
        self.turned_ps = m.ps("turned_ps", [P, banks, CHUNK])
        self.xn_ready = m.sem("xn_ready")
        self.turned = m.sem("turned")
        self.xnT_ready = m.sem("xnT_ready")
        self.xnT_used = m.sem("xnT_used")

    def apply(self, dve, c, b):
        k = self.k
        dve.wait_ge(self.xnT_used, c + 1)
        for j in range(CT):
            t = c * CT + j
            ins = dve.tensor_scalar(self.xn[:, b, j:j + 1, :], k.x[:, bass.ds(t, 1), :], k.rstd[:, bass.ds(t, 1)],
                                    k.shift[:, bass.ds(t, 1)], ALU.mult, ALU.add)
        ins.then_inc(self.xn_ready, 1)

    def prime_pe(self, pe):
        pe.sem_inc(self.xnT_used, self.RING)

    def prime_act(self, act):
        act.sem_inc(self.xnT_ready, self.banks)

    def turn(self, pe, c, b):
        pe.wait_ge(self.xn_ready, c + 1)
        for h in range(KD):
            pe.wait_ge(self.xnT_ready, c * KD + h + 1)
            for j in range(CT):
                ins = pe.transpose(self.turned_ps[:, h % self.banks, j * P:(j + 1) * P],
                                   self.xn[:, b, j, h * P:(h + 1) * P], self.k.ident[:, :])
            ins.then_inc(self.turned, 1)

    def keep(self, act, c, b):
        act.wait_ge(self.xnT_used, c + 1)
        for h in range(KD):
            act.wait_ge(self.turned, c * KD + h + 1)
            act.activation(self.xnT[:, b, h, :], self.turned_ps[:, h % self.banks, :], ACT.Copy) \
               .then_inc(self.xnT_ready, 1)

    def wait_xnT(self, eng, c):
        eng.wait_ge(self.xnT_ready, self.banks + (c + 1) * KD)


FFN0_STEPS = 20


def ffn0(nc, k, a, name):
    with ExitStack() as stack:
        m = Core(nc, stack, name)
        w = m.sb("w", [P, KD, C0])
        w2 = m.sb("w2", [R0, D])
        other = m.sb("other", [P, KD, C0])
        center = m.sb("center", [P, N0])
        slope = m.sb("slope", [P, N0])
        const = m.sb("const", [P, C0])
        nd = Normed(m, k)
        y = m.sb("y", [P, 2, CT, C0])
        sq = m.sb("sq", [P, CT, N0 * S0])
        score = m.sb("score", [P, CT, N0])
        len2 = m.sb("len2", [P, CT, N0])
        inv = m.sb("inv", [P, CT, N0])
        z = m.sb("z", [P, CT, N0])
        ez = m.sb("ez", [P, CT, N0])
        gate = m.sb("gate", [P, CT, N0])
        best = m.sb("best", [P, CT])
        first = m.sb("first", [P, CT])
        keepc = m.sb("keepc", [P, CT])
        mod = m.sb("mod", [P, CT, R0])
        modT = m.sb("modT", [R0, CHUNK])
        w_ps = m.ps("w_ps", [P, CT, 256])
        mod_ps = m.ps("mod_ps", [P, CHUNK])
        out_ps = m.ps("out_ps", [P, CT, D])
        loaded = m.sem("loaded")
        prepared, const_ps_ready, const_ready = m.sem("prepared"), m.sem("const_ps_ready"), m.sem("const_ready")
        first_done = m.sem("first_done")
        y_ready = m.sem("y_ready")
        z_ready = m.sem("z_ready")
        ez_ready = m.sem("ez_ready")
        mod_ready = m.sem("mod_ready")
        mod_turned = m.sem("mod_turned")
        modT_ready = m.sem("modT_ready")
        out_done = m.sem("out_done")
        out_used = m.sem("out_used")
        steps = m.sem("steps")
        block = stack.enter_context(nc.Block())

        @block.sync
        def _(sp):
            sp.dma_start(w[:, :, :], a["ffn0_w"].rearrange("(k p) c -> p k c", p=P)).then_inc(loaded, 16)
            sp.dma_start(other[:, :, :], a["ffn0_other"].rearrange("(k p) c -> p k c", p=P)).then_inc(loaded, 16)
            sp.dma_start(w2[:, :], a["ffn0_w2"]).then_inc(loaded, 16)
            sp.dma_start(center[:, :], a["ffn0_center"]).then_inc(loaded, 16)
            sp.dma_start(slope[:, :], a["ffn0_slope"]).then_inc(loaded, 16)
            sp.wait_ge(loaded, 80)

        @block.vector
        def _(dve):
            dve.sem_inc(y_ready, 1)
            dve.sem_inc(out_used, 1)
            dve.wait_ge(loaded, 80)
            dve.tensor_tensor(other[:, :, :], other[:, :, :], w[:, :, :], ALU.mult).then_inc(prepared, 1)
            dve.wait_ge(const_ps_ready, 1)
            dve.tensor_copy(const[:, 0:C0 - N0], w_ps[:, 0, 0:C0 - N0]).then_inc(const_ready, 1)
            dve.tensor_scalar(const[:, C0 - N0:C0], w_ps[:, 0, C0 - N0:C0], 0.5, None, ALU.mult) \
               .then_inc(const_ready, 1)
            dve.wait_ge(const_ready, 2)
            with dve.Fori(0, CHUNKS // 2) as i:
                s = Steps(dve, steps, i * (2 * FFN0_STEPS))
                for b in range(2):
                    nd.apply(dve, i * 2 + b, b)
                for b in range(2):
                    c = i * 2 + b
                    yb = y[:, b, :, :]
                    t0 = c * CT
                    dve.wait_ge(first_done, c + 1)
                    dve.tensor_tensor(yb, w_ps[:, :, 0:C0], bcast(const[:, :].rearrange("p (o c) -> p o c", o=1),
                                                                 [P, CT, C0]), ALU.subtract).then_inc(y_ready, 1)
                    dve.wait_ge(y_ready, 1 + c + 1)
                    s.mark(dve.tensor_tensor(sq[:, :, :], yb[:, :, 0:64], yb[:, :, 0:64], ALU.mult))
                    s.link(dve.scalar_tensor_tensor(
                        out=len2[:, :, :], in0=yb[:, :, C0 - N0:C0], scalar=-2.0,
                        in1=bcast(k.length2[:, bass.ds(t0, CT)].rearrange("p (c o) -> p c o", o=1), [P, CT, N0]),
                        op0=ALU.mult, op1=ALU.add))
                    s.mark(dve.tensor_reduce(score[:, :, :], sq[:, :, :].rearrange("p c (n s) -> p c n s", s=S0),
                                             AX.X, ALU.add))
                    s.link(dve.reciprocal(inv[:, :, :], len2[:, :, :]))
                    s.link(dve.tensor_tensor(score[:, :, :], score[:, :, :], inv[:, :, :], ALU.mult))
                    s.link(dve.tensor_tensor(score[:, :, :], score[:, :, :], bcast(
                        center[:, :].rearrange("p (o n) -> p o n", o=1), [P, CT, N0]), ALU.subtract))
                    dve.tensor_tensor(z[:, :, :], score[:, :, :], bcast(
                        slope[:, :].rearrange("p (o n) -> p o n", o=1), [P, CT, N0]), ALU.mult).then_inc(z_ready, 1)
                    dve.wait_ge(ez_ready, c + 1)
                    s.link(dve.tensor_scalar(inv[:, :, :], ez[:, :, :], 1.0, None, ALU.add))
                    s.link(dve.reciprocal(gate[:, :, :], inv[:, :, :]))
                    s.link(dve.tensor_reduce(best[:, :], gate[:, :, :], AX.X, ALU.max))
                    best_b = bcast(best[:, :].rearrange("p (c o) -> p c o", o=1), [P, CT, N0])
                    s.link(dve.tensor_tensor(score[:, :, :], gate[:, :, :], best_b, ALU.is_equal))
                    s.link(dve.tensor_tensor(score[:, :, :], score[:, :, :], k.rev[:, :, :], ALU.mult))
                    s.link(dve.tensor_reduce(first[:, :], score[:, :, :], AX.X, ALU.max))
                    s.link(dve.tensor_tensor(score[:, :, :], score[:, :, :], bcast(
                        first[:, :].rearrange("p (c o) -> p c o", o=1), [P, CT, N0]), ALU.is_equal))
                    s.link(dve.scalar_tensor_tensor(out=mod[:, :, 64:R0], in0=score[:, :, :], scalar=0.5,
                                                    in1=best_b, op0=ALU.mult, op1=ALU.mult))
                    s.mark(dve.tensor_scalar(keepc[:, :], best[:, :], -0.5, 0.5, ALU.mult, ALU.add))
                    dve.tensor_tensor(
                        mod[:, :, 0:64].rearrange("p c (n s) -> p c n s", s=S0),
                        yb[:, :, 64:128].rearrange("p c (n s) -> p c n s", s=S0),
                        bcast(mod[:, :, 64:R0].rearrange("p c (n o) -> p c n o", o=1), [P, CT, N0, S0]),
                        ALU.mult).then_inc(mod_ready, 1)
                    s.wait()
                    for j in range(CT):
                        s.mark(dve.scalar_tensor_tensor(
                            out=k.x[:, bass.ds(t0 + j, 1), :], in0=nd.xn[:, b, j:j + 1, :], scalar=keepc[:, j:j + 1],
                            in1=k.x[:, bass.ds(t0 + j, 1), :], op0=ALU.mult, op1=ALU.add))
                    s.wait()
                    dve.wait_ge(out_done, c + 1)
                    s.link(dve.tensor_tensor(k.x[:, bass.ds(t0, CT), :], k.x[:, bass.ds(t0, CT), :], out_ps[:, :, :],
                                             ALU.add))
                    dve.sem_inc(out_used, 1)
                assert s.n == 2 * FFN0_STEPS, s.n

        @block.scalar
        def _(act):
            nd.prime_act(act)
            act.sem_inc(modT_ready, 1)
            with act.Fori(0, CHUNKS // 2) as i:
                for b in range(2):
                    nd.keep(act, i * 2 + b, b)
                for b in range(2):
                    c = i * 2 + b
                    act.wait_ge(z_ready, c + 1)
                    act.activation(ez[:, :, :], z[:, :, :], ACT.Exp, scale=-1.0).then_inc(ez_ready, 1)
                    act.wait_ge(mod_turned, c + 1)
                    act.activation(modT[:, :], mod_ps[0:R0, :], ACT.Copy).then_inc(modT_ready, 1)

        @block.tensor
        def _(pe):
            nd.prime_pe(pe)
            pe.wait_ge(prepared, 1)
            for kt in range(KD):
                ins = pe.matmul(w_ps[:, 0, 0:C0], k.ones[:, :], other[:, kt, :], start=(kt == 0), stop=(kt == KD - 1))
            ins.then_inc(const_ps_ready, 1)
            pe.wait_ge(const_ready, 2)
            with pe.Fori(0, CHUNKS // 2) as i:
                for b in range(2):
                    nd.turn(pe, i * 2 + b, b)
                for b in range(2):
                    c = i * 2 + b
                    nd.wait_xnT(pe, c)
                    pe.wait_ge(y_ready, c + 1)
                    for j in range(CT):
                        for kt in range(KD):
                            ins = pe.matmul(w_ps[:, j, 0:C0], nd.xnT[:, b, kt, j * P:(j + 1) * P], w[:, kt, :],
                                            start=(kt == 0), stop=(kt == KD - 1))
                    ins.then_inc(first_done, 1)
                    pe.wait_ge(mod_ready, c + 1)
                    pe.wait_ge(modT_ready, c + 1)
                    for j in range(CT):
                        ins = pe.transpose(mod_ps[0:R0, j * P:(j + 1) * P], mod[:, j, :], k.ident[:, :])
                    ins.then_inc(mod_turned, 1)
                    pe.wait_ge(modT_ready, 1 + c + 1)
                    pe.wait_ge(out_used, c + 1)
                    for j in range(CT):
                        ins = pe.matmul(out_ps[:, j, :], modT[:, j * P:(j + 1) * P], w2[:, :], start=True, stop=True)
                    ins.then_inc(out_done, 1)
                    pe.wait_ge(out_used, 1 + c + 1)
                    pe.sem_inc(nd.xnT_used, 1)


def qkv0(nc, k, a, v_aug):
    with ExitStack() as stack:
        m = Core(nc, stack, "qkv0_")
        wq = m.sb("wq", [P, KD, H0 * D0])
        wk = m.sb("wk", [P, KD, G0 * D0])
        wv = m.sb("wv", [P, KD, G0 * D0])
        bq = m.sb("bq", [P, 2])
        bk = m.sb("bk", [G0 * D0, 1])
        bv = m.sb("bv", [P, G0 * D0])
        nd = Normed(m, k)
        pieces = m.sb("pieces", [P, 2, 3, 2, CHUNK], F16)
        qk_ps = m.ps("qk_ps", [P, 3, CHUNK])
        v_ps = m.ps("v_ps", [P, CT, G0 * D0])
        loaded = m.sem("loaded")
        product = m.sem("product")
        high = m.sem("high")
        low = m.sem("low")
        v_done = m.sem("v_done")
        v_used = m.sem("v_used")
        padded = m.sem("padded")
        stored = [m.sem("stored0"), m.sem("stored1")]
        block = stack.enter_context(nc.Block())
        rows = [P, P, G0 * D0]

        @block.sync
        def _(sp):
            for b in range(2):
                sp.sem_inc(stored[b], 48)
            sp.dma_start(wq[:, :, :], a["wq0"].rearrange("(k p) c -> p k c", p=P)).then_inc(loaded, 16)
            sp.dma_start(wk[:, :, :], a["wk0"].rearrange("(k p) c -> p k c", p=P)).then_inc(loaded, 16)
            sp.dma_start(wv[:, :, :], a["wv0"].rearrange("(k p) c -> p k c", p=P)).then_inc(loaded, 16)
            sp.dma_start(bq[:, :], a["bq0"]).then_inc(loaded, 16)
            sp.dma_start(bk[:, :], a["bk0"].rearrange("(p o) -> p o", o=1)).then_inc(loaded, 16)
            sp.dma_start(bv[:, :], a["bv0"]).then_inc(loaded, 16)
            with sp.Fori(0, CHUNKS // 2) as i:
                for b in range(2):
                    c = i * 2 + b
                    sp.wait_ge(low, 3 + (c + 1) * 3)
                    for n in range(2):
                        sp.dma_start(a["q0_scr"][n, :, :, bass.ds(c * CHUNK, CHUNK)], pieces[:, b, n, :, :]) \
                          .then_inc(stored[b], 16)
                    sp.dma_start(a["k0_scr"][:, :, bass.ds(c * CHUNK, CHUNK)],
                                 pieces[0:G0 * D0, b, 2, :, :]).then_inc(stored[b], 16)
            for b in range(2):
                sp.wait_ge(stored[b], 48 * (1 + CHUNKS // 2))

        @block.gpsimd
        def _(pool):
            pool.memset(v_aug[:, :, :, D0:D0 + 1], 1.0).then_inc(padded, 1)
            pool.memset(v_aug[:, :, :, D0 + 1:VW], 0.0).then_inc(padded, 1)
            pool.wait_ge(padded, 2)

        @block.vector
        def _(dve):
            dve.sem_inc(low, 3)
            dve.sem_inc(v_used, 1)
            dve.wait_ge(loaded, 96)
            with dve.Fori(0, CHUNKS // 2) as i:
                for b in range(2):
                    nd.apply(dve, i * 2 + b, b)
                for b in range(2):
                    c = i * 2 + b
                    for n in range(3):
                        r = rows[n]
                        bias = bq[:, n:n + 1] if n < 2 else bk[:, 0:1]
                        dve.wait_ge(high, c * 3 + n + 1)
                        dve.scalar_tensor_tensor(out=pieces[0:r, b, n, 1, :], in0=qk_ps[0:r, n, :], scalar=bias,
                                                 in1=pieces[0:r, b, n, 0, :], op0=ALU.add, op1=ALU.subtract) \
                           .then_inc(low, 1)
                    dve.wait_ge(v_done, c + 1)
                    dve.tensor_tensor(
                        v_aug[:, bass.ds(c * CT, CT), :, 0:D0],
                        v_ps[:, :, :].rearrange("p c (g d) -> p c g d", g=G0),
                        bcast(bv[:, :].rearrange("p (o g d) -> p o g d", o=1, g=G0), [P, CT, G0, D0]),
                        ALU.add).then_inc(v_used, 1)

        @block.scalar
        def _(act):
            nd.prime_act(act)
            act.wait_ge(loaded, 96)
            with act.Fori(0, CHUNKS // 2) as i:
                for b in range(2):
                    nd.keep(act, i * 2 + b, b)
                for b in range(2):
                    c = i * 2 + b
                    act.wait_ge(stored[b], (i + 1) * 48)
                    for n in range(3):
                        r = rows[n]
                        bias = bq[:, n:n + 1] if n < 2 else bk[:, 0:1]
                        act.wait_ge(product, c * 3 + n + 1)
                        act.activation(pieces[0:r, b, n, 0, :], qk_ps[0:r, n, :], ACT.Identity, bias=bias) \
                           .then_inc(high, 1)

        @block.tensor
        def _(pe):
            nd.prime_pe(pe)
            pe.wait_ge(loaded, 96)
            with pe.Fori(0, CHUNKS // 2) as i:
                for b in range(2):
                    nd.turn(pe, i * 2 + b, b)
                for b in range(2):
                    c = i * 2 + b
                    nd.wait_xnT(pe, c)
                    for n in range(3):
                        pe.wait_ge(low, (c + 1) * 3)
                        for kt in range(KD):
                            wn = wq[:, kt, n * P:(n + 1) * P] if n < 2 else wk[:, kt, :]
                            ins = pe.matmul(qk_ps[0:rows[n], n, :], wn, nd.xnT[:, b, kt, :], start=(kt == 0),
                                            stop=(kt == KD - 1))
                        ins.then_inc(product, 1)
                    pe.wait_ge(v_used, c + 1)
                    for j in range(CT):
                        for kt in range(KD):
                            ins = pe.matmul(v_ps[:, j, :], nd.xnT[:, b, kt, j * P:(j + 1) * P], wv[:, kt, :],
                                            start=(kt == 0), stop=(kt == KD - 1))
                    ins.then_inc(v_done, 1)
                    pe.wait_ge(v_done, c + 1)
                    pe.sem_inc(nd.xnT_used, 1)


class Attn0Plan:

    units = [(c, kt) for c in range(CHUNKS) for kt in range(CT * c + CT)]
    maxima = [(qt, kc, h) for qt in range(TILES) for kc in range(qt // CT + 1) for h in range(QUAD)]
    UNITS, MAXIMA = len(units), len(maxima)

    @classmethod
    def maxima_at(cls, u):
        return range(u * cls.MAXIMA // cls.UNITS, (u + 1) * cls.MAXIMA // cls.UNITS)


def attn0(nc, k, a, v_aug, att):
    plan = Attn0Plan
    SCALE = float(D0) ** -0.5
    with ExitStack() as stack:
        m = Core(nc, stack, "attn0_")
        qs = m.sb("qs", [P, H0, T], F16)
        ks = m.sb("ks", [P, G0, T], F16)
        kmax = m.sb("kmax", [P, G0, T], F16)
        v_now = m.sb("v_now", [P, TILES, VW])
        part = m.sb("part", [P, QUAD, TILES, CHUNKS])
        mx = m.sb("mx", [P, 2, QUAD, TILES])
        mxT = m.sb("mxT", [QUAD * TILES, P], F16)
        prob = m.sb("prob", [P, 2, QUAD, CHUNK])
        oT = m.sb("oT", [P, 2, CHUNK])
        inv = m.sb("inv", [P, CT, QUAD])
        score_ps = m.ps("score_ps", [P, 2, 2, CHUNK])
        max_ps = m.ps("max_ps", [P, 2, CHUNK])
        o_ps = m.ps("o_ps", [P, CHUNK])
        misc_ps = m.ps("misc_ps", [P, CHUNK])
        blank = m.sem("blank")
        loaded = m.sem("loaded")
        max_done = m.sem("max_done")
        max_used = m.sem("max_used")
        part_blank = m.sem("part_blank")
        mx_ready = m.sem("mx_ready")
        mx_turned = m.sem("mx_turned")
        mxT_ready = m.sem("mxT_ready")
        row_set = m.sem("row_set")
        v_set = m.sem("v_set")
        scored = m.sem("scored")
        exped = m.sem("exped")
        weighed = m.sem("weighed")
        o_kept = m.sem("o_kept")
        o_turned = m.sem("o_turned")
        o_out = m.sem("o_out")
        inv_ready = m.sem("inv_ready")
        block = stack.enter_context(nc.Block())
        PU, PM = plan.UNITS, plan.MAXIMA

        @block.gpsimd
        def _(pool):
            for t in (qs, ks, kmax):
                pool.memset(t[64:P, :, :], 0.0).then_inc(blank, 1)
            pool.wait_ge(blank, 3)
            pool.memset(part[:, :, :, :], NEG).then_inc(part_blank, 1)
            pool.wait_ge(part_blank, 1)
            pool.memset(mx[:, 1, :, :], 0.0).then_inc(part_blank, 1)
            pool.wait_ge(part_blank, 2)
            pool.memset(ks[64:65, :, :], 1.0).then_inc(blank, 1)
            pool.wait_ge(blank, 4)

        @block.sync
        def _(sp):
            q = a["q0_scr"].rearrange("m (h r) e t -> (m h) r e t", r=D0)
            kk = a["k0_scr"].rearrange("(g r) e t -> g r e t", r=D0)
            for r, (pq, pk) in enumerate(((0, 0), (1, 0), (0, 1), (1, 1))):
                rows = slice(r * D0, (r + 1) * D0)
                sp.dma_start(qs[rows, :, :], q[:, :, pq, :].rearrange("h r t -> r h t")).then_inc(loaded, 16)
                sp.dma_start(ks[rows, :, :], kk[:, :, pk, :].rearrange("g r t -> r g t")).then_inc(loaded, 16)
                sp.dma_start(kmax[rows, :, :], kk[:, :, pk, :].rearrange("g r t -> r g t")).then_inc(loaded, 16)

            def set_row(g):
                sp.wait_ge(mxT_ready, g + 1)
                sp.dma_start(qs[64:65, bass.ds(g * QUAD, QUAD), :].rearrange("o h (t p) -> o (h t) p", p=P),
                             mxT[:, :]).then_inc(row_set, 16)

            sp.wait_ge(blank, 4)
            set_row(0)
            with sp.Fori(0, QUADS - 1) as g:
                set_row(g + 1)
            sp.wait_ge(row_set, 16 * QUADS)

        @block.vector
        def _(dve):
            dve.sem_inc(max_used, 2)
            dve.sem_inc(o_kept, 1)
            dve.sem_inc(o_out, 1)
            dve.wait_ge(part_blank, 2)

            def reduce_max(g, n):
                qt, kc, h = plan.maxima[n]
                w = min(CHUNK, (qt + 1) * P - kc * CHUNK)
                tile = g * PM + n
                dve.wait_ge(max_done, tile + 1)
                dve.tensor_reduce(part[:, h, qt, kc:kc + 1], max_ps[:, n % 2, 0:w], AX.X, ALU.max) \
                   .then_inc(max_used, 1)
                if n + 1 == PM:
                    dve.wait_ge(max_used, 2 + tile + 1)
                    dve.tensor_reduce(mx[:, 0, :, :], part[:, :, :, :], AX.X, ALU.max, negate=True) \
                       .then_inc(mx_ready, 1)
                    dve.wait_ge(mx_turned, g + 1)
                    if not isinstance(g, int) or g > 0:
                        dve.wait_ge(row_set, 16 * g)
                    dve.tensor_copy(mxT[:, :], misc_ps[0:QUAD * TILES, 0:P]).then_inc(mxT_ready, 1)

            def keep_o(g, c):
                dve.wait_ge(weighed, 2 + g * PU + CT * (c + 1) * (c + 2) // 2)
                dve.tensor_copy(oT[:, c % 2, :], o_ps[:, :]).then_inc(o_kept, 1)

            def put_out(g, c):
                dve.wait_ge(o_turned, g * CHUNKS + c + 1)
                o = misc_ps[:, :].rearrange("p (t h w) -> p t h w", t=CT, h=QUAD)
                dve.reciprocal(inv[:, :, :], o[:, :, :, D0:D0 + 1].rearrange("p t h o -> p t (h o)")).then_inc(inv_ready, 1)
                dve.wait_ge(inv_ready, g * CHUNKS + c + 1)
                dve.tensor_tensor(
                    att[:, CT * c:CT * (c + 1), bass.ds(g * QUAD, QUAD), :], o[:, :, :, 0:D0],
                    bcast(inv[:, :, :].rearrange("p t (h o) -> p t h o", o=1), [P, CT, QUAD, D0]),
                    ALU.mult).then_inc(o_out, 1)

            def one_pass(g, nxt):
                dve.wait_ge(weighed, 2 + g * PU)
                dve.tensor_copy(v_now[:, :, :], v_aug[:, :, bass.ds(g // 2, 1), :].rearrange("p t o w -> p t (o w)")) \
                   .then_inc(v_set, 1)
                for u, (c, kt) in enumerate(plan.units):
                    if nxt:
                        for n in plan.maxima_at(u):
                            if n + 1 < PM:
                                reduce_max(g + 1, n)
                    if c > 0 and kt == 1:
                        keep_o(g, c - 1)
                    if c > 0 and kt == 3:
                        put_out(g, c - 1)
                keep_o(g, CHUNKS - 1)
                put_out(g, CHUNKS - 1)
                if nxt:
                    reduce_max(g + 1, PM - 1)

            for n in range(PM):
                reduce_max(0, n)
            with dve.Fori(0, QUADS - 1) as g:
                one_pass(g, True)
            one_pass(QUADS - 1, False)

        @block.scalar
        def _(act):
            act.sem_inc(exped, 2)

            def one_pass(g):
                for u, (c, kt) in enumerate(plan.units):
                    off = max(0, kt - CT * c) * P
                    act.wait_ge(weighed, g * PU + u + 1)
                    for pair in range(2):
                        act.wait_ge(scored, (g * PU + u) * 2 + pair + 1)
                        act.activation(prob[:, u % 2, 2 * pair:2 * pair + 2, off:CHUNK],
                                       score_ps[:, pair, :, off:CHUNK], ACT.Exp, scale=SCALE).then_inc(exped, 1)

            with act.Fori(0, QUADS) as g:
                one_pass(g)

        @block.tensor
        def _(pe):
            pe.sem_inc(weighed, 2)
            pe.wait_ge(loaded, 12 * 16)
            pe.wait_ge(blank, 4)
            pe.wait_ge(part_blank, 2)

            def max_tile(g, n):
                qt, kc, h = plan.maxima[n]
                w = min(CHUNK, (qt + 1) * P - kc * CHUNK)
                diagonal = kc == qt // CT
                pe.wait_ge(max_used, g * PM + n + 1)
                out = max_ps[:, n % 2, :]
                ins = pe.matmul(out[:, 0:w],
                                qs[:, bass.ds(g * QUAD + h, 1), qt * P:(qt + 1) * P].rearrange("p o t -> p (o t)"),
                                kmax[:, bass.ds(g // 2, 1), kc * CHUNK:kc * CHUNK + w].rearrange("p o t -> p (o t)"),
                                start=True, stop=not diagonal)
                if diagonal:
                    ins = pe.matmul(out[:, w - P:w], k.identb[:, :], k.mask_qk[:, :], start=False, stop=True)
                ins.then_inc(max_done, 1)

            def turn_maxima(g):
                pe.wait_ge(mx_ready, g + 1)
                pe.wait_ge(o_out, 1 + g * CHUNKS)
                pe.transpose(misc_ps[:, 0:P], mx[:, :, :, :].rearrange("p o h t -> p (o h t)"), k.ident[:, :]) \
                  .then_inc(mx_turned, 1)

            def score(g, u):
                c, kt = plan.units[u]
                off = max(0, kt - CT * c) * P
                for pair in range(2):
                    pe.wait_ge(exped, (g * PU + u) * 2 + pair + 1)
                    for h in range(2):
                        head = g * QUAD + 2 * pair + h
                        diagonal = kt >= CT * c
                        ins = pe.matmul(score_ps[:, pair, h, off:CHUNK],
                                        ks[:, bass.ds(g // 2, 1), kt * P:(kt + 1) * P].rearrange("p o t -> p (o t)"),
                                        qs[:, bass.ds(head, 1), c * CHUNK + off:(c + 1) * CHUNK]
                                        .rearrange("p o t -> p (o t)"), start=True, stop=not diagonal)
                        if diagonal:
                            ins = pe.matmul(score_ps[:, pair, h, off:off + P], k.identb[:, :], k.mask_kq[:, :],
                                            start=False, stop=True)
                    ins.then_inc(scored, 1)

            def weigh(g, u):
                c, kt = plan.units[u]
                off = max(0, kt - CT * c) * P
                pe.wait_ge(exped, 2 + (g * PU + u + 1) * 2)
                if kt == 0:
                    pe.wait_ge(o_kept, g * CHUNKS + c + 1)
                for h in range(QUAD):
                    ins = pe.matmul(o_ps[32 * h:32 * h + 32, off:CHUNK], v_now[:, kt, :], prob[:, u % 2, h, off:CHUNK],
                                    start=(kt == 0), stop=(kt == CT * c + CT - 1), skip_group_check=True)
                ins.then_inc(weighed, 1)

            def turn_o(g, c):
                pe.wait_ge(o_kept, 1 + g * CHUNKS + c + 1)
                if c == 0:
                    pe.wait_ge(mxT_ready, g + 1)
                pe.wait_ge(o_out, g * CHUNKS + c + 1)
                for t in range(CT):
                    ins = pe.transpose(misc_ps[:, t * P:(t + 1) * P], oT[:, c % 2, t * P:(t + 1) * P], k.ident[:, :])
                ins.then_inc(o_turned, 1)

            def one_pass(g, nxt):
                pe.wait_ge(row_set, 16 * (g + 1))
                pe.wait_ge(v_set, g + 1)
                for u, (c, kt) in enumerate(plan.units):
                    score(g, u)
                    if nxt:
                        for n in plan.maxima_at(u):
                            max_tile(g + 1, n)
                    if u > 0:
                        weigh(g, u - 1)
                    if c > 0 and kt == 2:
                        turn_o(g, c - 1)
                weigh(g, PU - 1)
                turn_o(g, CHUNKS - 1)
                if nxt:
                    turn_maxima(g + 1)

            for n in range(PM):
                max_tile(0, n)
            turn_maxima(0)
            with pe.Fori(0, QUADS - 1) as g:
                one_pass(g, True)
            one_pass(QUADS - 1, False)


WO0_STEPS = 4


def wo0(nc, k, a, att):
    with ExitStack() as stack:
        m = Core(nc, stack, "wo0_")
        wo = m.sb("wo", [P, KD, D])
        bo = m.sb("bo", [P, D])
        part = m.sb("part", [P, 2, CT, D])
        partT = m.sb("partT", [P, 2, KD, CHUNK])
        turned_ps = m.ps("turned_ps", [P, KD, CHUNK])
        out_ps = m.ps("out_ps", [P, 2, CT, D])
        loaded = m.sem("loaded")
        copied, turned, kept = m.sem("copied"), m.sem("turned"), m.sem("kept")
        done, used, steps = m.sem("done"), m.sem("used"), m.sem("steps")
        block = stack.enter_context(nc.Block())

        @block.sync
        def _(sp):
            sp.dma_start(wo[:, :, :], a["wo0"].rearrange("(k p) c -> p k c", p=P)).then_inc(loaded, 16)
            sp.dma_start(bo[:, :], a["bo0"]).then_inc(loaded, 16)
            sp.wait_ge(loaded, 32)

        @block.vector
        def _(dve):
            dve.sem_inc(used, 2)
            dve.wait_ge(loaded, 32)
            with dve.Fori(0, CHUNKS // 2) as i:
                s = Steps(dve, steps, i * 2)
                for b in range(2):
                    c = i * 2 + b
                    dve.wait_ge(used, c + 1)
                    dve.tensor_copy(part[:, b, :, :], att[:, bass.ds(c * CT, CT), :, :]
                                    .rearrange("p t h w -> p t (h w)")).then_inc(copied, 1)
                for b in range(2):
                    c = i * 2 + b
                    x = k.x[:, bass.ds(c * CT, CT), :]
                    s.link(dve.tensor_tensor(x, x, bcast(bo[:, :].rearrange("p (o c) -> p o c", o=1), [P, CT, D]),
                                             ALU.add))
                    dve.wait_ge(done, c + 1)
                    dve.tensor_tensor(x, x, out_ps[:, b, :, :], ALU.add).then_inc(used, 1)

        @block.scalar
        def _(act):
            act.sem_inc(kept, 2)
            with act.Fori(0, CHUNKS // 2) as i:
                for b in range(2):
                    c = i * 2 + b
                    act.wait_ge(used, c + 1)
                    for h in range(KD):
                        act.wait_ge(turned, c * KD + h + 1)
                        act.activation(partT[:, b, h, :], turned_ps[:, h, :], ACT.Copy).then_inc(kept, 1)

        @block.tensor
        def _(pe):
            pe.wait_ge(loaded, 32)
            with pe.Fori(0, CHUNKS // 2) as i:
                for b in range(2):
                    c = i * 2 + b
                    pe.wait_ge(copied, c + 1)
                    for h in range(KD):
                        pe.wait_ge(kept, c * KD + h + 1)
                        for j in range(CT):
                            ins = pe.transpose(turned_ps[:, h, j * P:(j + 1) * P], part[:, b, j, h * P:(h + 1) * P],
                                               k.ident[:, :])
                        ins.then_inc(turned, 1)
                    pe.wait_ge(kept, 2 + (c + 1) * KD)
                    pe.wait_ge(used, c + 1)
                    for j in range(CT):
                        for kt in range(KD):
                            ins = pe.matmul(out_ps[:, b, j, :], partT[:, b, kt, j * P:(j + 1) * P], wo[:, kt, :],
                                            start=(kt == 0), stop=(kt == KD - 1))
                    ins.then_inc(done, 1)


FFN1_STEPS = 17


def ffn1(nc, k, a, name):
    with ExitStack() as stack:
        m = Core(nc, stack, name)
        w13 = m.sb("w13", [P, KD, X1, 2, I1])
        w2 = m.sb("w2", [P, X1, D])
        gw = m.sb("gw", [P, KD, E1])
        gb = m.sb("gb", [P, E1])
        nd = Normed(m, k, banks=1)
        lg = m.sb("lg", [P, CT, E1])
        el = m.sb("el", [P, CT, E1])
        prob = m.sb("prob", [P, CT, E1])
        bias = m.sb("bias", [P, CT, E1])
        pick = m.sb("pick", [P, CT, E1])
        chosen = m.sb("chosen", [P, CT, E1])
        top = m.sb("top", [P, CT])
        dw = m.sb("dw", [P, 2, CT, X1])
        act1 = m.sb("act1", [P, 2, CHUNK])
        hid = m.sb("hid", [P, 2, CHUNK])
        lg_ps = m.ps("lg_ps", [P, CT, E1])
        h_ps = m.ps("h_ps", [P, 2, 2, CHUNK])
        y_ps = m.ps("y_ps", [P, CT, D])
        loaded = m.sem("loaded")
        shared_set = m.sem("shared_set")
        lg_done = m.sem("lg_done")
        lg_ready = m.sem("lg_ready")
        el_ready = m.sem("el_ready")
        dw_ready = m.sem("dw_ready")
        h_done = m.sem("h_done")
        act_ready = m.sem("act_ready")
        hid_ready = m.sem("hid_ready")
        y_done = m.sem("y_done")
        y_used = m.sem("y_used")
        steps = m.sem("steps")
        block = stack.enter_context(nc.Block())

        @block.sync
        def _(sp):
            sp.dma_start(gw[:, :, :], a["gate1_w"].rearrange("(k p) c -> p k c", p=P)).then_inc(loaded, 16)
            sp.dma_start(gb[:, :], a["gate1_b"]).then_inc(loaded, 16)
            sp.dma_start(w13[:, :, :, :, :].rearrange("p k x w i -> p k (x w i)"),
                         a["w13"].rearrange("(k p) c -> p k c", p=P)).then_inc(loaded, 16)
            sp.dma_start(w2[:, :, :], a["w2"].rearrange("x p d -> p x d")).then_inc(loaded, 16)
            sp.wait_ge(loaded, 64)

        @block.vector
        def _(dve):
            dve.sem_inc(hid_ready, 2)
            dve.sem_inc(lg_ready, 1)
            dve.sem_inc(y_used, CT)
            dve.memset(dw[:, :, :, E1:X1], 0.5).then_inc(shared_set, 1)
            dve.wait_ge(shared_set, 1)
            dve.wait_ge(loaded, 64)

            def wide(ap):
                return bcast(ap.rearrange("p (c o) -> p c o", o=1), [P, CT, E1])

            def gating(s, c, b):
                dve.wait_ge(lg_done, c + 1)
                s.link(dve.tensor_reduce(top[:, :], lg_ps[:, :, :], AX.X, ALU.max))
                dve.tensor_tensor(lg[:, :, :], lg_ps[:, :, :], wide(top[:, :]), ALU.subtract).then_inc(lg_ready, 1)
                dve.wait_ge(el_ready, c + 1)
                s.link(dve.tensor_reduce(top[:, :], el[:, :, :], AX.X, ALU.add))
                s.link(dve.reciprocal(top[:, :], top[:, :]))
                s.link(dve.tensor_tensor(prob[:, :, :], el[:, :, :], wide(top[:, :]), ALU.mult))
                s.link(dve.tensor_tensor(bias[:, :, :], prob[:, :, :], bcast(
                    gb[:, :].rearrange("p (o e) -> p o e", o=1), [P, CT, E1]), ALU.add))
                for r in range(2):
                    out = (chosen, pick)[r]
                    s.link(dve.tensor_reduce(top[:, :], bias[:, :, :], AX.X, ALU.max))
                    s.link(dve.tensor_tensor(out[:, :, :], bias[:, :, :], wide(top[:, :]), ALU.is_equal))
                    s.link(dve.tensor_tensor(out[:, :, :], out[:, :, :], k.rev[:, :, :], ALU.mult))
                    s.link(dve.tensor_reduce(top[:, :], out[:, :, :], AX.X, ALU.max))
                    s.link(dve.tensor_tensor(out[:, :, :], out[:, :, :], wide(top[:, :]), ALU.is_equal))
                    if r == 0:
                        s.link(dve.scalar_tensor_tensor(out=bias[:, :, :], in0=chosen[:, :, :], scalar=NEG,
                                                        in1=bias[:, :, :], op0=ALU.mult, op1=ALU.add))
                s.link(dve.tensor_tensor(chosen[:, :, :], chosen[:, :, :], pick[:, :, :], ALU.add))
                dve.scalar_tensor_tensor(out=dw[:, b, :, 0:E1], in0=prob[:, :, :], scalar=0.5, in1=chosen[:, :, :],
                                         op0=ALU.mult, op1=ALU.mult).then_inc(dw_ready, 1)
                dve.wait_ge(dw_ready, c + 1)

            def add_y(e, q, c, b):
                dve.wait_ge(y_done, 2 + q + 1)
                for j in range(CT):
                    x = k.x[:, bass.ds(c * CT + j, 1), :]
                    dve.wait_ge(y_used, (q + 1) * CT)
                    dve.scalar_tensor_tensor(out=x, in0=y_ps[:, j:j + 1, :], scalar=dw[:, b, j, e:e + 1],
                                             in1=x, op0=ALU.mult, op1=ALU.add).then_inc(y_used, 1)

            with dve.Fori(0, CHUNKS // 2) as i:
                s = Steps(dve, steps, i * (2 * FFN1_STEPS))
                for b in range(2):
                    nd.apply(dve, i * 2 + b, b)
                for b in range(2):
                    c = i * 2 + b
                    gating(s, c, b)
                    for e in range(X1):
                        turn = b * X1 + e
                        q = i * (2 * X1) + turn
                        dve.wait_ge(act_ready, 2 + q + 1)
                        dve.wait_ge(y_done, q + 1)
                        dve.tensor_tensor(hid[:, turn % 2, :], act1[:, turn % 2, :], h_ps[:, turn % 2, 1, :],
                                          ALU.mult).then_inc(hid_ready, 1)
                        if e > 0:
                            add_y(e - 1, q - 1, c, b)
                    add_y(X1 - 1, q, c, b)
                assert s.n == 2 * FFN1_STEPS, s.n

        @block.scalar
        def _(act):
            nd.prime_act(act)
            act.sem_inc(act_ready, 2)
            with act.Fori(0, CHUNKS // 2) as i:
                for b in range(2):
                    nd.keep(act, i * 2 + b, b)
                for b in range(2):
                    c = i * 2 + b
                    act.wait_ge(lg_ready, 1 + c + 1)
                    act.activation(el[:, :, :], lg[:, :, :], ACT.Exp).then_inc(el_ready, 1)
                    for e in range(X1):
                        turn = b * X1 + e
                        q = i * (2 * X1) + turn
                        act.wait_ge(h_done, q + 1)
                        act.wait_ge(hid_ready, q + 1)
                        act.activation(act1[:, turn % 2, :], h_ps[:, turn % 2, 0, :], ACT.Silu) \
                           .then_inc(act_ready, 1)

        @block.tensor
        def _(pe):
            nd.prime_pe(pe)
            pe.sem_inc(y_done, 2)
            pe.wait_ge(loaded, 64)

            def first(c, b, e, turn, q):
                pe.wait_ge(hid_ready, q + 1)
                for n in range(2):
                    for kt in range(KD):
                        ins = pe.matmul(h_ps[:, turn % 2, n, :], w13[:, kt, e, n, :], nd.xnT[:, b, kt, :],
                                        start=(kt == 0), stop=(kt == KD - 1))
                ins.then_inc(h_done, 1)

            def second(e, turn, q):
                pe.wait_ge(hid_ready, 2 + q + 1)
                pe.wait_ge(y_used, (q + 1) * CT)
                for j in range(CT):
                    ins = pe.matmul(y_ps[:, j, :], hid[:, turn % 2, j * P:(j + 1) * P], w2[:, e, :],
                                    start=True, stop=True)
                ins.then_inc(y_done, 1)

            with pe.Fori(0, CHUNKS // 2) as i:
                for b in range(2):
                    nd.turn(pe, i * 2 + b, b)
                for b in range(2):
                    c = i * 2 + b
                    nd.wait_xnT(pe, c)
                    pe.wait_ge(lg_ready, c + 1)
                    for j in range(CT):
                        for kt in range(KD):
                            ins = pe.matmul(lg_ps[:, j, :], nd.xnT[:, b, kt, j * P:(j + 1) * P], gw[:, kt, :],
                                            start=(kt == 0), stop=(kt == KD - 1))
                    ins.then_inc(lg_done, 1)
                    for e in range(X1):
                        turn = b * X1 + e
                        q = i * (2 * X1) + turn
                        first(c, b, e, turn, q)
                        if e > 0:
                            second(e - 1, turn - 1, q - 1)
                    pe.wait_ge(h_done, q + 1)
                    pe.sem_inc(nd.xnT_used, 1)
                    second(X1 - 1, turn, q)


BANKS1 = QKV1 // CHUNK
ROT = BANKS1 - 1
HPB = CHUNK // D1


def qkv1(nc, k, a):
    with ExitStack() as stack:
        m = Core(nc, stack, "qkv1_")
        w = m.sb("w", [P, KD, QKV1])
        cos = m.sb("cos", [P, TILES, D1 // 2])
        sin = m.sb("sin", [P, TILES, D1 // 2])
        nd = Normed(m, k, banks=1)
        xc = m.sb("xc", [P, 2, HPB, 2, D1 // 2])
        xs = m.sb("xs", [P, 2, HPB, 2, D1 // 2])
        rot = m.sb("rot", [P, 2, HPB, D1])
        qk = m.sb("qk", [P, ROT * HPB, 2, CHUNK], F16)
        v = m.sb("v", [P, 2, 2, G1 * D1], F16)
        qkv_ps = m.ps("qkv_ps", [P, 3, CHUNK])
        turned_ps = m.ps("rot_ps", [P, 2, CHUNK])
        loaded = m.sem("loaded")
        product = m.sem("product")
        freed = m.sem("freed")
        scaled = m.sem("scaled")
        rot_ready = m.sem("rot_ready")
        rot_turned = m.sem("rot_turned")
        qk_high = m.sem("qk_high")
        qk_low = m.sem("qk_low")
        v_high = m.sem("v_high")
        v_low = m.sem("v_low")
        stored = m.sem("stored")
        v_stored = [m.sem("v_stored0"), m.sem("v_stored1")]
        block = stack.enter_context(nc.Block())
        NR = CT * ROT

        @block.sync
        def _(sp):
            sp.sem_inc(stored, 32)
            for b in range(2):
                sp.sem_inc(v_stored[b], 16)
            sp.dma_start(w[:, :, :], a["wqkv1"].rearrange("(k p) c -> p k c", p=P)).then_inc(loaded, 16)
            sp.dma_start(cos[:, :, :], a["cos"].rearrange("(t p) c -> p t c", p=P)).then_inc(loaded, 16)
            sp.dma_start(sin[:, :, :], a["sin"].rearrange("(t p) c -> p t c", p=P)).then_inc(loaded, 16)
            with sp.Fori(0, CHUNKS // 2) as i:
                for b in range(2):
                    c = i * 2 + b
                    for j in range(CT):
                        t = c * CT + j
                        sp.wait_ge(v_low, t + 1)
                        sp.dma_start(a["v1_scr"][bass.ds(t, 1), :, :, :].rearrange("o p e g -> p (o e) g"),
                                     v[:, j % 2, :, :]).then_inc(v_stored[j % 2], 16)
                    sp.wait_ge(qk_low, 2 + (c + 1) * NR)
                    for e in range(2):
                        sp.dma_start(a["qk1_scr"][:, :, e, bass.ds(c * CHUNK, CHUNK)].rearrange("h p t -> p h t"),
                                     qk[:, :, e, :]).then_inc(stored, 16)
            sp.wait_ge(stored, 32 * (1 + CHUNKS))
            for b in range(2):
                sp.wait_ge(v_stored[b], 16 * (1 + TILES // 2))

        def turn_order():
            return [(n, n - 2) for n in range(BANKS1)] + [(None, BANKS1 - 2)]

        @block.vector
        def _(dve):
            dve.sem_inc(freed, 3)
            dve.sem_inc(qk_low, 2)
            dve.wait_ge(loaded, 48)
            with dve.Fori(0, CHUNKS // 2) as i:
                for b in range(2):
                    nd.apply(dve, i * 2 + b, b)
                for b in range(2):
                    c = i * 2 + b
                    for j in range(CT):
                        t = c * CT + j
                        for n, r in turn_order():
                            if n is not None and n < ROT:
                                dve.wait_ge(product, t * BANKS1 + n + 1)
                                g = j * ROT + n
                                dve.wait_ge(rot_ready, t * ROT + n + 1)
                                ps = qkv_ps[:, n % 3, :].rearrange("p (h a w) -> p (h a) w", h=HPB, a=2)
                                for tab, out in ((cos, xc), (sin, xs)):
                                    ins = dve.tensor_tensor(
                                        out[:, g % 2, :, :, :].rearrange("p h a w -> p (h a) w"), ps,
                                        bcast(tab[:, bass.ds(t, 1), :], [P, 2 * HPB, D1 // 2]), ALU.mult)
                                    ins.then_inc(scaled, 1)
                                dve.wait_ge(scaled, (t * ROT + n + 1) * 2)
                                dve.sem_inc(freed, 1)
                            elif n == ROT:
                                dve.wait_ge(v_high, t + 1)
                                dve.tensor_tensor(v[:, j % 2, 1, :], qkv_ps[:, n % 3, :], v[:, j % 2, 0, :],
                                                  ALU.subtract).then_inc(v_low, 1)
                                dve.wait_ge(v_low, t + 1)
                                dve.sem_inc(freed, 1)
                            if r is not None and 0 <= r < ROT:
                                dve.wait_ge(qk_high, t * ROT + r + 1)
                                g = j * ROT + r
                                dve.tensor_tensor(
                                    qk[:, r * HPB:(r + 1) * HPB, 1, j * P:(j + 1) * P],
                                    turned_ps[:, g % 2, :].rearrange("p (h t) -> p h t", h=HPB),
                                    qk[:, r * HPB:(r + 1) * HPB, 0, j * P:(j + 1) * P], ALU.subtract) \
                                   .then_inc(qk_low, 1)

        @block.gpsimd
        def _(pool):
            pool.sem_inc(rot_ready, 2)
            with pool.Fori(0, CHUNKS // 2) as i:
                for b in range(2):
                    for j in range(CT):
                        t = (i * 2 + b) * CT + j
                        for n in range(ROT):
                            g = j * ROT + n
                            pool.wait_ge(scaled, (t * ROT + n + 1) * 2)
                            pool.wait_ge(rot_turned, t * ROT + n + 1)
                            out = rot[:, g % 2, :, :].rearrange("p h (a w) -> p h a w", a=2)
                            pool.tensor_tensor(out[:, :, 0, :], xc[:, g % 2, :, 0, :], xs[:, g % 2, :, 1, :],
                                               ALU.subtract)
                            pool.tensor_tensor(out[:, :, 1, :], xc[:, g % 2, :, 1, :], xs[:, g % 2, :, 0, :],
                                               ALU.add).then_inc(rot_ready, 1)

        @block.scalar
        def _(act):
            nd.prime_act(act)
            with act.Fori(0, CHUNKS // 2) as i:
                for b in range(2):
                    nd.keep(act, i * 2 + b, b)
                for b in range(2):
                    c = i * 2 + b
                    act.wait_ge(stored, (c + 1) * 32)
                    for j in range(CT):
                        t = c * CT + j
                        for n, r in turn_order():
                            if n == ROT:
                                act.wait_ge(product, t * BANKS1 + n + 1)
                                act.wait_ge(v_stored[j % 2], c * 32 + (j // 2 + 1) * 16)
                                act.activation(v[:, j % 2, 0, :], qkv_ps[:, n % 3, :], ACT.Copy).then_inc(v_high, 1)
                            if r is not None and 0 <= r < ROT:
                                g = j * ROT + r
                                act.wait_ge(rot_turned, 2 + t * ROT + r + 1)
                                act.activation(qk[:, r * HPB:(r + 1) * HPB, 0, j * P:(j + 1) * P],
                                               turned_ps[:, g % 2, :].rearrange("p (h t) -> p h t", h=HPB),
                                               ACT.Copy).then_inc(qk_high, 1)

        @block.tensor
        def _(pe):
            nd.prime_pe(pe)
            pe.sem_inc(rot_turned, 2)
            pe.wait_ge(loaded, 48)
            with pe.Fori(0, CHUNKS // 2) as i:
                for b in range(2):
                    nd.turn(pe, i * 2 + b, b)
                for b in range(2):
                    c = i * 2 + b
                    nd.wait_xnT(pe, c)
                    for j in range(CT):
                        t = c * CT + j
                        for n, r in turn_order():
                            if n is not None:
                                pe.wait_ge(freed, t * BANKS1 + n + 1)
                                for kt in range(KD):
                                    ins = pe.matmul(qkv_ps[:, n % 3, :], nd.xnT[:, b, kt, j * P:(j + 1) * P],
                                                    w[:, kt, n * CHUNK:(n + 1) * CHUNK], start=(kt == 0),
                                                    stop=(kt == KD - 1))
                                ins.then_inc(product, 1)
                            if r is not None and 0 <= r < ROT:
                                g = j * ROT + r
                                pe.wait_ge(rot_ready, 2 + t * ROT + r + 1)
                                pe.wait_ge(qk_low, t * ROT + r + 1)
                                for h in range(HPB):
                                    ins = pe.transpose(turned_ps[:, g % 2, h * P:(h + 1) * P], rot[:, g % 2, h, :],
                                                       k.ident[:, :])
                                ins.then_inc(rot_turned, 1)
                    pe.wait_ge(product, (c + 1) * CT * BANKS1)
                    pe.sem_inc(nd.xnT_used, 1)


class Attn1Plan:

    units = [(c, kp) for c in range(CHUNKS) for kp in range(2 * c + 2)]
    maxima = [(qt, kc) for qt in range(TILES) for kc in range(qt // CT + 1)]
    UNITS, MAXIMA, LEAD = len(units), len(maxima), 6
    LAG = 2
    RING = 4

    @classmethod
    def maxima_at(cls, u):
        n, left = u - cls.LEAD, cls.UNITS - cls.LEAD
        return range(n * cls.MAXIMA // left, (n + 1) * cls.MAXIMA // left) if n >= 0 else range(0)

    @staticmethod
    def offset(c, kt):
        return max(0, kt - CT * c) * P


def attn1(nc, k, a):
    plan = Attn1Plan
    SCALE = float(D1) ** -0.5
    PU, PM = plan.UNITS, plan.MAXIMA
    with ExitStack() as stack:
        m = Core(nc, stack, "attn1_")
        q = m.sb("q", [P, 2, 2, T], F16)
        kk = m.sb("kk", [P, 2, 2, T], F16)
        v = m.sb("v", [P, 2, TILES, VL + D1], F16)
        part = m.sb("part", [P, TILES, CHUNKS])
        mx = m.sb("mx", [P, 2, TILES])
        diag = m.sb("diag", [P, 2, T], BF16)
        prob = m.sb("prob", [P, 2, 2, CHUNK])
        high = m.sb("high", [P, plan.RING, 2, CHUNK], F16)
        low = m.sb("low", [P, plan.RING, 2, CHUNK], F16)
        inv = m.sb("inv", [P, CT])
        att = m.sb("att", [P, 2, CT, D1])
        score_ps = m.ps("score_ps", [P, 2, 2, CHUNK])
        max_ps = m.ps("max_ps", [P, 2, CHUNK])
        o_ps = m.ps("o_ps", [P, CT, 256])
        loaded = [m.sem("loaded0"), m.sem("loaded1")]
        blank = m.sem("blank")
        max_done = m.sem("max_done")
        max_used = m.sem("max_used")
        mx_ready = m.sem("mx_ready")
        diag_ready = m.sem("diag_ready")
        scored = m.sem("scored")
        exped = m.sem("exped")
        low_ready = m.sem("low_ready")
        weighed = m.sem("weighed")
        inv_ready = m.sem("inv_ready")
        o_used = m.sem("o_used")
        stored = [m.sem("stored0"), m.sem("stored1")]
        block = stack.enter_context(nc.Block())

        def all_passes(eng, one_pass, first=None):
            if first:
                first()
            with eng.Fori(0, H1 // 2 - 1) as i:
                for b in range(2):
                    one_pass(i * 2 + b, b, True)
            one_pass(H1 - 2, 0, True)
            one_pass(H1 - 1, 1, False)

        @block.sync
        def _(sp):
            def load(h, b):
                g = h // (H1 // G1)
                sp.dma_start(q[:, b, :, :], a["qk1_scr"][bass.ds(h, 1), :, :, :].rearrange("o p e t -> p (o e) t")) \
                  .then_inc(loaded[b], 16)
                sp.dma_start(kk[:, b, :, :], a["qk1_scr"][bass.ds(g + H1, 1), :, :, :]
                             .rearrange("o p e t -> p (o e) t")).then_inc(loaded[b], 16)
                for e, at in ((0, 0), (1, VL)):
                    sp.dma_start(v[:, b, :, at:at + D1],
                                 a["v1_scr"][:, :, e, bass.ds(g * D1, D1)].rearrange("t p d -> p t d")) \
                      .then_inc(loaded[b], 16)

            def one_pass(h, b, nxt):
                if nxt:
                    sp.wait_ge(weighed, plan.RING + h * PU)
                    load(h + 1, 1 - b)
                for c in range(CHUNKS):
                    sp.wait_ge(o_used, 1 + h * CHUNKS + c + 1)
                    sp.dma_start(a["att_scr"][bass.ds(c * CT, CT), :, bass.ds(h * D1, D1)].rearrange("t p d -> p t d"),
                                 att[:, c % 2, :, :]).then_inc(stored[c % 2], 16)

            for b in range(2):
                sp.sem_inc(stored[b], 16)
            load(0, 0)
            all_passes(sp, one_pass)
            for b in range(2):
                sp.wait_ge(stored[b], 16 * (1 + H1 * CHUNKS // 2))

        @block.gpsimd
        def _(pool):
            pool.memset(part[:, :, :], NEG).then_inc(blank, 1)
            pool.wait_ge(blank, 1)
            pool.memset(v[:, :, :, D1:VL], 1.0).then_inc(blank, 1)
            pool.wait_ge(blank, 2)

            def make_diag(h, b):
                if not isinstance(h, int) or h > 0:
                    pool.wait_ge(weighed, plan.RING + (h - 1) * PU)
                for c in range(CHUNKS):
                    pool.wait_ge(mx_ready, h * CHUNKS + c + 1)
                    pool.tensor_tensor(
                        diag[:, b, c * CHUNK:(c + 1) * CHUNK].rearrange("p (t j) -> p t j", t=CT),
                        bcast(k.minusb[:, :].rearrange("p (o j) -> p o j", o=1), [P, CT, P]),
                        bcast(mx[:, b, CT * c:CT * c + CT].rearrange("p (t o) -> p t o", o=1), [P, CT, P]),
                        ALU.mult).then_inc(diag_ready, 1)

            def one_pass(h, b, nxt):
                if nxt:
                    make_diag(h + 1, 1 - b)

            all_passes(pool, one_pass, lambda: make_diag(0, 0))

        @block.vector
        def _(dve):
            dve.sem_inc(max_used, 2)
            dve.sem_inc(low_ready, 2)
            dve.sem_inc(o_used, 1)
            dve.wait_ge(blank, 2)

            def reduce_max(h, b, n):
                qt, kc = plan.maxima[n]
                w = min(CHUNK, (qt + 1) * P - kc * CHUNK)
                tile = h * PM + n
                dve.wait_ge(max_done, tile + 1)
                dve.tensor_reduce(part[:, qt, kc:kc + 1], max_ps[:, n % 2, 0:w], AX.X, ALU.max).then_inc(max_used, 1)
                if kc == qt // CT and qt % CT == CT - 1:
                    c = qt // CT
                    dve.wait_ge(max_used, 2 + tile + 1)
                    dve.tensor_reduce(mx[:, b, CT * c:CT * c + CT], part[:, CT * c:CT * c + CT, :], AX.X, ALU.max) \
                       .then_inc(mx_ready, 1)
                    dve.wait_ge(mx_ready, h * CHUNKS + c + 1)

            def put_out(h, c):
                dve.wait_ge(weighed, plan.RING + h * PU + (c + 1) * (c + 2))
                dve.reciprocal(inv[:, :], o_ps[:, :, D1:VO].rearrange("p t o -> p (t o)")).then_inc(inv_ready, 1)
                dve.wait_ge(inv_ready, h * CHUNKS + c + 1)
                dve.wait_ge(stored[c % 2], (h * 2 + c // 2 + 1) * 16)
                dve.tensor_tensor(att[:, c % 2, :, :], o_ps[:, :, 0:D1],
                                  bcast(inv[:, :].rearrange("p (t o) -> p t o", o=1), [P, CT, D1]), ALU.mult) \
                   .then_inc(o_used, 1)

            def one_pass(h, b, nxt):
                for u, (c, kp) in enumerate(plan.units):
                    if nxt:
                        for n in plan.maxima_at(u):
                            reduce_max(h + 1, 1 - b, n)
                    unit = h * PU + u
                    off = plan.offset(c, 2 * kp)
                    dve.wait_ge(exped, 2 + unit + 1)
                    dve.wait_ge(weighed, unit + 1)
                    dve.tensor_tensor(low[:, u % plan.RING, :, off:CHUNK], prob[:, u % 2, :, off:CHUNK],
                                      high[:, u % plan.RING, :, off:CHUNK], ALU.subtract).then_inc(low_ready, 1)
                    if c > 0 and kp == plan.LAG - 1:
                        put_out(h, c - 1)
                put_out(h, CHUNKS - 1)

            def first():
                for n in range(PM):
                    reduce_max(0, 0, n)

            all_passes(dve, one_pass, first)

        @block.scalar
        def _(act):
            act.sem_inc(exped, 2)

            def one_pass(h, b, nxt):
                for u, (c, kp) in enumerate(plan.units):
                    unit = h * PU + u
                    off = plan.offset(c, 2 * kp)
                    act.wait_ge(scored, unit + 1)
                    act.wait_ge(weighed, unit + 1)
                    act.wait_ge(low_ready, unit + 1)
                    act.activation(high[:, u % plan.RING, :, off:CHUNK], score_ps[:, u % 2, :, off:CHUNK], ACT.Exp,
                                   scale=SCALE)
                    act.activation(prob[:, u % 2, :, off:CHUNK], score_ps[:, u % 2, :, off:CHUNK], ACT.Exp,
                                   scale=SCALE).then_inc(exped, 1)

            all_passes(act, one_pass)

        @block.tensor
        def _(pe):
            pe.sem_inc(weighed, plan.RING)
            pe.wait_ge(blank, 2)

            def max_tile(h, b, n):
                qt, kc = plan.maxima[n]
                w = min(CHUNK, (qt + 1) * P - kc * CHUNK)
                diagonal = kc == qt // CT
                pe.wait_ge(max_used, h * PM + n + 1)
                ins = pe.matmul(max_ps[:, n % 2, 0:w], q[:, b, 0, qt * P:(qt + 1) * P],
                                kk[:, b, 0, kc * CHUNK:kc * CHUNK + w], start=True, stop=not diagonal)
                if diagonal:
                    ins = pe.matmul(max_ps[:, n % 2, w - P:w], k.identb[:, :], k.mask_qk[:, :], start=False, stop=True)
                ins.then_inc(max_done, 1)

            def score(h, b, u, s):
                c, kp = plan.units[u]
                unit = h * PU + u
                if s == 0:
                    pe.wait_ge(exped, unit + 1)
                    if kp == 0:
                        pe.wait_ge(diag_ready, h * CHUNKS + c + 1)
                kt = 2 * kp + s
                off = plan.offset(c, 2 * kp)
                out = score_ps[:, u % 2, s, off:CHUNK]
                queries = slice(c * CHUNK + off, (c + 1) * CHUNK)
                keys = slice(kt * P, (kt + 1) * P)
                diagonal = kt >= CT * c
                pe.matmul(out, kk[:, b, 0, keys], q[:, b, 0, queries], start=True, stop=False)
                pe.matmul(out, kk[:, b, 0, keys], q[:, b, 1, queries], start=False, stop=False)
                pe.matmul(out, kk[:, b, 1, keys], q[:, b, 0, queries], start=False, stop=False)
                ins = pe.matmul(out, k.onesb[:, :], diag[:, b, queries], start=False, stop=not diagonal)
                if diagonal:
                    at = plan.offset(c, kt)
                    ins = pe.matmul(score_ps[:, u % 2, s, at:at + P], k.identb[:, :], k.mask_kq[:, :],
                                    start=False, stop=True)
                if s == 1:
                    ins.then_inc(scored, 1)

            def weigh(h, b, u, s):
                c, kp = plan.units[u]
                if s == 0:
                    pe.wait_ge(low_ready, 2 + h * PU + u + 1)
                    if kp == 0:
                        pe.wait_ge(o_used, h * CHUNKS + c + 1)
                kt = 2 * kp + s
                vh, vl = v[:, b, kt, 0:VO], v[:, b, kt, VL:VL + D1]
                for t in range(plan.offset(c, kt) // P, CT):
                    ph, pl = (p[:, u % plan.RING, s, t * P:(t + 1) * P] for p in (high, low))
                    start = kt == 0 and t % 2 == 0
                    pe.matmul(o_ps[:, t, 0:VO], ph, vh, start=start, stop=False, skip_group_check=True)
                    pe.matmul(o_ps[:, t, 0:D1], ph, vl, start=False, stop=False, skip_group_check=True)
                    ins = pe.matmul(o_ps[:, t, 0:VO], pl, vh, start=False, stop=(kp == 2 * c + 1 and s == 1),
                                    skip_group_check=True)
                if s == 1:
                    ins.then_inc(weighed, 1)

            def one_pass(h, b, nxt):
                for u in range(PU + plan.LAG):
                    if nxt and u == plan.LEAD:
                        pe.wait_ge(loaded[1 - b], 64 * ((h + 1) // 2 + 1))
                    tiles = list(plan.maxima_at(u)) if nxt and u < PU else []
                    parts = [(score, u, s) for s in range(2) if u < PU]
                    parts += [(weigh, u - plan.LAG, s) for s in range(2) if u >= plan.LAG]
                    for part, unit, s in parts:
                        part(h, b, unit, s)
                        if tiles:
                            max_tile(h + 1, 1 - b, tiles.pop(0))
                    for n in tiles:
                        max_tile(h + 1, 1 - b, n)

            def first():
                pe.wait_ge(loaded[0], 64)
                for n in range(PM):
                    max_tile(0, 0, n)

            all_passes(pe, one_pass, first)


def wo1(nc, k, a):
    HB = H1 // 4
    with ExitStack() as stack:
        m = Core(nc, stack, "wo1_")
        wo = m.sb("wo", [P, H1, D])
        att = m.sb("att", [P, 2, H1, D1])
        attT = m.sb("attT", [P, 2, H1, P])
        turned_ps = m.ps("turned_ps", [P, 4, CHUNK])
        out_ps = m.ps("out_ps", [P, 2, CHUNK])
        loaded = m.sem("loaded")
        att_in = [m.sem("att_in0"), m.sem("att_in1")]
        turned = m.sem("turned")
        kept = m.sem("kept")
        done = m.sem("done")
        used = m.sem("used")
        block = stack.enter_context(nc.Block())

        @block.sync
        def _(sp):
            sp.dma_start(wo[:, :, :], a["wo1"].rearrange("(h p) c -> p h c", p=P)).then_inc(loaded, 16)
            with sp.Fori(0, TILES // 2) as i:
                for b in range(2):
                    t = i * 2 + b
                    sp.wait_ge(turned, (i + 1) * 8)
                    sp.dma_start(att[:, b, :, :].rearrange("p h d -> p (h d)"),
                                 a["att_scr"][bass.ds(t, 1), :, :].rearrange("o p c -> (o p) c")) \
                      .then_inc(att_in[b], 16)
            sp.wait_ge(loaded, 16)

        @block.scalar
        def _(act):
            act.sem_inc(kept, 4)
            with act.Fori(0, TILES // 2) as i:
                for b in range(2):
                    t = i * 2 + b
                    act.wait_ge(used, t + 1)
                    for n in range(4):
                        act.wait_ge(turned, 8 + t * 4 + n + 1)
                        act.activation(attT[:, b, n * HB:(n + 1) * HB, :].rearrange("p h t -> p (h t)"),
                                       turned_ps[:, n, :], ACT.Copy).then_inc(kept, 1)

        @block.vector
        def _(dve):
            dve.sem_inc(used, 2)
            with dve.Fori(0, TILES // 2) as i:
                for b in range(2):
                    t = i * 2 + b
                    x = k.x[:, bass.ds(t, 1), :]
                    dve.wait_ge(done, t + 1)
                    dve.tensor_tensor(x, x, out_ps[:, b:b + 1, 0:D], ALU.add).then_inc(used, 1)

        @block.tensor
        def _(pe):
            pe.sem_inc(turned, 8)
            pe.wait_ge(loaded, 16)

            def turn(i, b):
                t = i * 2 + b
                pe.wait_ge(att_in[b], i * 16 + 16)
                for n in range(4):
                    pe.wait_ge(kept, t * 4 + n + 1)
                    for h in range(HB):
                        ins = pe.transpose(turned_ps[:, n, h * P:(h + 1) * P], att[:, b, n * HB + h, :],
                                           k.ident[:, :])
                    ins.then_inc(turned, 1)

            def product(i, b):
                t = i * 2 + b
                pe.wait_ge(kept, 4 + (t + 1) * 4)
                pe.wait_ge(used, t + 1)
                for h in range(H1):
                    ins = pe.matmul(out_ps[:, b, 0:D], attT[:, b, h, :], wo[:, h, :], start=(h == 0),
                                    stop=(h == H1 - 1))
                ins.then_inc(done, 1)

            with pe.Fori(0, TILES // 2) as i:
                for b in range(2):
                    turn(i, b)
                for b in range(2):
                    product(i, b)


def store(nc, k, a):
    with ExitStack() as stack:
        stored = Core(nc, stack, "st_").sem("stored")
        with nc.Block() as block:

            @block.sync
            def _(sp):
                sp.dma_start(a["out"].rearrange("o (t p) d -> p (o t) d", p=P), k.x[:, :, :]).then_inc(stored, 16)
                sp.wait_ge(stored, 16)


def program(nc, a, stages=9, start=0):
    a["q0_scr"] = nc.dram_tensor("q0_scr", (2, P, 2, T), F16, kind="Internal").ap()
    a["k0_scr"] = nc.dram_tensor("k0_scr", (G0 * D0, 2, T), F16, kind="Internal").ap()
    a["qk1_scr"] = nc.dram_tensor("qk1_scr", (H1 + G1, D1, 2, T), F16, kind="Internal").ap()
    a["v1_scr"] = nc.dram_tensor("v1_scr", (TILES, P, 2, G1 * D1), F16, kind="Internal").ap()
    a["att_scr"] = nc.dram_tensor("att_scr", (TILES, P, H1 * D1), F32, kind="Internal").ap()
    with ExitStack() as stack:
        k = Core(nc, stack)
        k.x = k.sb("x", [P, TILES, D])
        k.rstd = k.sb("rstd", [P, TILES])
        k.shift = k.sb("shift", [P, TILES])
        k.length2 = k.sb("length2", [P, TILES])
        k.ident = k.sb("ident", [P, P])
        k.identb = k.sb("identb", [P, P], BF16)
        k.minusb = k.sb("minusb", [P, P], BF16)
        k.mask_qk = k.sb("mask_qk", [P, P], BF16)
        k.mask_kq = k.sb("mask_kq", [P, P], BF16)
        k.ones = k.sb("ones", [P, P])
        k.onesb = k.sb("onesb", [P, P], BF16)
        k.eps = k.sb("eps", [P, 1])
        k.rev = k.sb("rev", [P, CT, N0])
        setup(nc, k, a)
        if start < 1 <= stages:
            norm_stats(nc, k, "n1_")
            ffn0(nc, k, a, "f1_")
        if start < 2 <= stages:
            with ExitStack() as inner:
                m = Core(nc, inner, "a0_")
                v_aug = m.sb("v_aug", [P, TILES, G0, VW])
                att = m.sb("att", [P, TILES, H0, D0])
                norm_stats(nc, k, "n2_")
                qkv0(nc, k, a, v_aug)
                attn0(nc, k, a, v_aug, att)
                wo0(nc, k, a, att)
        if start < 3 <= stages:
            norm_stats(nc, k, "n3_")
            ffn0(nc, k, a, "f3_")
        if start < 4 <= stages:
            norm_stats(nc, k, "n4_")
            ffn1(nc, k, a, "f4_")
        if start < 5 <= stages:
            norm_stats(nc, k, "n5_")
            qkv1(nc, k, a)
            attn1(nc, k, a)
            wo1(nc, k, a)
        if start < 6 <= stages:
            norm_stats(nc, k, "n6_")
            ffn1(nc, k, a, "f6_")
        store(nc, k, a)


def laid_out(inputs):
    import numpy as np

    i = {n: np.asarray(v) for n, v in inputs.items()}
    c = np.ascontiguousarray

    def on_all(row):
        return c(np.broadcast_to(row[None, :], (P, row.shape[0])))

    def columns(w):
        return np.transpose(w, (1, 0, 2)).reshape(D, -1)

    smd = i["L0_ffn_select_mean_diff"].T
    w1, w2, w3 = (np.concatenate([i[f"L1_ffn_W{n}"], i[f"L1_ffn_Ws{n}"][None]], 0) for n in (1, 2, 3))
    freqs = np.float32(1.0) / np.power(np.float32(10000.0), np.arange(0, D1, 2, dtype=np.float32) / np.float32(D1))
    angle = np.arange(T, dtype=np.float32)[:, None] * freqs[None, :]
    cos, sin = np.cos(angle), np.sin(angle)
    return {
        "x": i["L0_attn_x"],
        "ffn0_w": c(np.concatenate([columns(i["L0_ffn_select_weight"]), columns(i["L0_ffn_lora_update"]), smd], 1)),
        "ffn0_other": c(np.concatenate([np.repeat(smd, S0, 1), np.repeat(i["L0_ffn_debias_w"].T, S0, 1), smd], 1)),
        "ffn0_w2": c(np.concatenate([np.transpose(i["L0_ffn_lora_degen"], (0, 2, 1)).reshape(-1, D),
                                     i["L0_ffn_bias_w"]], 0)),
        "ffn0_center": on_all(i["L0_ffn_imp_center"]),
        "ffn0_slope": on_all(i["L0_ffn_imp_slope"]),
        "wq0": i["L0_attn_Wq"], "wk0": i["L0_attn_Wk"], "wv0": i["L0_attn_Wv"], "wo0": i["L0_attn_Wo"],
        "bq0": c(i["L0_attn_bq"].reshape(2, P).T), "bk0": i["L0_attn_bk"], "bv0": on_all(i["L0_attn_bv"]),
        "bo0": on_all(i["L0_attn_bo"]),
        "gate1_w": c(i["L1_ffn_gate_w"].T), "gate1_b": on_all(i["L1_ffn_gate_b"]),
        "w13": c(np.stack([w1, w3], 1).reshape(X1 * 2 * I1, D).T), "w2": c(np.transpose(w2, (0, 2, 1))),
        "wqkv1": i["L1_attn_Wqkv"], "wo1": i["L1_attn_Wo"], "cos": cos, "sin": sin,
    }


def kernel(**inputs):
    import concourse.bacc as bacc
    from concourse.bass_utils import run_bass_kernel_spmd

    nc = bacc.Bacc("TRN2", target_bir_lowering=False, num_devices=1)
    arrays, a = {}, {}
    for name, value in laid_out(inputs).items():
        arrays["in_" + name] = value
        a[name] = nc.dram_tensor("in_" + name, value.shape, mybir.dt.from_np(value.dtype), kind="ExternalInput").ap()
    a["out"] = nc.dram_tensor("out", (1, T, D), F32, kind="ExternalOutput").ap()
    program(nc, a)
    return run_bass_kernel_spmd(nc, [arrays], core_ids=[0]).results[0]["out"]
```

```python
from contextlib import ExitStack
from itertools import product

import concourse.bass as bass
from concourse import mybir

F32 = mybir.dt.float32
F16 = mybir.dt.float16
BF16 = mybir.dt.bfloat16
ACT = mybir.ActivationFunctionType
ALU = mybir.AluOpType
AX = mybir.AxisListType

P = 128
T = 2048
D = 256
TILES = T // P
CT = 4
CHUNK = CT * P
CHUNKS = T // CHUNK
KD = D // P
EPS = 1e-5
NEG = -1e30

N0, S0 = 8, 8
C0 = 2 * N0 * S0 + N0
R0 = N0 * S0 + N0

H0, G0, D0 = 16, 2, 16
QUAD = 4
QUADS = H0 // QUAD
PAIRS0 = ((0, 0), (1, 0), (0, 1), (1, 1))
VW = 32

E1, I1 = 8, 128
X1 = E1 + 1
H1, G1, D1 = 16, 4, 128
QKV1 = (H1 + 2 * G1) * D1
VO = D1 + 1
VL = D1 + 2


class Steps:

    def __init__(self, eng, sem, base=0):
        self.eng, self.sem, self.base, self.n = eng, sem, base, 0

    def mark(self, ins):
        self.n += 1
        ins.then_inc(self.sem, 1)
        return ins

    def wait(self):
        self.eng.wait_ge(self.sem, self.base + self.n)

    def link(self, ins):
        self.mark(ins)
        self.wait()


class Core:

    def __init__(self, nc, stack, prefix=""):
        self.nc, self.stack, self.prefix, self.sems = nc, stack, prefix, []
        stack.callback(self.clear)

    def clear(self):
        if self.sems:
            self.nc.clear_and_free_semaphores(self.sems)
            self.nc.all_engine_barrier()

    def sb(self, name, shape, dt=F32):
        return self.stack.enter_context(self.nc.sbuf_tensor(self.prefix + name, list(shape), dt))

    def ps(self, name, shape, dt=F32):
        return self.stack.enter_context(self.nc.psum_tensor(self.prefix + name, list(shape), dt))

    def sem(self, name):
        self.sems.append(self.nc.alloc_semaphore(self.prefix + name))
        return self.sems[-1]


def bcast(ap, shape):
    return ap.broadcast_to(list(shape))


def setup(nc, k, a):
    with ExitStack() as stack:
        m = Core(nc, stack, "su_")
        loaded, blank, made = m.sem("loaded"), m.sem("blank"), m.sem("made")
        with nc.Block() as block:

            @block.sync
            def _(sp):
                sp.dma_start(k.x[:, :, :], a["x"].rearrange("o (t p) d -> p (o t) d", p=P)).then_inc(loaded, 16)
                sp.wait_ge(loaded, 16)

            @block.gpsimd
            def _(pool):
                pool.memset(k.ident[:, :], 0.0).then_inc(blank, 1)
                pool.memset(k.identb[:, :], 0.0).then_inc(blank, 1)
                pool.memset(k.minusb[:, :], 0.0).then_inc(blank, 1)
                pool.memset(k.mask_qk[:, :], 0.0).then_inc(blank, 1)
                pool.memset(k.mask_kq[:, :], 0.0).then_inc(blank, 1)
                pool.memset(k.ones[:, :], 1.0).then_inc(made, 1)
                pool.memset(k.onesb[:, :], 1.0).then_inc(made, 1)
                pool.memset(k.eps[:, :], EPS).then_inc(made, 1)
                for n in range(N0):
                    pool.memset(k.rev[:, :, n:n + 1], float(N0 - n)).then_inc(made, 1)
                pool.wait_ge(blank, 5)
                for t, one in ((k.ident, 1.0), (k.identb, 1.0), (k.minusb, -1.0)):
                    pool.affine_select(out=t[:, :], in_=t[:, :], compare_op=ALU.not_equal, fill=one, base=0,
                                       pattern=[[-1, P]], channel_multiplier=1).then_inc(made, 1)
                pool.affine_select(out=k.mask_qk[:, :], in_=k.mask_qk[:, :], compare_op=ALU.is_ge, fill=NEG,
                                   base=0, pattern=[[-1, P]], channel_multiplier=1).then_inc(made, 1)
                pool.affine_select(out=k.mask_kq[:, :], in_=k.mask_kq[:, :], compare_op=ALU.is_ge, fill=NEG,
                                   base=0, pattern=[[1, P]], channel_multiplier=-1).then_inc(made, 1)
                pool.wait_ge(made, 3 + N0 + 5)


def norm_stats(nc, k, name):
    with ExitStack() as stack:
        m = Core(nc, stack, name)
        bn = m.sb("bn", [P, TILES, 6])
        mv = m.sb("mv", [P, TILES, 2])
        std = m.sb("std", [P, TILES])
        r0 = m.sb("r0", [P, TILES])
        vr = m.sb("vr", [P, TILES])
        half = m.sb("half", [P, TILES])
        steps, rooted = m.sem("steps"), m.sem("rooted")
        var_ready = m.sem("var_ready")
        with nc.Block() as block:

            @block.vector
            def _(dve):
                s = Steps(dve, steps)
                for t in range(TILES):
                    s.mark(dve.bn_stats(bn[:, t, :], k.x[:, t, :]))
                s.wait()
                for t in range(TILES):
                    ins = dve.bn_aggr(mv[:, t, :], bn[:, t, :])
                    if t < TILES - 1:
                        s.mark(ins)
                ins.then_inc(var_ready, 1)
                dve.wait_ge(var_ready, 1)
                s.link(dve.tensor_scalar(vr[:, :], mv[:, :, 1], EPS, None, ALU.add))
                dve.wait_ge(rooted, 1)
                s.link(dve.reciprocal(r0[:, :], std[:, :]))
                s.link(dve.tensor_tensor(half[:, :], r0[:, :], r0[:, :], ALU.mult))
                s.link(dve.tensor_tensor(half[:, :], half[:, :], vr[:, :], ALU.mult))
                s.link(dve.tensor_scalar(half[:, :], half[:, :], -0.5, 1.5, ALU.mult, ALU.add))
                s.link(dve.tensor_tensor(k.rstd[:, :], r0[:, :], half[:, :], ALU.mult))
                s.link(dve.scalar_tensor_tensor(out=k.shift[:, :], in0=mv[:, :, 0], scalar=-1.0,
                                                in1=k.rstd[:, :], op0=ALU.mult, op1=ALU.mult))
                s.link(dve.tensor_tensor(half[:, :], k.rstd[:, :], k.rstd[:, :], ALU.mult))
                s.link(dve.scalar_tensor_tensor(out=k.length2[:, :], in0=mv[:, :, 1], scalar=float(D),
                                                in1=half[:, :], op0=ALU.mult, op1=ALU.mult))

            @block.scalar
            def _(act):
                act.wait_ge(var_ready, 1)
                act.activation(std[:, :], mv[:, :, 1], ACT.Sqrt, bias=k.eps[:, 0:1]).then_inc(rooted, 1)


class Normed:

    RING = 2

    def __init__(self, m, k, banks=2):
        self.k, self.banks = k, banks
        self.xn = m.sb("xn", [P, self.RING, CT, D])
        self.xnT = m.sb("xnT", [P, self.RING, KD, CHUNK])
        self.turned_ps = m.ps("turned_ps", [P, banks, CHUNK])
        self.xn_ready = m.sem("xn_ready")
        self.turned = m.sem("turned")
        self.xnT_ready = m.sem("xnT_ready")
        self.xnT_used = m.sem("xnT_used")

    def apply(self, dve, c, b):
        k = self.k
        dve.wait_ge(self.xnT_used, c + 1)
        for j in range(CT):
            t = c * CT + j
            ins = dve.tensor_scalar(self.xn[:, b, j:j + 1, :], k.x[:, bass.ds(t, 1), :], k.rstd[:, bass.ds(t, 1)],
                                    k.shift[:, bass.ds(t, 1)], ALU.mult, ALU.add)
        ins.then_inc(self.xn_ready, 1)

    def prime_pe(self, pe):
        pe.sem_inc(self.xnT_used, self.RING)

    def prime_act(self, act):
        act.sem_inc(self.xnT_ready, self.banks)

    def turn(self, pe, c, b):
        pe.wait_ge(self.xn_ready, c + 1)
        for h in range(KD):
            pe.wait_ge(self.xnT_ready, c * KD + h + 1)
            for j in range(CT):
                ins = pe.transpose(self.turned_ps[:, h % self.banks, j * P:(j + 1) * P],
                                   self.xn[:, b, j, h * P:(h + 1) * P], self.k.ident[:, :])
            ins.then_inc(self.turned, 1)

    def keep(self, act, c, b):
        act.wait_ge(self.xnT_used, c + 1)
        for h in range(KD):
            act.wait_ge(self.turned, c * KD + h + 1)
            act.activation(self.xnT[:, b, h, :], self.turned_ps[:, h % self.banks, :], ACT.Copy) \
               .then_inc(self.xnT_ready, 1)

    def wait_xnT(self, eng, c):
        eng.wait_ge(self.xnT_ready, self.banks + (c + 1) * KD)


PRODUCT = ((0, 0), (0, 1), (1, 0))
W_SCALE = 64.0


class NormedPieces:

    def __init__(self, m, k, turned_ps):
        self.k, self.turned_ps = k, turned_ps
        self.xn = m.sb("xn", [P, TILES, D])
        self.xT = m.sb("xT", [P, 2, KD, T], F16)
        self.xn_ready = m.sem("xn_ready")
        self.turned = m.sem("turned")
        self.high = m.sem("high")
        self.low = m.sem("low")

    def halves(self):
        return [(n // KD, n % KD, n % 2, n) for n in range(CHUNKS * KD)]

    def make_pieces(self, act):
        for c, h, bank, n in self.halves():
            act.wait_ge(self.turned, n + 1)
            act.activation(self.xT[:, 0, h, c * CHUNK:(c + 1) * CHUNK], self.turned_ps[:, bank, :], ACT.Copy) \
               .then_inc(self.high, 1)

    def norm(self, dve):
        k = self.k
        dve.sem_inc(self.low, 2)

        def apply(c):
            for t in range(c * CT, (c + 1) * CT):
                ins = dve.tensor_scalar(self.xn[:, t, :], k.x[:, t, :], k.rstd[:, t:t + 1], k.shift[:, t:t + 1],
                                        ALU.mult, ALU.add)
            ins.then_inc(self.xn_ready, 1)

        apply(0)
        for c, h, bank, n in self.halves():
            if h == 0 and c + 1 < CHUNKS:
                apply(c + 1)
            at = slice(c * CHUNK, (c + 1) * CHUNK)
            dve.wait_ge(self.high, n + 1)
            dve.tensor_tensor(self.xT[:, 1, h, at], self.turned_ps[:, bank, :], self.xT[:, 0, h, at],
                              ALU.subtract).then_inc(self.low, 1)

    def turn(self, pe):
        for c, h, bank, n in self.halves():
            pe.wait_ge(self.xn_ready, c + 1)
            pe.wait_ge(self.low, n + 1)
            for j in range(CT):
                ins = pe.transpose(self.turned_ps[:, bank, j * P:(j + 1) * P],
                                   self.xn[:, c * CT + j, h * P:(h + 1) * P], self.k.ident[:, :])
            ins.then_inc(self.turned, 1)
        pe.wait_ge(self.low, 2 + CHUNKS * KD)


class Weights:

    def __init__(self, m, name, source, columns):
        self.name, self.source, self.columns = name, source, columns
        self.pieces = m.sb(name, [P, 2, columns], F16)

    def open(self, m):
        self.raw = m.sb(self.name + "_raw", [P, self.columns])
        self.loaded, self.steps = m.sem(self.name + "_loaded"), m.sem(self.name + "_steps")

    def load(self, sp):
        w = self.source
        raw = self.raw[:, :] if len(w.shape) == 2 else self.raw[:, :].rearrange("p (k c) -> p k c", k=w.shape[1])
        sp.dma_start(raw, w).then_inc(self.loaded, 16)

    def split(self, pool):
        s = Steps(pool, self.steps)
        pool.wait_ge(self.loaded, 16)
        for at in range(0, self.columns, PIECE):
            cols = slice(at, min(at + PIECE, self.columns))
            s.link(pool.tensor_scalar(self.raw[:, cols], self.raw[:, cols], W_SCALE, None, ALU.mult))
            s.link(pool.tensor_copy(self.pieces[:, 0, cols], self.raw[:, cols]))
            s.link(pool.tensor_tensor(self.pieces[:, 1, cols], self.raw[:, cols], self.pieces[:, 0, cols],
                                      ALU.subtract))


PIECE = 2048


FFN0_STEPS = 20


def ffn0(nc, k, a, name, prefetch=()):
    with ExitStack() as stack:
        m = Core(nc, stack, name)
        for weights in prefetch:
            weights.open(m)
        w = m.sb("w", [P, KD, C0])
        w2 = m.sb("w2", [R0, D])
        other = m.sb("other", [P, KD, C0])
        center = m.sb("center", [P, N0])
        slope = m.sb("slope", [P, N0])
        const = m.sb("const", [P, C0])
        nd = Normed(m, k)
        y = m.sb("y", [P, 2, CT, C0])
        sq = m.sb("sq", [P, CT, N0 * S0])
        score = m.sb("score", [P, CT, N0])
        len2 = m.sb("len2", [P, CT, N0])
        inv = m.sb("inv", [P, CT, N0])
        z = m.sb("z", [P, CT, N0])
        ez = m.sb("ez", [P, CT, N0])
        gate = m.sb("gate", [P, CT, N0])
        best = m.sb("best", [P, CT])
        first = m.sb("first", [P, CT])
        keepc = m.sb("keepc", [P, CT])
        mod = m.sb("mod", [P, CT, R0])
        modT = m.sb("modT", [R0, CHUNK])
        w_ps = m.ps("w_ps", [P, CT, 256])
        mod_ps = m.ps("mod_ps", [P, CHUNK])
        out_ps = m.ps("out_ps", [P, CT, D])
        loaded = m.sem("loaded")
        prepared, const_ps_ready, const_ready = m.sem("prepared"), m.sem("const_ps_ready"), m.sem("const_ready")
        first_done = m.sem("first_done")
        y_ready = m.sem("y_ready")
        z_ready = m.sem("z_ready")
        ez_ready = m.sem("ez_ready")
        mod_ready = m.sem("mod_ready")
        mod_turned = m.sem("mod_turned")
        modT_ready = m.sem("modT_ready")
        out_done = m.sem("out_done")
        out_used = m.sem("out_used")
        steps = m.sem("steps")
        block = stack.enter_context(nc.Block())

        @block.sync
        def _(sp):
            sp.dma_start(w[:, :, :], a["ffn0_w"].rearrange("(k p) c -> p k c", p=P)).then_inc(loaded, 16)
            sp.dma_start(other[:, :, :], a["ffn0_other"].rearrange("(k p) c -> p k c", p=P)).then_inc(loaded, 16)
            sp.dma_start(w2[:, :], a["ffn0_w2"]).then_inc(loaded, 16)
            sp.dma_start(center[:, :], a["ffn0_center"]).then_inc(loaded, 16)
            sp.dma_start(slope[:, :], a["ffn0_slope"]).then_inc(loaded, 16)
            for weights in prefetch:
                weights.load(sp)
            sp.wait_ge(loaded, 80)

        @block.gpsimd
        def _(pool):
            for weights in prefetch:
                weights.split(pool)

        @block.vector
        def _(dve):
            dve.sem_inc(y_ready, 1)
            dve.sem_inc(out_used, 1)
            dve.wait_ge(loaded, 80)
            dve.tensor_tensor(other[:, :, :], other[:, :, :], w[:, :, :], ALU.mult).then_inc(prepared, 1)
            dve.wait_ge(const_ps_ready, 1)
            dve.tensor_copy(const[:, 0:C0 - N0], w_ps[:, 0, 0:C0 - N0]).then_inc(const_ready, 1)
            dve.tensor_scalar(const[:, C0 - N0:C0], w_ps[:, 0, C0 - N0:C0], 0.5, None, ALU.mult) \
               .then_inc(const_ready, 1)
            dve.wait_ge(const_ready, 2)
            with dve.Fori(0, CHUNKS // 2) as i:
                s = Steps(dve, steps, i * (2 * FFN0_STEPS))
                for b in range(2):
                    nd.apply(dve, i * 2 + b, b)
                for b in range(2):
                    c = i * 2 + b
                    yb = y[:, b, :, :]
                    t0 = c * CT
                    dve.wait_ge(first_done, c + 1)
                    dve.tensor_tensor(yb, w_ps[:, :, 0:C0], bcast(const[:, :].rearrange("p (o c) -> p o c", o=1),
                                                                 [P, CT, C0]), ALU.subtract).then_inc(y_ready, 1)
                    dve.wait_ge(y_ready, 1 + c + 1)
                    s.mark(dve.tensor_tensor(sq[:, :, :], yb[:, :, 0:64], yb[:, :, 0:64], ALU.mult))
                    s.link(dve.scalar_tensor_tensor(
                        out=len2[:, :, :], in0=yb[:, :, C0 - N0:C0], scalar=-2.0,
                        in1=bcast(k.length2[:, bass.ds(t0, CT)].rearrange("p (c o) -> p c o", o=1), [P, CT, N0]),
                        op0=ALU.mult, op1=ALU.add))
                    s.mark(dve.tensor_reduce(score[:, :, :], sq[:, :, :].rearrange("p c (n s) -> p c n s", s=S0),
                                             AX.X, ALU.add))
                    s.link(dve.reciprocal(inv[:, :, :], len2[:, :, :]))
                    s.link(dve.tensor_tensor(score[:, :, :], score[:, :, :], inv[:, :, :], ALU.mult))
                    s.link(dve.tensor_tensor(score[:, :, :], score[:, :, :], bcast(
                        center[:, :].rearrange("p (o n) -> p o n", o=1), [P, CT, N0]), ALU.subtract))
                    dve.tensor_tensor(z[:, :, :], score[:, :, :], bcast(
                        slope[:, :].rearrange("p (o n) -> p o n", o=1), [P, CT, N0]), ALU.mult).then_inc(z_ready, 1)
                    dve.wait_ge(ez_ready, c + 1)
                    s.link(dve.tensor_scalar(inv[:, :, :], ez[:, :, :], 1.0, None, ALU.add))
                    s.link(dve.reciprocal(gate[:, :, :], inv[:, :, :]))
                    s.link(dve.tensor_reduce(best[:, :], gate[:, :, :], AX.X, ALU.max))
                    best_b = bcast(best[:, :].rearrange("p (c o) -> p c o", o=1), [P, CT, N0])
                    s.link(dve.tensor_tensor(score[:, :, :], gate[:, :, :], best_b, ALU.is_equal))
                    s.link(dve.tensor_tensor(score[:, :, :], score[:, :, :], k.rev[:, :, :], ALU.mult))
                    s.link(dve.tensor_reduce(first[:, :], score[:, :, :], AX.X, ALU.max))
                    s.link(dve.tensor_tensor(score[:, :, :], score[:, :, :], bcast(
                        first[:, :].rearrange("p (c o) -> p c o", o=1), [P, CT, N0]), ALU.is_equal))
                    s.link(dve.scalar_tensor_tensor(out=mod[:, :, 64:R0], in0=score[:, :, :], scalar=0.5,
                                                    in1=best_b, op0=ALU.mult, op1=ALU.mult))
                    s.mark(dve.tensor_scalar(keepc[:, :], best[:, :], -0.5, 0.5, ALU.mult, ALU.add))
                    dve.tensor_tensor(
                        mod[:, :, 0:64].rearrange("p c (n s) -> p c n s", s=S0),
                        yb[:, :, 64:128].rearrange("p c (n s) -> p c n s", s=S0),
                        bcast(mod[:, :, 64:R0].rearrange("p c (n o) -> p c n o", o=1), [P, CT, N0, S0]),
                        ALU.mult).then_inc(mod_ready, 1)
                    s.wait()
                    for j in range(CT):
                        s.mark(dve.scalar_tensor_tensor(
                            out=k.x[:, bass.ds(t0 + j, 1), :], in0=nd.xn[:, b, j:j + 1, :], scalar=keepc[:, j:j + 1],
                            in1=k.x[:, bass.ds(t0 + j, 1), :], op0=ALU.mult, op1=ALU.add))
                    s.wait()
                    dve.wait_ge(out_done, c + 1)
                    s.link(dve.tensor_tensor(k.x[:, bass.ds(t0, CT), :], k.x[:, bass.ds(t0, CT), :], out_ps[:, :, :],
                                             ALU.add))
                    dve.sem_inc(out_used, 1)
                assert s.n == 2 * FFN0_STEPS, s.n

        @block.scalar
        def _(act):
            nd.prime_act(act)
            act.sem_inc(modT_ready, 1)
            with act.Fori(0, CHUNKS // 2) as i:
                for b in range(2):
                    nd.keep(act, i * 2 + b, b)
                for b in range(2):
                    c = i * 2 + b
                    act.wait_ge(z_ready, c + 1)
                    act.activation(ez[:, :, :], z[:, :, :], ACT.Exp, scale=-1.0).then_inc(ez_ready, 1)
                    act.wait_ge(mod_turned, c + 1)
                    act.activation(modT[:, :], mod_ps[0:R0, :], ACT.Copy).then_inc(modT_ready, 1)

        @block.tensor
        def _(pe):
            nd.prime_pe(pe)
            pe.wait_ge(prepared, 1)
            for kt in range(KD):
                ins = pe.matmul(w_ps[:, 0, 0:C0], k.ones[:, :], other[:, kt, :], start=(kt == 0), stop=(kt == KD - 1))
            ins.then_inc(const_ps_ready, 1)
            pe.wait_ge(const_ready, 2)
            with pe.Fori(0, CHUNKS // 2) as i:
                for b in range(2):
                    nd.turn(pe, i * 2 + b, b)
                for b in range(2):
                    c = i * 2 + b
                    nd.wait_xnT(pe, c)
                    pe.wait_ge(y_ready, c + 1)
                    for j in range(CT):
                        for kt in range(KD):
                            ins = pe.matmul(w_ps[:, j, 0:C0], nd.xnT[:, b, kt, j * P:(j + 1) * P], w[:, kt, :],
                                            start=(kt == 0), stop=(kt == KD - 1))
                    ins.then_inc(first_done, 1)
                    pe.wait_ge(mod_ready, c + 1)
                    pe.wait_ge(modT_ready, c + 1)
                    for j in range(CT):
                        ins = pe.transpose(mod_ps[0:R0, j * P:(j + 1) * P], mod[:, j, :], k.ident[:, :])
                    ins.then_inc(mod_turned, 1)
                    pe.wait_ge(modT_ready, 1 + c + 1)
                    pe.wait_ge(out_used, c + 1)
                    for j in range(CT):
                        ins = pe.matmul(out_ps[:, j, :], modT[:, j * P:(j + 1) * P], w2[:, :], start=True, stop=True)
                    ins.then_inc(out_done, 1)
                    pe.wait_ge(out_used, 1 + c + 1)
                    pe.sem_inc(nd.xnT_used, 1)


def qkv0(nc, k, a, v_aug, qs, ks):
    with ExitStack() as stack:
        m = Core(nc, stack, "qkv0_")
        wq = m.sb("wq", [P, KD, H0 * D0])
        wk = m.sb("wk", [P, KD, G0 * D0])
        wv = m.sb("wv", [P, KD, G0 * D0])
        bq = m.sb("bq", [P, 2])
        bk = m.sb("bk", [G0 * D0, 1])
        bv = m.sb("bv", [P, G0 * D0])
        nd = Normed(m, k)
        pieces = m.sb("pieces", [P, 2, 3, 2, CHUNK], F16)
        qk_ps = m.ps("qk_ps", [P, 3, CHUNK])
        v_ps = m.ps("v_ps", [P, CT, G0 * D0])
        loaded = m.sem("loaded")
        product = m.sem("product")
        high = m.sem("high")
        low = m.sem("low")
        v_done = m.sem("v_done")
        v_used = m.sem("v_used")
        padded = m.sem("padded")
        stored = [m.sem("stored0"), m.sem("stored1")]
        in_dram = m.sem("in_dram")
        spread = m.sem("spread")
        block = stack.enter_context(nc.Block())
        rows = [P, P, G0 * D0]

        @block.sync
        def _(sp):
            for b in range(2):
                sp.sem_inc(stored[b], 48)
            sp.dma_start(wq[:, :, :], a["wq0"].rearrange("(k p) c -> p k c", p=P)).then_inc(loaded, 16)
            sp.dma_start(wk[:, :, :], a["wk0"].rearrange("(k p) c -> p k c", p=P)).then_inc(loaded, 16)
            sp.dma_start(wv[:, :, :], a["wv0"].rearrange("(k p) c -> p k c", p=P)).then_inc(loaded, 16)
            sp.dma_start(bq[:, :], a["bq0"]).then_inc(loaded, 16)
            sp.dma_start(bk[:, :], a["bk0"].rearrange("(p o) -> p o", o=1)).then_inc(loaded, 16)
            sp.dma_start(bv[:, :], a["bv0"]).then_inc(loaded, 16)
            with sp.Fori(0, CHUNKS // 2) as i:
                for b in range(2):
                    c = i * 2 + b
                    sp.wait_ge(low, 3 + (c + 1) * 3)
                    for n in range(2):
                        sp.dma_start(a["q0_scr"][n, :, :, bass.ds(c * CHUNK, CHUNK)], pieces[:, b, n, :, :]) \
                          .then_inc(stored[b], 16)
                    sp.dma_start(a["k0_scr"][:, :, bass.ds(c * CHUNK, CHUNK)],
                                 pieces[0:G0 * D0, b, 2, :, :]).then_inc(stored[b], 16)
                    sp.wait_ge(stored[b], 48 * (i + 2))
                    sp.sem_inc(in_dram, 1)
                    tokens = bass.ds(c * CHUNK, CHUNK)
                    for r, (pq, pk) in enumerate(PAIRS0):
                        to = slice(r * D0, (r + 1) * D0)
                        sp.dma_start(qs[to, :, tokens], a["q0_scr"].rearrange("m (h r) e t -> r (m h) e t", r=D0)
                                     [:, :, pq, tokens]).then_inc(spread, 16)
                        sp.dma_start(ks[to, :, tokens], a["k0_scr"].rearrange("(g r) e t -> r g e t", r=D0)
                                     [:, :, pk, tokens]).then_inc(spread, 16)
            sp.wait_ge(spread, 16 * CHUNKS * 2 * len(PAIRS0))

        @block.gpsimd
        def _(pool):
            pool.memset(v_aug[:, :, :, D0:D0 + 1], 1.0).then_inc(padded, 1)
            pool.memset(v_aug[:, :, :, D0 + 1:VW], 0.0).then_inc(padded, 1)
            pool.wait_ge(padded, 2)
            pool.memset(ks[64:P, :, :], 0.0).then_inc(padded, 1)
            pool.wait_ge(padded, 3)
            pool.memset(ks[64:65, :, :], 1.0).then_inc(padded, 1)
            pool.wait_ge(padded, 4)
            pool.memset(qs[64:P, :, :], 0.0).then_inc(padded, 1)
            pool.wait_ge(padded, 5)

        @block.vector
        def _(dve):
            dve.sem_inc(low, 3)
            dve.sem_inc(v_used, 1)
            dve.wait_ge(loaded, 96)
            with dve.Fori(0, CHUNKS // 2) as i:
                for b in range(2):
                    nd.apply(dve, i * 2 + b, b)
                for b in range(2):
                    c = i * 2 + b
                    for n in range(3):
                        r = rows[n]
                        bias = bq[:, n:n + 1] if n < 2 else bk[:, 0:1]
                        dve.wait_ge(high, c * 3 + n + 1)
                        dve.scalar_tensor_tensor(out=pieces[0:r, b, n, 1, :], in0=qk_ps[0:r, n, :], scalar=bias,
                                                 in1=pieces[0:r, b, n, 0, :], op0=ALU.add, op1=ALU.subtract) \
                           .then_inc(low, 1)
                    dve.wait_ge(v_done, c + 1)
                    dve.tensor_tensor(
                        v_aug[:, bass.ds(c * CT, CT), :, 0:D0],
                        v_ps[:, :, :].rearrange("p c (g d) -> p c g d", g=G0),
                        bcast(bv[:, :].rearrange("p (o g d) -> p o g d", o=1, g=G0), [P, CT, G0, D0]),
                        ALU.add).then_inc(v_used, 1)

        @block.scalar
        def _(act):
            nd.prime_act(act)
            act.wait_ge(loaded, 96)
            with act.Fori(0, CHUNKS // 2) as i:
                for b in range(2):
                    nd.keep(act, i * 2 + b, b)
                for b in range(2):
                    c = i * 2 + b
                    act.wait_ge(stored[b], (i + 1) * 48)
                    for n in range(3):
                        r = rows[n]
                        bias = bq[:, n:n + 1] if n < 2 else bk[:, 0:1]
                        act.wait_ge(product, c * 3 + n + 1)
                        act.activation(pieces[0:r, b, n, 0, :], qk_ps[0:r, n, :], ACT.Identity, bias=bias) \
                           .then_inc(high, 1)

        @block.tensor
        def _(pe):
            nd.prime_pe(pe)
            pe.wait_ge(loaded, 96)
            with pe.Fori(0, CHUNKS // 2) as i:
                for b in range(2):
                    nd.turn(pe, i * 2 + b, b)
                for b in range(2):
                    c = i * 2 + b
                    nd.wait_xnT(pe, c)
                    for n in range(3):
                        pe.wait_ge(low, (c + 1) * 3)
                        for kt in range(KD):
                            wn = wq[:, kt, n * P:(n + 1) * P] if n < 2 else wk[:, kt, :]
                            ins = pe.matmul(qk_ps[0:rows[n], n, :], wn, nd.xnT[:, b, kt, :], start=(kt == 0),
                                            stop=(kt == KD - 1))
                        ins.then_inc(product, 1)
                    pe.wait_ge(v_used, c + 1)
                    for j in range(CT):
                        for kt in range(KD):
                            ins = pe.matmul(v_ps[:, j, :], nd.xnT[:, b, kt, j * P:(j + 1) * P], wv[:, kt, :],
                                            start=(kt == 0), stop=(kt == KD - 1))
                    ins.then_inc(v_done, 1)
                    pe.wait_ge(v_done, c + 1)
                    pe.sem_inc(nd.xnT_used, 1)


class Attn0Plan:

    units = [(c, kt) for c in range(CHUNKS) for kt in range(CT * c + CT)]
    maxima = [(qt, kc, h) for qt in range(TILES) for kc in range(qt // CT + 1) for h in range(QUAD)]
    UNITS, MAXIMA = len(units), len(maxima)
    LEAD = 80
    LAG = 2
    RING = 4
    STEPS = UNITS + LAG

    @classmethod
    def maxima_at(cls, u):
        at = [cls.LEAD + v * cls.MAXIMA // cls.STEPS for v in (u, u + 1)]
        return [(n % cls.MAXIMA, n // cls.MAXIMA) for n in range(*at)]

    @classmethod
    def ends_chunk(cls, n):
        c = cls.maxima[n][0] // CT
        last = n + 1 == cls.MAXIMA or cls.maxima[n + 1][0] // CT > c
        return c if last else None


def attn0(nc, k, v_aug, qs, ks, att):
    plan = Attn0Plan
    SCALE = float(D0) ** -0.5
    with ExitStack() as stack:
        m = Core(nc, stack, "attn0_")
        k_now = m.sb("k_now", [P, T], F16)
        v_now = m.sb("v_now", [P, TILES, VW])
        part = m.sb("part", [P, TILES, QUAD, CHUNKS])
        mx = m.sb("mx", [P, P])
        mxT = m.sb("mxT", [QUAD * CT, P], F16)
        prob = m.sb("prob", [P, plan.RING, QUAD, CHUNK])
        oT = m.sb("oT", [P, CHUNK])
        inv = m.sb("inv", [P, CT, QUAD])
        score_ps = m.ps("score_ps", [P, 2, 2, CHUNK])
        max_ps = m.ps("max_ps", [P, 2, CHUNK])
        o_ps = m.ps("o_ps", [P, CHUNK])
        misc_ps = m.ps("misc_ps", [P, CHUNK])
        max_done = m.sem("max_done")
        max_used = m.sem("max_used")
        part_blank = m.sem("part_blank")
        mx_ready = m.sem("mx_ready")
        mx_turned = m.sem("mx_turned")
        mxT_ready = m.sem("mxT_ready")
        row_set = m.sem("row_set")
        now_set = m.sem("now_set")
        scored = m.sem("scored")
        exped = m.sem("exped")
        weighed = m.sem("weighed")
        o_kept = m.sem("o_kept")
        o_turned = m.sem("o_turned")
        o_out = m.sem("o_out")
        inv_ready = m.sem("inv_ready")
        block = stack.enter_context(nc.Block())
        PU, PM = plan.UNITS, plan.MAXIMA

        @block.gpsimd
        def _(pool):
            pool.memset(part[:, :, :, :], NEG).then_inc(part_blank, 1)
            pool.wait_ge(part_blank, 1)
            pool.memset(mx[:, :], 0.0).then_inc(part_blank, 1)
            pool.wait_ge(part_blank, 2)

        @block.sync
        def _(sp):
            sp.sem_inc(row_set, 16 * QUAD)
            def set_row(g, c):
                sp.wait_ge(mxT_ready, g * CHUNKS + c + 1)
                for h in range(QUAD):
                    sp.dma_start(qs[64:65, bass.ds(g * QUAD + h, 1), c * CHUNK:(c + 1) * CHUNK]
                                 .rearrange("o h (t p) -> o (h t) p", p=P), mxT[h * CT:(h + 1) * CT, :]) \
                      .then_inc(row_set, 16)

            with sp.Fori(0, QUADS) as g:
                for c in range(CHUNKS):
                    set_row(g, c)
            sp.wait_ge(row_set, 16 * QUAD * (1 + QUADS * CHUNKS))

        def all_passes(eng, first, one_pass):
            first()
            with eng.Fori(0, QUADS - 1) as g:
                one_pass(g, True)
            one_pass(QUADS - 1, False)

        @block.vector
        def _(dve):
            dve.sem_inc(max_used, 2)
            dve.sem_inc(o_out, 1)
            dve.wait_ge(part_blank, 2)

            def reduce_max(g, n):
                qt, kc, h = plan.maxima[n]
                w = min(CHUNK, (qt + 1) * P - kc * CHUNK)
                tile = g * PM + n
                dve.wait_ge(max_done, tile + 1)
                dve.tensor_reduce(part[:, qt, h, kc:kc + 1], max_ps[:, n % 2, 0:w], AX.X, ALU.max).then_inc(max_used, 1)
                c = plan.ends_chunk(n)
                if c is not None:
                    dve.wait_ge(max_used, 2 + tile + 1)
                    dve.tensor_reduce(mx[:, 0:QUAD * CT].rearrange("p (h t) -> p t h", t=CT),
                                      part[:, CT * c:CT * c + CT, :, :], AX.X, ALU.max, negate=True) \
                       .then_inc(mx_ready, 1)

            def keep_maxima(g, c):
                dve.wait_ge(mx_turned, g * CHUNKS + c + 1)
                dve.wait_ge(row_set, 16 * QUAD * (g * CHUNKS + c + 1))
                dve.tensor_copy(mxT[:, :], misc_ps[0:QUAD * CT, 0:P]).then_inc(mxT_ready, 1)

            def set_now(g):
                dve.tensor_copy(k_now[:, :], ks[:, bass.ds(g // 2, 1), :].rearrange("p o t -> p (o t)")) \
                   .then_inc(now_set, 1)
                dve.tensor_copy(v_now[:, :, :], v_aug[:, :, bass.ds(g // 2, 1), :].rearrange("p t o w -> p t (o w)")) \
                   .then_inc(now_set, 1)

            def put_out(g, c):
                dve.wait_ge(o_turned, g * CHUNKS + c + 1)
                o = misc_ps[:, :].rearrange("p (t h w) -> p t h w", t=CT, h=QUAD)
                dve.reciprocal(inv[:, :, :], o[:, :, :, D0:D0 + 1].rearrange("p t h o -> p t (h o)")).then_inc(inv_ready, 1)
                dve.wait_ge(inv_ready, g * CHUNKS + c + 1)
                dve.tensor_tensor(
                    att[:, CT * c:CT * (c + 1), bass.ds(g * QUAD, QUAD), :], o[:, :, :, 0:D0],
                    bcast(inv[:, :, :].rearrange("p t (h o) -> p t h o", o=1), [P, CT, QUAD, D0]),
                    ALU.mult).then_inc(o_out, 1)

            def first():
                set_now(0)
                for n in range(plan.LEAD):
                    reduce_max(0, n)
                    if plan.ends_chunk(n) is not None:
                        keep_maxima(0, plan.ends_chunk(n))

            def one_pass(g, nxt):
                for u in range(plan.STEPS):
                    c, kt = plan.units[u] if u < PU else (CHUNKS, u - PU)
                    if c > 0 and kt == plan.LAG + 1:
                        put_out(g, c - 1)
                    for n, later in plan.maxima_at(u):
                        if nxt or not later:
                            reduce_max(g + later, n)
                            if plan.ends_chunk(n) is not None:
                                keep_maxima(g + later, plan.ends_chunk(n))
                if nxt:
                    dve.wait_ge(weighed, plan.RING + (g + 1) * PU)
                    set_now(g + 1)
                put_out(g, CHUNKS - 1)

            all_passes(dve, first, one_pass)

        @block.scalar
        def _(act):
            act.sem_inc(exped, 2)
            act.sem_inc(o_kept, 1)

            def keep_o(g, c):
                act.wait_ge(weighed, plan.RING + g * PU + CT * (c + 1) * (c + 2) // 2)
                act.wait_ge(o_out, g * CHUNKS + c + 1)
                act.activation(oT[:, :], o_ps[:, :], ACT.Copy).then_inc(o_kept, 1)

            with act.Fori(0, QUADS) as g:
                for u, (c, kt) in enumerate(plan.units):
                    off = max(0, kt - CT * c) * P
                    if c > 0 and kt == plan.LAG:
                        keep_o(g, c - 1)
                    act.wait_ge(weighed, g * PU + u + 1)
                    for pair in range(2):
                        act.wait_ge(scored, (g * PU + u) * 2 + pair + 1)
                        act.activation(prob[:, u % plan.RING, 2 * pair:2 * pair + 2, off:CHUNK],
                                       score_ps[:, pair, :, off:CHUNK], ACT.Exp, scale=SCALE).then_inc(exped, 1)
                keep_o(g, CHUNKS - 1)

        @block.tensor
        def _(pe):
            pe.sem_inc(weighed, plan.RING)
            pe.wait_ge(part_blank, 2)

            def max_tile(g, n):
                qt, kc, h = plan.maxima[n]
                w = min(CHUNK, (qt + 1) * P - kc * CHUNK)
                diagonal = kc == qt // CT
                pe.wait_ge(max_used, g * PM + n + 1)
                out = max_ps[:, n % 2, :]
                ins = pe.matmul(out[:, 0:w],
                                qs[:, bass.ds(g * QUAD + h, 1), qt * P:(qt + 1) * P].rearrange("p o t -> p (o t)"),
                                ks[:, bass.ds(g // 2, 1), kc * CHUNK:kc * CHUNK + w].rearrange("p o t -> p (o t)"),
                                start=True, stop=not diagonal)
                if diagonal:
                    ins = pe.matmul(out[:, w - P:w], k.identb[:, :], k.mask_qk[:, :], start=False, stop=True)
                ins.then_inc(max_done, 1)

            def turn_maxima(g, c, outputs):
                pe.wait_ge(mx_ready, g * CHUNKS + c + 1)
                pe.wait_ge(o_out, outputs + 1)
                pe.transpose(misc_ps[:, 0:P], mx[:, :], k.ident[:, :]).then_inc(mx_turned, 1)

            def score(g, u, pair):
                c, kt = plan.units[u]
                off = max(0, kt - CT * c) * P
                if pair == 0 and kt == 0:
                    pe.wait_ge(row_set, 16 * QUAD * (1 + g * CHUNKS + c + 1))
                pe.wait_ge(exped, (g * PU + u) * 2 + pair + 1)
                for h in range(2):
                    head = g * QUAD + 2 * pair + h
                    diagonal = kt >= CT * c
                    ins = pe.matmul(score_ps[:, pair, h, off:CHUNK],
                                    k_now[:, kt * P:(kt + 1) * P],
                                    qs[:, bass.ds(head, 1), c * CHUNK + off:(c + 1) * CHUNK]
                                    .rearrange("p o t -> p (o t)"), start=True, stop=not diagonal)
                    if diagonal:
                        ins = pe.matmul(score_ps[:, pair, h, off:off + P], k.identb[:, :], k.mask_kq[:, :],
                                        start=False, stop=True)
                ins.then_inc(scored, 1)

            def weigh(g, u, pair):
                c, kt = plan.units[u]
                off = max(0, kt - CT * c) * P
                pe.wait_ge(exped, 2 + (g * PU + u) * 2 + pair + 1)
                if kt == 0 and pair == 0:
                    pe.wait_ge(o_kept, g * CHUNKS + c + 1)
                for h in range(2 * pair, 2 * pair + 2):
                    ins = pe.matmul(o_ps[32 * h:32 * h + 32, off:CHUNK], v_now[:, kt, :],
                                    prob[:, u % plan.RING, h, off:CHUNK],
                                    start=(kt == 0), stop=(kt == CT * c + CT - 1), skip_group_check=True)
                if pair == 1:
                    ins.then_inc(weighed, 1)

            def turn_o(g, c, maxima):
                pe.wait_ge(o_kept, 1 + g * CHUNKS + c + 1)
                pe.wait_ge(mxT_ready, maxima)
                pe.wait_ge(o_out, g * CHUNKS + c + 1)
                for t in range(CT):
                    ins = pe.transpose(misc_ps[:, t * P:(t + 1) * P], oT[:, t * P:(t + 1) * P], k.ident[:, :])
                ins.then_inc(o_turned, 1)

            def first():
                for n in range(plan.LEAD):
                    max_tile(0, n)
                    if plan.ends_chunk(n) is not None:
                        turn_maxima(0, plan.ends_chunk(n), 0)

            def one_pass(g, nxt):
                pe.wait_ge(now_set, (g + 1) * 2)
                outputs = 0
                maxima = sum(plan.ends_chunk(n) is not None for n in range(plan.LEAD))
                for u in range(plan.STEPS):
                    c, kt = plan.units[u] if u < PU else (CHUNKS, u - PU)
                    tiles = [t for t in plan.maxima_at(u) if nxt or not t[1]]
                    for step in range(4):
                        if step < 2 and u < PU:
                            score(g, u, step)
                        if step >= 2 and u >= plan.LAG:
                            weigh(g, u - plan.LAG, step - 2)
                        for n, later in tiles[step:step + 1]:
                            max_tile(g + later, n)
                            if plan.ends_chunk(n) is not None:
                                turn_maxima(g + later, plan.ends_chunk(n), g * CHUNKS + outputs)
                                maxima += 1
                    if c > 0 and kt == plan.LAG:
                        turn_o(g, c - 1, g * CHUNKS + maxima)
                        outputs += 1
                turn_o(g, CHUNKS - 1, g * CHUNKS + maxima)

            all_passes(pe, first, one_pass)


def wo0(nc, k, a, att):
    with ExitStack() as stack:
        m = Core(nc, stack, "wo0_")
        wo = m.sb("wo", [P, KD, D])
        bo = m.sb("bo", [P, D])
        part = m.sb("part", [P, 2, CT, D])
        partT = m.sb("partT", [P, 2, KD, CHUNK])
        turned_ps = m.ps("turned_ps", [P, KD, CHUNK])
        out_ps = m.ps("out_ps", [P, 2, CT, D])
        loaded = m.sem("loaded")
        copied, turned, kept = m.sem("copied"), m.sem("turned"), m.sem("kept")
        done, used, steps = m.sem("done"), m.sem("used"), m.sem("steps")
        block = stack.enter_context(nc.Block())

        @block.sync
        def _(sp):
            sp.dma_start(wo[:, :, :], a["wo0"].rearrange("(k p) c -> p k c", p=P)).then_inc(loaded, 16)
            sp.dma_start(bo[:, :], a["bo0"]).then_inc(loaded, 16)
            sp.wait_ge(loaded, 32)

        @block.vector
        def _(dve):
            dve.sem_inc(used, 2)
            dve.wait_ge(loaded, 32)
            with dve.Fori(0, CHUNKS // 2) as i:
                s = Steps(dve, steps, i * 2)
                for b in range(2):
                    c = i * 2 + b
                    dve.wait_ge(used, c + 1)
                    dve.tensor_copy(part[:, b, :, :], att[:, bass.ds(c * CT, CT), :, :]
                                    .rearrange("p t h w -> p t (h w)")).then_inc(copied, 1)
                for b in range(2):
                    c = i * 2 + b
                    x = k.x[:, bass.ds(c * CT, CT), :]
                    s.link(dve.tensor_tensor(x, x, bcast(bo[:, :].rearrange("p (o c) -> p o c", o=1), [P, CT, D]),
                                             ALU.add))
                    dve.wait_ge(done, c + 1)
                    dve.tensor_tensor(x, x, out_ps[:, b, :, :], ALU.add).then_inc(used, 1)

        @block.scalar
        def _(act):
            act.sem_inc(kept, 2)
            with act.Fori(0, CHUNKS // 2) as i:
                for b in range(2):
                    c = i * 2 + b
                    act.wait_ge(used, c + 1)
                    for h in range(KD):
                        act.wait_ge(turned, c * KD + h + 1)
                        act.activation(partT[:, b, h, :], turned_ps[:, h, :], ACT.Copy).then_inc(kept, 1)

        @block.tensor
        def _(pe):
            pe.wait_ge(loaded, 32)
            with pe.Fori(0, CHUNKS // 2) as i:
                for b in range(2):
                    c = i * 2 + b
                    pe.wait_ge(copied, c + 1)
                    for h in range(KD):
                        pe.wait_ge(kept, c * KD + h + 1)
                        for j in range(CT):
                            ins = pe.transpose(turned_ps[:, h, j * P:(j + 1) * P], part[:, b, j, h * P:(h + 1) * P],
                                               k.ident[:, :])
                        ins.then_inc(turned, 1)
                    pe.wait_ge(kept, 2 + (c + 1) * KD)
                    pe.wait_ge(used, c + 1)
                    for j in range(CT):
                        for kt in range(KD):
                            ins = pe.matmul(out_ps[:, b, j, :], partT[:, b, kt, j * P:(j + 1) * P], wo[:, kt, :],
                                            start=(kt == 0), stop=(kt == KD - 1))
                    ins.then_inc(done, 1)


FFN1_STEPS = 17


def ffn1(nc, k, a, name, w13_pieces, gw_pieces, prefetch=()):
    with ExitStack() as stack:
        m = Core(nc, stack, name)
        for weights in prefetch:
            weights.open(m)
        w13 = w13_pieces.pieces[:, :, :].rearrange("p e (k x w i) -> p e k x w i", k=KD, x=X1, w=2)
        gw = gw_pieces.pieces[:, :, :].rearrange("p e (k x) -> p e k x", k=KD)
        w2 = m.sb("w2", [P, X1, D])
        gb = m.sb("gb", [P, E1])
        lg = m.sb("lg", [P, CT, E1])
        el = m.sb("el", [P, CT, E1])
        prob = m.sb("prob", [P, CT, E1])
        bias = m.sb("bias", [P, CT, E1])
        pick = m.sb("pick", [P, CT, E1])
        chosen = m.sb("chosen", [P, CT, E1])
        top = m.sb("top", [P, CT])
        dw = m.sb("dw", [P, 2, CT, X1])
        act1 = m.sb("act1", [P, 2, CHUNK])
        hid = m.sb("hid", [P, 2, CHUNK])
        lg_ps = m.ps("lg_ps", [P, CT, E1])
        h_ps = m.ps("h_ps", [P, 2, 2, CHUNK])
        y_ps = m.ps("y_ps", [P, CT, D])
        nd = NormedPieces(m, k, y_ps[:, :, :].rearrange("p (b t) d -> p b (t d)", b=2))
        loaded = m.sem("loaded")
        shared_set = m.sem("shared_set")
        lg_done = m.sem("lg_done")
        lg_ready = m.sem("lg_ready")
        el_ready = m.sem("el_ready")
        dw_ready = m.sem("dw_ready")
        h_done = m.sem("h_done")
        act_ready = m.sem("act_ready")
        hid_ready = m.sem("hid_ready")
        y_done = m.sem("y_done")
        y_used = m.sem("y_used")
        steps = m.sem("steps")
        block = stack.enter_context(nc.Block())

        @block.sync
        def _(sp):
            sp.dma_start(gb[:, :], a["gate1_b"]).then_inc(loaded, 16)
            sp.dma_start(w2[:, :, :], a["w2"].rearrange("x p d -> p x d")).then_inc(loaded, 16)
            for weights in prefetch:
                weights.load(sp)
            sp.wait_ge(loaded, 32)

        @block.gpsimd
        def _(pool):
            for weights in prefetch:
                weights.split(pool)

        @block.vector
        def _(dve):
            dve.sem_inc(hid_ready, 2)
            dve.sem_inc(lg_ready, 1)
            dve.sem_inc(y_used, CT)
            dve.memset(dw[:, :, :, E1:X1], 0.5).then_inc(shared_set, 1)
            dve.wait_ge(shared_set, 1)
            nd.norm(dve)
            dve.wait_ge(loaded, 32)

            def wide(ap):
                return bcast(ap.rearrange("p (c o) -> p c o", o=1), [P, CT, E1])

            def gating(s, c, b):
                dve.wait_ge(lg_done, c + 1)
                s.link(dve.tensor_reduce(top[:, :], lg_ps[:, :, :], AX.X, ALU.max))
                dve.tensor_tensor(lg[:, :, :], lg_ps[:, :, :], wide(top[:, :]), ALU.subtract).then_inc(lg_ready, 1)
                dve.wait_ge(el_ready, c + 1)
                s.link(dve.tensor_reduce(top[:, :], el[:, :, :], AX.X, ALU.add))
                s.link(dve.reciprocal(top[:, :], top[:, :]))
                s.link(dve.tensor_tensor(prob[:, :, :], el[:, :, :], wide(top[:, :]), ALU.mult))
                s.link(dve.tensor_tensor(bias[:, :, :], prob[:, :, :], bcast(
                    gb[:, :].rearrange("p (o e) -> p o e", o=1), [P, CT, E1]), ALU.add))
                for r in range(2):
                    out = (chosen, pick)[r]
                    s.link(dve.tensor_reduce(top[:, :], bias[:, :, :], AX.X, ALU.max))
                    s.link(dve.tensor_tensor(out[:, :, :], bias[:, :, :], wide(top[:, :]), ALU.is_equal))
                    s.link(dve.tensor_tensor(out[:, :, :], out[:, :, :], k.rev[:, :, :], ALU.mult))
                    s.link(dve.tensor_reduce(top[:, :], out[:, :, :], AX.X, ALU.max))
                    s.link(dve.tensor_tensor(out[:, :, :], out[:, :, :], wide(top[:, :]), ALU.is_equal))
                    if r == 0:
                        s.link(dve.scalar_tensor_tensor(out=bias[:, :, :], in0=chosen[:, :, :], scalar=NEG,
                                                        in1=bias[:, :, :], op0=ALU.mult, op1=ALU.add))
                s.link(dve.tensor_tensor(chosen[:, :, :], chosen[:, :, :], pick[:, :, :], ALU.add))
                dve.scalar_tensor_tensor(out=dw[:, b, :, 0:E1], in0=prob[:, :, :], scalar=0.5, in1=chosen[:, :, :],
                                         op0=ALU.mult, op1=ALU.mult).then_inc(dw_ready, 1)
                dve.wait_ge(dw_ready, c + 1)

            def add_y(e, q, c, b):
                dve.wait_ge(y_done, 2 + q + 1)
                for j in range(CT):
                    x = k.x[:, bass.ds(c * CT + j, 1), :]
                    dve.wait_ge(y_used, (q + 1) * CT)
                    dve.scalar_tensor_tensor(out=x, in0=y_ps[:, j:j + 1, :], scalar=dw[:, b, j, e:e + 1],
                                             in1=x, op0=ALU.mult, op1=ALU.add).then_inc(y_used, 1)

            with dve.Fori(0, CHUNKS // 2) as i:
                s = Steps(dve, steps, i * (2 * FFN1_STEPS))
                for b in range(2):
                    c = i * 2 + b
                    gating(s, c, b)
                    for e in range(X1):
                        turn = b * X1 + e
                        q = i * (2 * X1) + turn
                        dve.wait_ge(act_ready, 2 + q + 1)
                        dve.wait_ge(y_done, q + 1)
                        dve.scalar_tensor_tensor(out=hid[:, turn % 2, :], in0=h_ps[:, turn % 2, 1, :],
                                                 scalar=1 / W_SCALE, in1=act1[:, turn % 2, :], op0=ALU.mult,
                                                 op1=ALU.mult).then_inc(hid_ready, 1)
                        if e > 0:
                            add_y(e - 1, q - 1, c, b)
                    add_y(X1 - 1, q, c, b)
                assert s.n == 2 * FFN1_STEPS, s.n

        @block.scalar
        def _(act):
            act.sem_inc(act_ready, 2)
            nd.make_pieces(act)
            with act.Fori(0, CHUNKS // 2) as i:
                for b in range(2):
                    c = i * 2 + b
                    act.wait_ge(lg_ready, 1 + c + 1)
                    act.activation(el[:, :, :], lg[:, :, :], ACT.Exp, scale=1 / W_SCALE).then_inc(el_ready, 1)
                    for e in range(X1):
                        turn = b * X1 + e
                        q = i * (2 * X1) + turn
                        act.wait_ge(h_done, q + 1)
                        act.wait_ge(hid_ready, q + 1)
                        act.activation(act1[:, turn % 2, :], h_ps[:, turn % 2, 0, :], ACT.Silu,
                                       scale=1 / W_SCALE) \
                           .then_inc(act_ready, 1)

        @block.tensor
        def _(pe):
            pe.sem_inc(y_done, 2)
            nd.turn(pe)
            pe.wait_ge(loaded, 32)

            def first(c, b, e, turn, q):
                pe.wait_ge(hid_ready, q + 1)
                for n in range(2):
                    for step, (kt, (pw, px)) in enumerate(product(range(KD), PRODUCT)):
                        ins = pe.matmul(h_ps[:, turn % 2, n, :], w13[:, pw, kt, e, n, :],
                                        nd.xT[:, px, kt, bass.ds(c * CHUNK, CHUNK)], start=(step == 0),
                                        stop=(step == KD * len(PRODUCT) - 1))
                ins.then_inc(h_done, 1)

            def second(e, turn, q):
                pe.wait_ge(hid_ready, 2 + q + 1)
                pe.wait_ge(y_used, (q + 1) * CT)
                for j in range(CT):
                    ins = pe.matmul(y_ps[:, j, :], hid[:, turn % 2, j * P:(j + 1) * P], w2[:, e, :],
                                    start=True, stop=True)
                ins.then_inc(y_done, 1)

            with pe.Fori(0, CHUNKS // 2) as i:
                for b in range(2):
                    c = i * 2 + b
                    pe.wait_ge(lg_ready, c + 1)
                    for j in range(CT):
                        for step, (kt, px, pw) in enumerate(product(range(KD), range(2), range(2))):
                            ins = pe.matmul(lg_ps[:, j, :], nd.xT[:, px, kt, bass.ds((c * CT + j) * P, P)],
                                            gw[:, pw, kt, :], start=(step == 0), stop=(step == KD * 4 - 1))
                    ins.then_inc(lg_done, 1)
                    for e in range(X1):
                        turn = b * X1 + e
                        q = i * (2 * X1) + turn
                        first(c, b, e, turn, q)
                        if e > 0:
                            second(e - 1, turn - 1, q - 1)
                    second(X1 - 1, turn, q)


BANKS1 = QKV1 // CHUNK
ROT = BANKS1 - 1
HPB = CHUNK // D1
PART = CHUNK // 2
PARTS = T // PART


def qkv1(nc, k, a, w_pieces):
    with ExitStack() as stack:
        m = Core(nc, stack, "qkv1_")
        w = w_pieces.pieces[:, :, :].rearrange("p e (k c) -> p e k c", k=KD)
        cos = m.sb("cos", [P, TILES, D1 // 2])
        sin = m.sb("sin", [P, TILES, D1 // 2])
        xc = m.sb("xc", [P, 2, HPB, 2, D1 // 2])
        xs = m.sb("xs", [P, 2, HPB, 2, D1 // 2])
        rot = m.sb("rot", [P, 2, HPB, D1])
        qk = m.sb("qk", [P, 2, ROT * HPB, 2, PART], F16)
        v = m.sb("v", [P, 2, 2, G1 * D1], F16)
        qkv_ps = m.ps("qkv_ps", [P, 3, CHUNK])
        turned_ps = m.ps("rot_ps", [P, 2, CHUNK])
        nd = NormedPieces(m, k, turned_ps)
        loaded = m.sem("loaded")
        done = m.sem("done")
        freed = m.sem("freed")
        scaled = m.sem("scaled")
        rot_ready = m.sem("rot_ready")
        rot_turned = m.sem("rot_turned")
        qk_high = m.sem("qk_high")
        qk_low = m.sem("qk_low")
        v_high = m.sem("v_high")
        v_low = m.sem("v_low")
        stored = [m.sem("stored0"), m.sem("stored1")]
        v_stored = [m.sem("v_stored0"), m.sem("v_stored1")]
        block = stack.enter_context(nc.Block())
        PT = PART // P
        NR = PT * ROT

        @block.sync
        def _(sp):
            for b in range(2):
                sp.sem_inc(stored[b], 32)
                sp.sem_inc(v_stored[b], 16)
            sp.dma_start(cos[:, :, :], a["cos"].rearrange("(t p) c -> p t c", p=P)).then_inc(loaded, 16)
            sp.dma_start(sin[:, :, :], a["sin"].rearrange("(t p) c -> p t c", p=P)).then_inc(loaded, 16)
            with sp.Fori(0, PARTS // 2) as i:
                for b in range(2):
                    c = i * 2 + b
                    for j in range(PT):
                        t = c * PT + j
                        sp.wait_ge(v_low, t + 1)
                        sp.dma_start(a["v1_scr"][bass.ds(t, 1), :, :, :].rearrange("o p e g -> p (o e) g"),
                                     v[:, j % 2, :, :]).then_inc(v_stored[j % 2], 16)
                    sp.wait_ge(qk_low, 2 + (c + 1) * NR)
                    for e in range(2):
                        sp.dma_start(a["qk1_scr"][:, :, e, bass.ds(c * PART, PART)].rearrange("h p t -> p h t"),
                                     qk[:, b, :, e, :]).then_inc(stored[b], 16)
            for b in range(2):
                sp.wait_ge(stored[b], 32 * (1 + PARTS // 2))
                sp.wait_ge(v_stored[b], 16 * (1 + TILES // 2))

        def turn_order():
            return [(n, n - 2) for n in range(BANKS1)] + [(None, BANKS1 - 2)]

        @block.vector
        def _(dve):
            dve.sem_inc(freed, 3)
            dve.sem_inc(qk_low, 2)
            nd.norm(dve)
            dve.wait_ge(loaded, 32)
            with dve.Fori(0, PARTS // 2) as i:
                for b in range(2):
                    c = i * 2 + b
                    for j in range(PT):
                        t = c * PT + j
                        for n, r in turn_order():
                            if n is not None and n < ROT:
                                dve.wait_ge(done, t * BANKS1 + n + 1)
                                g = j * ROT + n
                                dve.wait_ge(rot_ready, t * ROT + n + 1)
                                ps = qkv_ps[:, n % 3, :].rearrange("p (h a w) -> p (h a) w", h=HPB, a=2)
                                for tab, out in ((cos, xc), (sin, xs)):
                                    ins = dve.scalar_tensor_tensor(
                                        out=out[:, g % 2, :, :, :].rearrange("p h a w -> p (h a) w"), in0=ps,
                                        scalar=1 / W_SCALE, in1=bcast(tab[:, bass.ds(t, 1), :],
                                                                      [P, 2 * HPB, D1 // 2]),
                                        op0=ALU.mult, op1=ALU.mult)
                                    ins.then_inc(scaled, 1)
                                dve.wait_ge(scaled, (t * ROT + n + 1) * 2)
                                dve.sem_inc(freed, 1)
                            elif n == ROT:
                                dve.wait_ge(v_high, t + 1)
                                dve.scalar_tensor_tensor(out=v[:, j % 2, 1, :], in0=qkv_ps[:, n % 3, :],
                                                         scalar=1 / W_SCALE, in1=v[:, j % 2, 0, :], op0=ALU.mult,
                                                         op1=ALU.subtract).then_inc(v_low, 1)
                                dve.wait_ge(v_low, t + 1)
                                dve.sem_inc(freed, 1)
                            if r is not None and 0 <= r < ROT:
                                dve.wait_ge(qk_high, t * ROT + r + 1)
                                g = j * ROT + r
                                dve.tensor_tensor(
                                    qk[:, b, r * HPB:(r + 1) * HPB, 1, j * P:(j + 1) * P],
                                    turned_ps[:, g % 2, :].rearrange("p (h t) -> p h t", h=HPB),
                                    qk[:, b, r * HPB:(r + 1) * HPB, 0, j * P:(j + 1) * P], ALU.subtract) \
                                   .then_inc(qk_low, 1)

        @block.gpsimd
        def _(pool):
            pool.sem_inc(rot_ready, 2)
            with pool.Fori(0, PARTS // 2) as i:
                for b in range(2):
                    for j in range(PT):
                        t = (i * 2 + b) * PT + j
                        for n in range(ROT):
                            g = j * ROT + n
                            pool.wait_ge(scaled, (t * ROT + n + 1) * 2)
                            pool.wait_ge(rot_turned, t * ROT + n + 1)
                            out = rot[:, g % 2, :, :].rearrange("p h (a w) -> p h a w", a=2)
                            pool.tensor_tensor(out[:, :, 0, :], xc[:, g % 2, :, 0, :], xs[:, g % 2, :, 1, :],
                                               ALU.subtract)
                            pool.tensor_tensor(out[:, :, 1, :], xc[:, g % 2, :, 1, :], xs[:, g % 2, :, 0, :],
                                               ALU.add).then_inc(rot_ready, 1)

        @block.scalar
        def _(act):
            nd.make_pieces(act)
            with act.Fori(0, PARTS // 2) as i:
                for b in range(2):
                    c = i * 2 + b
                    act.wait_ge(stored[b], (i + 1) * 32)
                    for j in range(PT):
                        t = c * PT + j
                        for n, r in turn_order():
                            if n == ROT:
                                act.wait_ge(done, t * BANKS1 + n + 1)
                                act.wait_ge(v_stored[j % 2], c * 16 + 16)
                                act.activation(v[:, j % 2, 0, :], qkv_ps[:, n % 3, :], ACT.Copy, scale=1 / W_SCALE) \
                                   .then_inc(v_high, 1)
                            if r is not None and 0 <= r < ROT:
                                g = j * ROT + r
                                act.wait_ge(rot_turned, 2 + t * ROT + r + 1)
                                act.activation(qk[:, b, r * HPB:(r + 1) * HPB, 0, j * P:(j + 1) * P],
                                               turned_ps[:, g % 2, :].rearrange("p (h t) -> p h t", h=HPB),
                                               ACT.Copy).then_inc(qk_high, 1)

        @block.tensor
        def _(pe):
            pe.sem_inc(rot_turned, 2)
            nd.turn(pe)
            with pe.Fori(0, PARTS // 2) as i:
                for b in range(2):
                    for j in range(PT):
                        t = (i * 2 + b) * PT + j
                        for n, r in turn_order():
                            if n is not None:
                                pe.wait_ge(freed, t * BANKS1 + n + 1)
                                for step, (kt, (px, pw)) in enumerate(product(range(KD), PRODUCT)):
                                    ins = pe.matmul(qkv_ps[:, n % 3, :], nd.xT[:, px, kt, bass.ds(t * P, P)],
                                                    w[:, pw, kt, n * CHUNK:(n + 1) * CHUNK], start=(step == 0),
                                                    stop=(step == KD * len(PRODUCT) - 1))
                                ins.then_inc(done, 1)
                            if r is not None and 0 <= r < ROT:
                                g = j * ROT + r
                                pe.wait_ge(rot_ready, 2 + t * ROT + r + 1)
                                pe.wait_ge(qk_low, t * ROT + r + 1)
                                for h in range(HPB):
                                    ins = pe.transpose(turned_ps[:, g % 2, h * P:(h + 1) * P], rot[:, g % 2, h, :],
                                                       k.ident[:, :])
                                ins.then_inc(rot_turned, 1)


class Attn1Plan:

    units = [(c, kp) for c in range(CHUNKS) for kp in range(2 * c + 2)]
    maxima = [(qt, kc) for qt in range(TILES) for kc in range(qt // CT + 1)]
    UNITS, MAXIMA, LEAD = len(units), len(maxima), 6
    LAG = 2
    RING = 4

    @classmethod
    def maxima_at(cls, u):
        n, left = u - cls.LEAD, cls.UNITS - cls.LEAD
        return range(n * cls.MAXIMA // left, (n + 1) * cls.MAXIMA // left) if n >= 0 else range(0)

    @staticmethod
    def offset(c, kt):
        return max(0, kt - CT * c) * P


def attn1(nc, k, a, prefetch=()):
    plan = Attn1Plan
    SCALE = float(D1) ** -0.5
    PU, PM = plan.UNITS, plan.MAXIMA
    with ExitStack() as stack:
        m = Core(nc, stack, "attn1_")
        for weights in prefetch:
            weights.open(m)
        q = m.sb("q", [P, 2, 2, T], F16)
        kk = m.sb("kk", [P, 2, 2, T], F16)
        v = m.sb("v", [P, 2, TILES, VL + D1], F16)
        part = m.sb("part", [P, TILES, CHUNKS])
        mx = m.sb("mx", [P, 2, TILES])
        diag = m.sb("diag", [P, 2, T], BF16)
        prob = m.sb("prob", [P, 2, 2, CHUNK])
        high = m.sb("high", [P, plan.RING, 2, CHUNK], F16)
        low = m.sb("low", [P, plan.RING, 2, CHUNK], F16)
        inv = m.sb("inv", [P, CT])
        att = m.sb("att", [P, 2, CT, D1])
        score_ps = m.ps("score_ps", [P, 2, 2, CHUNK])
        max_ps = m.ps("max_ps", [P, 2, CHUNK])
        o_ps = m.ps("o_ps", [P, CT, 256])
        loaded = [m.sem("loaded0"), m.sem("loaded1")]
        blank = m.sem("blank")
        max_done = m.sem("max_done")
        max_used = m.sem("max_used")
        mx_ready = m.sem("mx_ready")
        diag_ready = m.sem("diag_ready")
        scored = m.sem("scored")
        exped = m.sem("exped")
        low_ready = m.sem("low_ready")
        weighed = m.sem("weighed")
        inv_ready = m.sem("inv_ready")
        o_used = m.sem("o_used")
        stored = [m.sem("stored0"), m.sem("stored1")]
        block = stack.enter_context(nc.Block())

        def all_passes(eng, one_pass, first=None):
            if first:
                first()
            with eng.Fori(0, H1 // 2 - 1) as i:
                for b in range(2):
                    one_pass(i * 2 + b, b, True)
            one_pass(H1 - 2, 0, True)
            one_pass(H1 - 1, 1, False)

        @block.sync
        def _(sp):
            def load(h, b):
                g = h // (H1 // G1)
                sp.dma_start(q[:, b, :, :], a["qk1_scr"][bass.ds(h, 1), :, :, :].rearrange("o p e t -> p (o e) t")) \
                  .then_inc(loaded[b], 16)
                sp.dma_start(kk[:, b, :, :], a["qk1_scr"][bass.ds(g + H1, 1), :, :, :]
                             .rearrange("o p e t -> p (o e) t")).then_inc(loaded[b], 16)
                for e, at in ((0, 0), (1, VL)):
                    sp.dma_start(v[:, b, :, at:at + D1],
                                 a["v1_scr"][:, :, e, bass.ds(g * D1, D1)].rearrange("t p d -> p t d")) \
                      .then_inc(loaded[b], 16)

            def one_pass(h, b, nxt):
                if nxt:
                    sp.wait_ge(weighed, plan.RING + h * PU)
                    load(h + 1, 1 - b)
                for c in range(CHUNKS):
                    sp.wait_ge(o_used, 1 + h * CHUNKS + c + 1)
                    sp.dma_start(a["att_scr"][bass.ds(c * CT, CT), :, bass.ds(h * D1, D1)].rearrange("t p d -> p t d"),
                                 att[:, c % 2, :, :]).then_inc(stored[c % 2], 16)

            for b in range(2):
                sp.sem_inc(stored[b], 16)
            load(0, 0)
            for weights in prefetch:
                weights.load(sp)
            all_passes(sp, one_pass)
            for b in range(2):
                sp.wait_ge(stored[b], 16 * (1 + H1 * CHUNKS // 2))

        @block.gpsimd
        def _(pool):
            pool.memset(part[:, :, :], NEG).then_inc(blank, 1)
            pool.wait_ge(blank, 1)
            pool.memset(v[:, :, :, D1:VL], 1.0).then_inc(blank, 1)
            pool.wait_ge(blank, 2)

            def make_diag(h, b):
                if not isinstance(h, int) or h > 0:
                    pool.wait_ge(weighed, plan.RING + (h - 1) * PU)
                for c in range(CHUNKS):
                    pool.wait_ge(mx_ready, h * CHUNKS + c + 1)
                    pool.tensor_tensor(
                        diag[:, b, c * CHUNK:(c + 1) * CHUNK].rearrange("p (t j) -> p t j", t=CT),
                        bcast(k.minusb[:, :].rearrange("p (o j) -> p o j", o=1), [P, CT, P]),
                        bcast(mx[:, b, CT * c:CT * c + CT].rearrange("p (t o) -> p t o", o=1), [P, CT, P]),
                        ALU.mult).then_inc(diag_ready, 1)

            def one_pass(h, b, nxt):
                if nxt:
                    make_diag(h + 1, 1 - b)

            all_passes(pool, one_pass, lambda: make_diag(0, 0))
            for weights in prefetch:
                weights.split(pool)

        @block.vector
        def _(dve):
            dve.sem_inc(max_used, 2)
            dve.sem_inc(low_ready, 2)
            dve.sem_inc(o_used, 1)
            dve.wait_ge(blank, 2)

            def reduce_max(h, b, n):
                qt, kc = plan.maxima[n]
                w = min(CHUNK, (qt + 1) * P - kc * CHUNK)
                tile = h * PM + n
                dve.wait_ge(max_done, tile + 1)
                dve.tensor_reduce(part[:, qt, kc:kc + 1], max_ps[:, n % 2, 0:w], AX.X, ALU.max).then_inc(max_used, 1)
                if kc == qt // CT and qt % CT == CT - 1:
                    c = qt // CT
                    dve.wait_ge(max_used, 2 + tile + 1)
                    dve.tensor_reduce(mx[:, b, CT * c:CT * c + CT], part[:, CT * c:CT * c + CT, :], AX.X, ALU.max) \
                       .then_inc(mx_ready, 1)
                    dve.wait_ge(mx_ready, h * CHUNKS + c + 1)

            def put_out(h, c):
                dve.wait_ge(weighed, plan.RING + h * PU + (c + 1) * (c + 2))
                dve.reciprocal(inv[:, :], o_ps[:, :, D1:VO].rearrange("p t o -> p (t o)")).then_inc(inv_ready, 1)
                dve.wait_ge(inv_ready, h * CHUNKS + c + 1)
                dve.wait_ge(stored[c % 2], (h * 2 + c // 2 + 1) * 16)
                dve.tensor_tensor(att[:, c % 2, :, :], o_ps[:, :, 0:D1],
                                  bcast(inv[:, :].rearrange("p (t o) -> p t o", o=1), [P, CT, D1]), ALU.mult) \
                   .then_inc(o_used, 1)

            def one_pass(h, b, nxt):
                for u, (c, kp) in enumerate(plan.units):
                    if nxt:
                        for n in plan.maxima_at(u):
                            reduce_max(h + 1, 1 - b, n)
                    unit = h * PU + u
                    off = plan.offset(c, 2 * kp)
                    dve.wait_ge(exped, 2 + unit + 1)
                    dve.wait_ge(weighed, unit + 1)
                    dve.tensor_tensor(low[:, u % plan.RING, :, off:CHUNK], prob[:, u % 2, :, off:CHUNK],
                                      high[:, u % plan.RING, :, off:CHUNK], ALU.subtract).then_inc(low_ready, 1)
                    if c > 0 and kp == plan.LAG - 1:
                        put_out(h, c - 1)
                put_out(h, CHUNKS - 1)

            def first():
                for n in range(PM):
                    reduce_max(0, 0, n)

            all_passes(dve, one_pass, first)

        @block.scalar
        def _(act):
            act.sem_inc(exped, 2)

            def one_pass(h, b, nxt):
                for u, (c, kp) in enumerate(plan.units):
                    unit = h * PU + u
                    off = plan.offset(c, 2 * kp)
                    act.wait_ge(scored, unit + 1)
                    act.wait_ge(weighed, unit + 1)
                    act.wait_ge(low_ready, unit + 1)
                    act.activation(high[:, u % plan.RING, :, off:CHUNK], score_ps[:, u % 2, :, off:CHUNK], ACT.Exp,
                                   scale=SCALE)
                    act.activation(prob[:, u % 2, :, off:CHUNK], score_ps[:, u % 2, :, off:CHUNK], ACT.Exp,
                                   scale=SCALE).then_inc(exped, 1)

            all_passes(act, one_pass)

        @block.tensor
        def _(pe):
            pe.sem_inc(weighed, plan.RING)
            pe.wait_ge(blank, 2)

            def max_tile(h, b, n):
                qt, kc = plan.maxima[n]
                w = min(CHUNK, (qt + 1) * P - kc * CHUNK)
                diagonal = kc == qt // CT
                pe.wait_ge(max_used, h * PM + n + 1)
                ins = pe.matmul(max_ps[:, n % 2, 0:w], q[:, b, 0, qt * P:(qt + 1) * P],
                                kk[:, b, 0, kc * CHUNK:kc * CHUNK + w], start=True, stop=not diagonal)
                if diagonal:
                    ins = pe.matmul(max_ps[:, n % 2, w - P:w], k.identb[:, :], k.mask_qk[:, :], start=False, stop=True)
                ins.then_inc(max_done, 1)

            def score(h, b, u, s):
                c, kp = plan.units[u]
                unit = h * PU + u
                if s == 0:
                    pe.wait_ge(exped, unit + 1)
                    if kp == 0:
                        pe.wait_ge(diag_ready, h * CHUNKS + c + 1)
                kt = 2 * kp + s
                off = plan.offset(c, 2 * kp)
                out = score_ps[:, u % 2, s, off:CHUNK]
                queries = slice(c * CHUNK + off, (c + 1) * CHUNK)
                keys = slice(kt * P, (kt + 1) * P)
                diagonal = kt >= CT * c
                pe.matmul(out, kk[:, b, 0, keys], q[:, b, 0, queries], start=True, stop=False)
                pe.matmul(out, kk[:, b, 0, keys], q[:, b, 1, queries], start=False, stop=False)
                pe.matmul(out, kk[:, b, 1, keys], q[:, b, 0, queries], start=False, stop=False)
                ins = pe.matmul(out, k.onesb[:, :], diag[:, b, queries], start=False, stop=not diagonal)
                if diagonal:
                    at = plan.offset(c, kt)
                    ins = pe.matmul(score_ps[:, u % 2, s, at:at + P], k.identb[:, :], k.mask_kq[:, :],
                                    start=False, stop=True)
                if s == 1:
                    ins.then_inc(scored, 1)

            def weigh(h, b, u, s):
                c, kp = plan.units[u]
                if s == 0:
                    pe.wait_ge(low_ready, 2 + h * PU + u + 1)
                    if kp == 0:
                        pe.wait_ge(o_used, h * CHUNKS + c + 1)
                kt = 2 * kp + s
                vh, vl = v[:, b, kt, 0:VO], v[:, b, kt, VL:VL + D1]
                for t in range(plan.offset(c, kt) // P, CT):
                    ph, pl = (p[:, u % plan.RING, s, t * P:(t + 1) * P] for p in (high, low))
                    start = kt == 0 and t % 2 == 0
                    pe.matmul(o_ps[:, t, 0:VO], ph, vh, start=start, stop=False, skip_group_check=True)
                    pe.matmul(o_ps[:, t, 0:D1], ph, vl, start=False, stop=False, skip_group_check=True)
                    ins = pe.matmul(o_ps[:, t, 0:VO], pl, vh, start=False, stop=(kp == 2 * c + 1 and s == 1),
                                    skip_group_check=True)
                if s == 1:
                    ins.then_inc(weighed, 1)

            def one_pass(h, b, nxt):
                for u in range(PU + plan.LAG):
                    if nxt and u == plan.LEAD:
                        pe.wait_ge(loaded[1 - b], 64 * ((h + 1) // 2 + 1))
                    tiles = list(plan.maxima_at(u)) if nxt and u < PU else []
                    parts = [(score, u, s) for s in range(2) if u < PU]
                    parts += [(weigh, u - plan.LAG, s) for s in range(2) if u >= plan.LAG]
                    for part, unit, s in parts:
                        part(h, b, unit, s)
                        if tiles:
                            max_tile(h + 1, 1 - b, tiles.pop(0))
                    for n in tiles:
                        max_tile(h + 1, 1 - b, n)

            def first():
                pe.wait_ge(loaded[0], 64)
                for n in range(PM):
                    max_tile(0, 0, n)

            all_passes(pe, one_pass, first)


def wo1(nc, k, a, wo_pieces):
    HB = H1 // 4
    with ExitStack() as stack:
        m = Core(nc, stack, "wo1_")
        wo = wo_pieces.pieces[:, :, :].rearrange("p e (h c) -> p e h c", h=H1)
        att = m.sb("att", [P, 2, H1, D1])
        attT = m.sb("attT", [P, 2, 2, H1, P], F16)
        turned_ps = m.ps("turned_ps", [P, 4, CHUNK])
        out_ps = m.ps("out_ps", [P, 2, CHUNK])
        att_in = [m.sem("att_in0"), m.sem("att_in1")]
        turned = m.sem("turned")
        high = m.sem("high")
        low = m.sem("low")
        done = m.sem("done")
        used = m.sem("used")
        block = stack.enter_context(nc.Block())

        @block.sync
        def _(sp):
            with sp.Fori(0, TILES // 2) as i:
                for b in range(2):
                    t = i * 2 + b
                    sp.wait_ge(turned, (i + 1) * 8)
                    sp.dma_start(att[:, b, :, :].rearrange("p h d -> p (h d)"),
                                 a["att_scr"][bass.ds(t, 1), :, :].rearrange("o p c -> (o p) c")) \
                      .then_inc(att_in[b], 16)

        @block.scalar
        def _(act):
            with act.Fori(0, TILES // 2) as i:
                for b in range(2):
                    t = i * 2 + b
                    act.wait_ge(used, t + 1)
                    for n in range(4):
                        act.wait_ge(turned, 8 + t * 4 + n + 1)
                        act.activation(attT[:, b, 0, n * HB:(n + 1) * HB, :].rearrange("p h t -> p (h t)"),
                                       turned_ps[:, n, :], ACT.Copy).then_inc(high, 1)

        @block.vector
        def _(dve):
            dve.sem_inc(used, 2)
            dve.sem_inc(low, 4)
            with dve.Fori(0, TILES // 2) as i:
                for b in range(2):
                    t = i * 2 + b
                    for n in range(4):
                        dve.wait_ge(high, t * 4 + n + 1)
                        dve.tensor_tensor(attT[:, b, 1, n * HB:(n + 1) * HB, :].rearrange("p h t -> p (h t)"),
                                          turned_ps[:, n, :],
                                          attT[:, b, 0, n * HB:(n + 1) * HB, :].rearrange("p h t -> p (h t)"),
                                          ALU.subtract).then_inc(low, 1)
                for b in range(2):
                    t = i * 2 + b
                    x = k.x[:, bass.ds(t, 1), :]
                    dve.wait_ge(done, t + 1)
                    dve.scalar_tensor_tensor(out=x, in0=out_ps[:, b:b + 1, 0:D], scalar=1 / W_SCALE, in1=x,
                                             op0=ALU.mult, op1=ALU.add).then_inc(used, 1)

        @block.tensor
        def _(pe):
            pe.sem_inc(turned, 8)

            def turn(i, b):
                t = i * 2 + b
                pe.wait_ge(att_in[b], i * 16 + 16)
                for n in range(4):
                    pe.wait_ge(low, t * 4 + n + 1)
                    for h in range(HB):
                        ins = pe.transpose(turned_ps[:, n, h * P:(h + 1) * P], att[:, b, n * HB + h, :],
                                           k.ident[:, :])
                    ins.then_inc(turned, 1)

            def multiply(i, b):
                t = i * 2 + b
                pe.wait_ge(low, 4 + (t + 1) * 4)
                pe.wait_ge(used, t + 1)
                for step, (h, (px, pw)) in enumerate(product(range(H1), PRODUCT)):
                    ins = pe.matmul(out_ps[:, b, 0:D], attT[:, b, px, h, :], wo[:, pw, h, :], start=(step == 0),
                                    stop=(step == H1 * len(PRODUCT) - 1))
                ins.then_inc(done, 1)

            with pe.Fori(0, TILES // 2) as i:
                for b in range(2):
                    turn(i, b)
                for b in range(2):
                    multiply(i, b)


def store(nc, k, a):
    with ExitStack() as stack:
        stored = Core(nc, stack, "st_").sem("stored")
        with nc.Block() as block:

            @block.sync
            def _(sp):
                sp.dma_start(a["out"].rearrange("o (t p) d -> p (o t) d", p=P), k.x[:, :, :]).then_inc(stored, 16)
                sp.wait_ge(stored, 16)


def fetch(nc, prefetch):
    with ExitStack() as stack:
        m = Core(nc, stack, "fetch_")
        for weights in prefetch:
            weights.open(m)
        with nc.Block() as block:

            @block.sync
            def _(sp):
                for weights in prefetch:
                    weights.load(sp)

            @block.gpsimd
            def _(pool):
                for weights in prefetch:
                    weights.split(pool)


def program(nc, a, stages=9, start=0):
    a["q0_scr"] = nc.dram_tensor("q0_scr", (2, P, 2, T), F16, kind="Internal").ap()
    a["k0_scr"] = nc.dram_tensor("k0_scr", (G0 * D0, 2, T), F16, kind="Internal").ap()
    a["qk1_scr"] = nc.dram_tensor("qk1_scr", (H1 + G1, D1, 2, T), F16, kind="Internal").ap()
    a["v1_scr"] = nc.dram_tensor("v1_scr", (TILES, P, 2, G1 * D1), F16, kind="Internal").ap()
    a["att_scr"] = nc.dram_tensor("att_scr", (TILES, P, H1 * D1), F32, kind="Internal").ap()
    with ExitStack() as stack:
        k = Core(nc, stack)
        k.x = k.sb("x", [P, TILES, D])
        k.rstd = k.sb("rstd", [P, TILES])
        k.shift = k.sb("shift", [P, TILES])
        k.length2 = k.sb("length2", [P, TILES])
        k.ident = k.sb("ident", [P, P])
        k.identb = k.sb("identb", [P, P], BF16)
        k.minusb = k.sb("minusb", [P, P], BF16)
        k.mask_qk = k.sb("mask_qk", [P, P], BF16)
        k.mask_kq = k.sb("mask_kq", [P, P], BF16)
        k.ones = k.sb("ones", [P, P])
        k.onesb = k.sb("onesb", [P, P], BF16)
        k.eps = k.sb("eps", [P, 1])
        k.rev = k.sb("rev", [P, CT, N0])
        setup(nc, k, a)
        if start < 1 <= stages:
            norm_stats(nc, k, "n1_")
            ffn0(nc, k, a, "f1_")
        if start < 2 <= stages:
            with ExitStack() as inner:
                m = Core(nc, inner, "a0_")
                v_aug = m.sb("v_aug", [P, TILES, G0, VW])
                att = m.sb("att", [P, TILES, H0, D0])
                norm_stats(nc, k, "n2_")
                qs = m.sb("qs", [P, H0, T], F16)
                ks = m.sb("ks", [P, G0, T], F16)
                qkv0(nc, k, a, v_aug, qs, ks)
                attn0(nc, k, v_aug, qs, ks, att)
                wo0(nc, k, a, att)
        w13 = Weights(k, "w13", a["w13"].rearrange("(k p) c -> p k c", p=P), KD * X1 * 2 * I1)
        wqkv = Weights(k, "wqkv", a["wqkv1"].rearrange("(k p) c -> p k c", p=P), KD * QKV1)
        wo = Weights(k, "wo", a["wo1"].rearrange("(h p) c -> p h c", p=P), H1 * D)
        gw = Weights(k, "gw", a["gate1_w"].rearrange("(k p) c -> p k c", p=P), KD * E1)
        if start < 3 <= stages:
            norm_stats(nc, k, "n3_")
            ffn0(nc, k, a, "f3_", (gw, w13))
        elif stages > 3:
            fetch(nc, (gw, w13))
        if start < 4 <= stages:
            norm_stats(nc, k, "n4_")
            ffn1(nc, k, a, "f4_", w13, gw, (wqkv,))
        elif stages > 4:
            fetch(nc, (wqkv,))
        if start < 5 <= stages:
            norm_stats(nc, k, "n5_")
            qkv1(nc, k, a, wqkv)
            attn1(nc, k, a, (wo,))
            wo1(nc, k, a, wo)
        if start < 6 <= stages:
            norm_stats(nc, k, "n6_")
            ffn1(nc, k, a, "f6_", w13, gw)
        store(nc, k, a)


def laid_out(inputs):
    import numpy as np

    i = {n: np.asarray(v) for n, v in inputs.items()}
    c = np.ascontiguousarray

    def on_all(row):
        return c(np.broadcast_to(row[None, :], (P, row.shape[0])))

    def columns(w):
        return np.transpose(w, (1, 0, 2)).reshape(D, -1)

    smd = i["L0_ffn_select_mean_diff"].T
    w1, w2, w3 = (np.concatenate([i[f"L1_ffn_W{n}"], i[f"L1_ffn_Ws{n}"][None]], 0) for n in (1, 2, 3))
    freqs = np.float32(1.0) / np.power(np.float32(10000.0), np.arange(0, D1, 2, dtype=np.float32) / np.float32(D1))
    angle = np.arange(T, dtype=np.float32)[:, None] * freqs[None, :]
    cos, sin = np.cos(angle), np.sin(angle)
    return {
        "x": i["L0_attn_x"],
        "ffn0_w": c(np.concatenate([columns(i["L0_ffn_select_weight"]), columns(i["L0_ffn_lora_update"]), smd], 1)),
        "ffn0_other": c(np.concatenate([np.repeat(smd, S0, 1), np.repeat(i["L0_ffn_debias_w"].T, S0, 1), smd], 1)),
        "ffn0_w2": c(np.concatenate([np.transpose(i["L0_ffn_lora_degen"], (0, 2, 1)).reshape(-1, D),
                                     i["L0_ffn_bias_w"]], 0)),
        "ffn0_center": on_all(i["L0_ffn_imp_center"]),
        "ffn0_slope": on_all(i["L0_ffn_imp_slope"]),
        "wq0": i["L0_attn_Wq"], "wk0": i["L0_attn_Wk"], "wv0": i["L0_attn_Wv"], "wo0": i["L0_attn_Wo"],
        "bq0": c(i["L0_attn_bq"].reshape(2, P).T), "bk0": i["L0_attn_bk"], "bv0": on_all(i["L0_attn_bv"]),
        "bo0": on_all(i["L0_attn_bo"]),
        "gate1_w": c(i["L1_ffn_gate_w"].T), "gate1_b": on_all(i["L1_ffn_gate_b"]),
        "w13": c(np.stack([w1, w3], 1).reshape(X1 * 2 * I1, D).T), "w2": c(np.transpose(w2, (0, 2, 1))),
        "wqkv1": i["L1_attn_Wqkv"], "wo1": i["L1_attn_Wo"], "cos": cos, "sin": sin,
    }


def kernel(**inputs):
    import concourse.bacc as bacc
    from concourse.bass_utils import run_bass_kernel_spmd

    nc = bacc.Bacc("TRN2", target_bir_lowering=False, num_devices=1)
    arrays, a = {}, {}
    for name, value in laid_out(inputs).items():
        arrays["in_" + name] = value
        a[name] = nc.dram_tensor("in_" + name, value.shape, mybir.dt.from_np(value.dtype), kind="ExternalInput").ap()
    a["out"] = nc.dram_tensor("out", (1, T, D), F32, kind="ExternalOutput").ap()
    program(nc, a)
    return run_bass_kernel_spmd(nc, [arrays], core_ids=[0]).results[0]["out"]
```

```python
from contextlib import ExitStack
from itertools import product

import concourse.bass as bass
from concourse import mybir

F32 = mybir.dt.float32
F16 = mybir.dt.float16
BF16 = mybir.dt.bfloat16
ACT = mybir.ActivationFunctionType
ALU = mybir.AluOpType
AX = mybir.AxisListType

P = 128
T = 2048
D = 256
TILES = T // P
CT = 4
CHUNK = CT * P
CHUNKS = T // CHUNK
HT = TILES // 2
KD = D // P
EPS = 1e-5
NEG = -1e30

N0, S0 = 8, 8
C0 = 2 * N0 * S0 + N0
R0 = N0 * S0 + N0

H0, G0, D0 = 16, 2, 16
V0 = (H0 + G0) * D0
QKV0 = V0 + G0 * D0
QUAD = 4
QUADS = H0 // QUAD
PAIRS0 = ((0, 0), (1, 0), (0, 1), (1, 1))
VW = 32

E1, I1 = 8, 128
X1 = E1 + 1
H1, G1, D1 = 16, 4, 128
QKV1 = (H1 + 2 * G1) * D1
VO = D1 + 1
VL = D1 + 2


class Steps:

    def __init__(self, eng, sem, base=0):
        self.eng, self.sem, self.base, self.n = eng, sem, base, 0

    def mark(self, ins):
        self.n += 1
        ins.then_inc(self.sem, 1)
        return ins

    def wait(self):
        self.eng.wait_ge(self.sem, self.base + self.n)

    def link(self, ins):
        self.mark(ins)
        self.wait()


class Core:

    def __init__(self, nc, stack, prefix=""):
        self.nc, self.stack, self.prefix, self.sems = nc, stack, prefix, []
        stack.callback(self.clear)

    def clear(self):
        if self.sems:
            self.nc.clear_and_free_semaphores(self.sems)
            self.nc.all_engine_barrier()

    def sb(self, name, shape, dt=F32):
        return self.stack.enter_context(self.nc.sbuf_tensor(self.prefix + name, list(shape), dt))

    def ps(self, name, shape, dt=F32):
        return self.stack.enter_context(self.nc.psum_tensor(self.prefix + name, list(shape), dt))

    def sem(self, name):
        self.sems.append(self.nc.alloc_semaphore(self.prefix + name))
        return self.sems[-1]


def bcast(ap, shape):
    return ap.broadcast_to(list(shape))


def setup(nc, k, a):
    with ExitStack() as stack:
        m = Core(nc, stack, "su_")
        loaded = [m.sem(f"loaded{c}") for c in range(CHUNKS)]
        blank, made = m.sem("blank"), m.sem("made")
        with nc.Block() as block:

            @block.sync
            def _(sp):
                for c in range(CHUNKS):
                    at = slice(c * CT, (c + 1) * CT)
                    sp.dma_start(k.x[:, at, :], a["x"].rearrange("o (t p) d -> p (o t) d", p=P)[:, at, :]) \
                      .then_inc(loaded[c], 16)

            @block.vector
            def _(dve):
                for c in range(CHUNKS):
                    dve.wait_ge(loaded[c], 16)
                    take_stats(dve, k, c * CT, CT)

            @block.gpsimd
            def _(pool):
                pool.memset(k.ident[:, :], 0.0).then_inc(blank, 1)
                pool.memset(k.identb[:, :], 0.0).then_inc(blank, 1)
                pool.memset(k.minusb[:, :], 0.0).then_inc(blank, 1)
                pool.memset(k.mask_qk[:, :], 0.0).then_inc(blank, 1)
                pool.memset(k.mask_kq[:, :], 0.0).then_inc(blank, 1)
                pool.memset(k.ones[:, :], 1.0).then_inc(made, 1)
                pool.memset(k.onesb[:, :], 1.0).then_inc(made, 1)
                pool.memset(k.eps[:, :], EPS).then_inc(made, 1)
                for n in range(N0):
                    pool.memset(k.rev[:, :, n:n + 1], float(N0 - n)).then_inc(made, 1)
                pool.wait_ge(blank, 5)
                for t, one in ((k.ident, 1.0), (k.identb, 1.0), (k.minusb, -1.0)):
                    pool.affine_select(out=t[:, :], in_=t[:, :], compare_op=ALU.not_equal, fill=one, base=0,
                                       pattern=[[-1, P]], channel_multiplier=1).then_inc(made, 1)
                pool.affine_select(out=k.mask_qk[:, :], in_=k.mask_qk[:, :], compare_op=ALU.is_ge, fill=NEG,
                                   base=0, pattern=[[-1, P]], channel_multiplier=1).then_inc(made, 1)
                pool.affine_select(out=k.mask_kq[:, :], in_=k.mask_kq[:, :], compare_op=ALU.is_ge, fill=NEG,
                                   base=0, pattern=[[1, P]], channel_multiplier=-1).then_inc(made, 1)
                pool.wait_ge(made, 3 + N0 + 5)


def take_stats(dve, k, t, n=1):
    for j in range(n):
        ins = dve.bn_stats(k.bn[:, bass.ds(t + j, 1), :].rearrange("p o s -> p (o s)"),
                           k.x[:, bass.ds(t + j, 1), :].rearrange("p o d -> p (o d)"))
    return ins


class Norm:

    def __init__(self, m, k):
        self.k = k
        self.mv = m.sb("mv", [P, TILES, 2])
        self.std, self.r0, self.vr, self.half = (m.sb(n, [P, TILES]) for n in ("std", "r0", "vr", "half"))
        self.steps = m.sem("norm_steps")
        self.var_ready = m.sem("var_ready")
        self.rooted = m.sem("rooted")

    def scale(self, dve):
        k, mv, r0, vr, half = self.k, self.mv, self.r0, self.vr, self.half
        s = Steps(dve, self.steps)
        for t in range(TILES):
            dve.bn_aggr(mv[:, t, :], k.bn[:, t, :]).then_inc(self.var_ready, 1)
        dve.wait_ge(self.var_ready, TILES)
        s.link(dve.tensor_scalar(vr[:, :], mv[:, :, 1], EPS, None, ALU.add))
        dve.wait_ge(self.rooted, 1)
        s.link(dve.reciprocal(r0[:, :], self.std[:, :]))
        s.link(dve.tensor_tensor(half[:, :], r0[:, :], r0[:, :], ALU.mult))
        s.link(dve.tensor_tensor(half[:, :], half[:, :], vr[:, :], ALU.mult))
        s.link(dve.tensor_scalar(half[:, :], half[:, :], -0.5, 1.5, ALU.mult, ALU.add))
        s.link(dve.tensor_tensor(k.rstd[:, :], r0[:, :], half[:, :], ALU.mult))
        s.link(dve.scalar_tensor_tensor(out=k.shift[:, :], in0=mv[:, :, 0], scalar=-1.0,
                                        in1=k.rstd[:, :], op0=ALU.mult, op1=ALU.mult))

    def lengths(self, dve, length2, sem):
        rstd, half = self.k.rstd, self.half
        dve.tensor_tensor(half[:, :], rstd[:, :], rstd[:, :], ALU.mult).then_inc(sem, 1)
        dve.wait_ge(sem, 1)
        dve.scalar_tensor_tensor(out=length2[:, :], in0=self.mv[:, :, 1], scalar=float(D), in1=half[:, :],
                                 op0=ALU.mult, op1=ALU.mult).then_inc(sem, 1)

    def root(self, act):
        act.wait_ge(self.var_ready, TILES)
        act.activation(self.std[:, :], self.mv[:, :, 1], ACT.Sqrt, bias=self.k.eps[:, 0:1]).then_inc(self.rooted, 1)


PRODUCT = ((0, 0), (0, 1), (1, 0))
PIECE = 2048
W_SCALE = 64.0


class NormedPieces:

    def __init__(self, m, k, turned_ps):
        self.k, self.stats = k, Norm(m, k)
        self.turned_ps = turned_ps
        self.xn = m.sb("xn", [P, TILES, D])
        self.xT = m.sb("xT", [P, 2, KD, T], F16)
        self.xn_ready = m.sem("xn_ready")
        self.turned = m.sem("turned")
        self.high = m.sem("xT_high")
        self.low = m.sem("xT_low")

    def halves(self):
        return [(n // KD, n % KD, n % 2, n) for n in range(CHUNKS * KD)]

    def make_pieces(self, act):
        self.stats.root(act)
        for c, h, bank, n in self.halves():
            act.wait_ge(self.turned, n + 1)
            act.activation(self.xT[:, 0, h, c * CHUNK:(c + 1) * CHUNK], self.turned_ps[:, bank, :], ACT.Copy) \
               .then_inc(self.high, 1)

    def norm(self, dve):
        k = self.k
        self.stats.scale(dve)
        dve.sem_inc(self.low, 2)

        def apply(c):
            for t in range(c * CT, (c + 1) * CT):
                ins = dve.tensor_scalar(self.xn[:, t, :], k.x[:, t, :], k.rstd[:, t:t + 1], k.shift[:, t:t + 1],
                                        ALU.mult, ALU.add)
            ins.then_inc(self.xn_ready, 1)

        apply(0)
        for c, h, bank, n in self.halves():
            if h == 0 and c + 1 < CHUNKS:
                apply(c + 1)
            at = slice(c * CHUNK, (c + 1) * CHUNK)
            dve.wait_ge(self.high, n + 1)
            dve.tensor_tensor(self.xT[:, 1, h, at], self.turned_ps[:, bank, :], self.xT[:, 0, h, at],
                              ALU.subtract).then_inc(self.low, 1)

    def turn(self, pe):
        for c, h, bank, n in self.halves():
            pe.wait_ge(self.xn_ready, c + 1)
            pe.wait_ge(self.low, n + 1)
            for j in range(CT):
                ins = pe.transpose(self.turned_ps[:, bank, j * P:(j + 1) * P],
                                   self.xn[:, c * CT + j, h * P:(h + 1) * P], self.k.ident[:, :])
            ins.then_inc(self.turned, 1)
        pe.wait_ge(self.low, 2 + CHUNKS * KD)


class Weights:

    def __init__(self, m, name, source, columns):
        self.name, self.source, self.columns = name, source, columns
        self.pieces = m.sb(name, [P, 2, columns], F16)

    def open(self, m):
        self.raw = m.sb(self.name + "_raw", [P, self.columns])
        self.loaded, self.steps = m.sem(self.name + "_loaded"), m.sem(self.name + "_steps")

    def load(self, sp):
        w = self.source
        raw = self.raw[:, :] if len(w.shape) == 2 else self.raw[:, :].rearrange("p (k c) -> p k c", k=w.shape[1])
        sp.dma_start(raw, w).then_inc(self.loaded, 16)

    def split(self, pool):
        s = Steps(pool, self.steps)
        pool.wait_ge(self.loaded, 16)
        for at in range(0, self.columns, PIECE):
            cols = slice(at, min(at + PIECE, self.columns))
            s.link(pool.tensor_scalar(self.raw[:, cols], self.raw[:, cols], W_SCALE, None, ALU.mult))
            s.link(pool.tensor_copy(self.pieces[:, 0, cols], self.raw[:, cols]))
            s.link(pool.tensor_tensor(self.pieces[:, 1, cols], self.raw[:, cols], self.pieces[:, 0, cols],
                                      ALU.subtract))


def ffn0(nc, k, a, name, prefetch=()):
    with ExitStack() as stack:
        m = Core(nc, stack, name)
        for weights in prefetch:
            weights.open(m)
        w = m.sb("w", [P, KD, C0])
        w2 = m.sb("w2", [R0, D])
        other = m.sb("other", [P, KD, C0])
        center = m.sb("center", [P, N0])
        slope = m.sb("slope", [P, N0])
        const = m.sb("const", [P, C0])
        xn = m.sb("xn", [P, TILES, D])
        xnT = m.sb("xnT", [P, KD, T])
        y = m.sb("y", [P, TILES, C0])
        sq = m.sb("sq", [P, HT, N0 * S0])
        score = m.sb("score", [P, HT, N0])
        len2 = m.sb("len2", [P, HT, N0])
        inv = m.sb("inv", [P, HT, N0])
        z = m.sb("z", [P, HT, N0])
        ez = m.sb("ez", [P, HT, N0])
        gate = m.sb("gate", [P, HT, N0])
        best = m.sb("best", [P, HT])
        first = m.sb("first", [P, HT])
        factor = m.sb("factor", [P, TILES])
        term = m.sb("term", [P, TILES])
        mod = m.sb("mod", [P, TILES, R0])
        modT = m.sb("modT", [R0, 2, CHUNK])
        turned_ps = m.ps("turned_ps", [P, 2, CHUNK])
        w_ps = m.ps("w_ps", [P, 2, 2, 256])
        mod_ps = m.ps("mod_ps", [P, 2, CHUNK])
        out_ps = m.ps("out_ps", [P, 2, 2, D])
        loaded = m.sem("loaded")
        prepared, const_ps_ready, const_ready = m.sem("prepared"), m.sem("const_ps_ready"), m.sem("const_ready")
        norm = Norm(m, k)
        length2 = m.sb("length2", [P, TILES])
        lengths = m.sem("lengths")
        xn_ready = m.sem("xn_ready")
        turned = m.sem("turned")
        xnT_ready = m.sem("xnT_ready")
        first_done = m.sem("first_done")
        y_ready = m.sem("y_ready")
        z_ready = m.sem("z_ready")
        ez_ready = m.sem("ez_ready")
        mod_ready = m.sem("mod_ready")
        mod_turned = m.sem("mod_turned")
        modT_ready = m.sem("modT_ready")
        out_done = m.sem("out_done")
        out_used = m.sem("out_used")
        steps = m.sem("steps")
        block = stack.enter_context(nc.Block())

        @block.sync
        def _(sp):
            sp.dma_start(w[:, :, :], a["ffn0_w"].rearrange("(k p) c -> p k c", p=P)).then_inc(loaded, 16)
            sp.dma_start(other[:, :, :], a["ffn0_other"].rearrange("(k p) c -> p k c", p=P)).then_inc(loaded, 16)
            sp.dma_start(w2[:, :], a["ffn0_w2"]).then_inc(loaded, 16)
            sp.dma_start(center[:, :], a["ffn0_center"]).then_inc(loaded, 16)
            sp.dma_start(slope[:, :], a["ffn0_slope"]).then_inc(loaded, 16)
            for weights in prefetch:
                weights.load(sp)
            sp.wait_ge(loaded, 80)

        @block.gpsimd
        def _(pool):
            for weights in prefetch:
                weights.split(pool)

        def wide(row, tiles):
            over = "p (c o) -> p c o" if tiles else "p (o c) -> p o c"
            return bcast(row.rearrange(over, o=1), [P, HT, N0])

        @block.vector
        def _(dve):
            norm.scale(dve)
            s = Steps(dve, steps)
            for c in range(CHUNKS):
                for t in range(c * CT, (c + 1) * CT):
                    ins = dve.tensor_scalar(xn[:, t, :], k.x[:, t, :], k.rstd[:, t:t + 1], k.shift[:, t:t + 1],
                                            ALU.mult, ALU.add)
                ins.then_inc(xn_ready, 1)
            norm.lengths(dve, length2, lengths)
            dve.wait_ge(loaded, 80)
            dve.tensor_tensor(other[:, :, :], other[:, :, :], w[:, :, :], ALU.mult).then_inc(prepared, 1)
            dve.wait_ge(const_ps_ready, 1)
            sums = w_ps[:, 1, 1, :]
            dve.tensor_copy(const[:, 0:C0 - N0], sums[:, 0:C0 - N0]).then_inc(const_ready, 1)
            dve.tensor_scalar(const[:, C0 - N0:C0], sums[:, C0 - N0:C0], 0.5, None, ALU.mult).then_inc(const_ready, 1)
            dve.wait_ge(const_ready, 2)

            def keep_y(half):
                for p in range(half * HT // 2, (half + 1) * HT // 2):
                    dve.wait_ge(first_done, p + 1)
                    dve.tensor_tensor(y[:, 2 * p:2 * p + 2, :], w_ps[:, p % 2, :, 0:C0],
                                      bcast(const[:, :].rearrange("p (o c) -> p o c", o=1), [P, 2, C0]),
                                      ALU.subtract).then_inc(y_ready, 1)

            def gates(half):
                at = slice(half * HT, (half + 1) * HT)
                yh = y[:, at, :]
                dve.wait_ge(y_ready, (half + 1) * HT // 2)
                s.mark(dve.tensor_tensor(sq[:, :, :], yh[:, :, 0:64], yh[:, :, 0:64], ALU.mult))
                dve.wait_ge(lengths, 2)
                s.link(dve.scalar_tensor_tensor(out=len2[:, :, :], in0=yh[:, :, C0 - N0:C0], scalar=-2.0,
                                                in1=wide(length2[:, at], True), op0=ALU.mult, op1=ALU.add))
                s.mark(dve.tensor_reduce(score[:, :, :], sq[:, :, :].rearrange("p c (n s) -> p c n s", s=S0),
                                         AX.X, ALU.add))
                s.link(dve.reciprocal(inv[:, :, :], len2[:, :, :]))
                s.link(dve.tensor_tensor(score[:, :, :], score[:, :, :], inv[:, :, :], ALU.mult))
                s.link(dve.tensor_tensor(score[:, :, :], score[:, :, :], wide(center[:, :], False), ALU.subtract))
                dve.tensor_tensor(z[:, :, :], score[:, :, :], wide(slope[:, :], False), ALU.mult).then_inc(z_ready, 1)
                dve.wait_ge(ez_ready, half + 1)
                s.link(dve.tensor_scalar(inv[:, :, :], ez[:, :, :], 1.0, None, ALU.add))
                s.link(dve.reciprocal(gate[:, :, :], inv[:, :, :]))
                s.link(dve.tensor_reduce(best[:, :], gate[:, :, :], AX.X, ALU.max))
                s.link(dve.tensor_tensor(score[:, :, :], gate[:, :, :], wide(best[:, :], True), ALU.is_equal))
                s.link(dve.tensor_tensor(score[:, :, :], score[:, :, :], k.rev[:, 0:HT, :], ALU.mult))
                s.link(dve.tensor_reduce(first[:, :], score[:, :, :], AX.X, ALU.max))
                s.link(dve.tensor_tensor(score[:, :, :], score[:, :, :], wide(first[:, :], True), ALU.is_equal))
                s.link(dve.scalar_tensor_tensor(out=mod[:, at, 64:R0], in0=score[:, :, :], scalar=0.5,
                                                in1=wide(best[:, :], True), op0=ALU.mult, op1=ALU.mult))
                dve.tensor_tensor(
                    mod[:, at, 0:64].rearrange("p c (n s) -> p c n s", s=S0),
                    yh[:, :, 64:128].rearrange("p c (n s) -> p c n s", s=S0),
                    bcast(mod[:, at, 64:R0].rearrange("p c (n o) -> p c n o", o=1), [P, HT, N0, S0]),
                    ALU.mult).then_inc(mod_ready, 1)
                s.link(dve.tensor_scalar(best[:, :], best[:, :], -0.5, 0.5, ALU.mult, ALU.add))
                s.mark(dve.tensor_tensor(term[:, at], best[:, :], k.shift[:, at], ALU.mult))
                s.link(dve.tensor_tensor(factor[:, at], best[:, :], k.rstd[:, at], ALU.mult))
                s.link(dve.tensor_scalar(factor[:, at], factor[:, at], 1.0, None, ALU.add))
                for t in range(half * HT, (half + 1) * HT):
                    s.mark(dve.tensor_scalar(k.x[:, t, :], k.x[:, t, :], factor[:, t:t + 1], term[:, t:t + 1],
                                             ALU.mult, ALU.add))

            def add_out(half):
                for p in range(half * HT // 2, (half + 1) * HT // 2):
                    dve.wait_ge(out_done, p + 1)
                    x = k.x[:, 2 * p:2 * p + 2, :]
                    dve.tensor_tensor(x, x, out_ps[:, p % 2, :, :], ALU.add).then_inc(out_used, 1)
                    dve.wait_ge(out_used, p + 1)
                    take_stats(dve, k, 2 * p, 2)

            keep_y(0)
            gates(0)
            keep_y(1)
            gates(1)
            s.wait()
            add_out(0)
            add_out(1)

        @block.scalar
        def _(act):
            norm.root(act)
            for n in range(CHUNKS * KD):
                c, h = n // KD, n % KD
                act.wait_ge(turned, n + 1)
                act.activation(xnT[:, h, c * CHUNK:(c + 1) * CHUNK], turned_ps[:, n % 2, :], ACT.Copy) \
                   .then_inc(xnT_ready, 1)

            for half in range(2):
                act.wait_ge(z_ready, half + 1)
                act.activation(ez[:, :, :], z[:, :, :], ACT.Exp, scale=-1.0).then_inc(ez_ready, 1)
                for c in range(half * CHUNKS // 2, (half + 1) * CHUNKS // 2):
                    act.wait_ge(mod_turned, c + 1)
                    if c >= 2:
                        act.wait_ge(out_done, (c - 1) * CT // 2)
                    act.activation(modT[:, c % 2, :], mod_ps[0:R0, c % 2, :], ACT.Copy).then_inc(modT_ready, 1)

        @block.tensor
        def _(pe):
            for n in range(CHUNKS * KD):
                c, h = n // KD, n % KD
                pe.wait_ge(xn_ready, c + 1)
                if n >= 2:
                    pe.wait_ge(xnT_ready, n - 1)
                for j in range(CT):
                    ins = pe.transpose(turned_ps[:, n % 2, j * P:(j + 1) * P],
                                       xn[:, c * CT + j, h * P:(h + 1) * P], k.ident[:, :])
                ins.then_inc(turned, 1)
            pe.wait_ge(prepared, 1)
            for kt in range(KD):
                ins = pe.matmul(w_ps[:, 1, 1, 0:C0], k.ones[:, :], other[:, kt, :], start=(kt == 0),
                                stop=(kt == KD - 1))
            ins.then_inc(const_ps_ready, 1)
            pe.wait_ge(const_ready, 2)

            def first_products(half):
                for p in range(half * HT // 2, (half + 1) * HT // 2):
                    pe.wait_ge(xnT_ready, (2 * p // CT + 1) * KD)
                    if p >= 2:
                        pe.wait_ge(y_ready, p - 1)
                    for j in range(2):
                        t = 2 * p + j
                        for kt in range(KD):
                            ins = pe.matmul(w_ps[:, p % 2, j, 0:C0], xnT[:, kt, t * P:(t + 1) * P], w[:, kt, :],
                                            start=(kt == 0), stop=(kt == KD - 1))
                    ins.then_inc(first_done, 1)

            def second_products(half):
                pe.wait_ge(mod_ready, half + 1)
                for c in range(half * CHUNKS // 2, (half + 1) * CHUNKS // 2):
                    if c >= 2:
                        pe.wait_ge(modT_ready, c - 1)
                    for j in range(CT):
                        ins = pe.transpose(mod_ps[0:R0, c % 2, j * P:(j + 1) * P], mod[:, c * CT + j, :],
                                           k.ident[:, :])
                    ins.then_inc(mod_turned, 1)
                for p in range(half * HT // 2, (half + 1) * HT // 2):
                    c = 2 * p // CT
                    pe.wait_ge(modT_ready, c + 1)
                    if p >= 2:
                        pe.wait_ge(out_used, p - 1)
                    for j in range(2):
                        at = (2 * p + j) % CT * P
                        ins = pe.matmul(out_ps[:, p % 2, j, :], modT[:, c % 2, at:at + P], w2[:, :], start=True,
                                        stop=True)
                    ins.then_inc(out_done, 1)

            for half in range(2):
                first_products(half)
            for half in range(2):
                second_products(half)


def qkv0(nc, k, a, w_pieces, v_aug, qs, ks):
    with ExitStack() as stack:
        m = Core(nc, stack, "qkv0_")
        w = w_pieces.pieces[:, :, :].rearrange("p e (k c) -> p e k c", k=KD)
        bq = m.sb("bq", [P, 2])
        bk = m.sb("bk", [G0 * D0, 1])
        bv = m.sb("bv", [P, G0 * D0])
        full = m.sb("full", [P, 3, CHUNK])
        pieces = m.sb("pieces", [P, 2, 3, 2, CHUNK], F16)
        qk_ps = m.ps("qk_ps", [P, 3, CHUNK])
        v_ps = m.ps("v_ps", [P, CT, G0 * D0])
        nd = NormedPieces(m, k, m.ps("turned_ps", [P, 2, CHUNK]))
        loaded = m.sem("loaded")
        done = m.sem("done")
        high = m.sem("high")
        low = m.sem("low")
        v_done = m.sem("v_done")
        v_used = m.sem("v_used")
        padded = m.sem("padded")
        stored = [m.sem("stored0"), m.sem("stored1")]
        in_dram = m.sem("in_dram")
        spread = m.sem("spread")
        block = stack.enter_context(nc.Block())
        rows = [P, P, G0 * D0]

        @block.sync
        def _(sp):
            for b in range(2):
                sp.sem_inc(stored[b], 48)
            sp.dma_start(bq[:, :], a["bq0"]).then_inc(loaded, 16)
            sp.dma_start(bk[:, :], a["bk0"].rearrange("(p o) -> p o", o=1)).then_inc(loaded, 16)
            sp.dma_start(bv[:, :], a["bv0"]).then_inc(loaded, 16)
            with sp.Fori(0, CHUNKS // 2) as i:
                for b in range(2):
                    c = i * 2 + b
                    sp.wait_ge(low, 3 + (c + 1) * 3)
                    for n in range(2):
                        sp.dma_start(a["q0_scr"][n, :, :, bass.ds(c * CHUNK, CHUNK)], pieces[:, b, n, :, :]) \
                          .then_inc(stored[b], 16)
                    sp.dma_start(a["k0_scr"][:, :, bass.ds(c * CHUNK, CHUNK)],
                                 pieces[0:G0 * D0, b, 2, :, :]).then_inc(stored[b], 16)
                for b in range(2):
                    sp.wait_ge(stored[b], 48 * (i + 2))
                sp.sem_inc(in_dram, 1)
                tokens = bass.ds(i * (2 * CHUNK), 2 * CHUNK)
                for r, (pq, pk) in enumerate(PAIRS0):
                    to = slice(r * D0, (r + 1) * D0)
                    sp.dma_start(qs[to, :, tokens], a["q0_scr"].rearrange("m (h r) e t -> r (m h) e t", r=D0)
                                 [:, :, pq, tokens]).then_inc(spread, 16)
                    sp.dma_start(ks[to, :, tokens], a["k0_scr"].rearrange("(g r) e t -> r g e t", r=D0)
                                 [:, :, pk, tokens]).then_inc(spread, 16)
            sp.wait_ge(spread, 16 * CHUNKS // 2 * 2 * len(PAIRS0))

        @block.gpsimd
        def _(pool):
            pool.memset(v_aug[:, :, :, D0:D0 + 1], 1.0).then_inc(padded, 1)
            pool.memset(v_aug[:, :, :, D0 + 1:VW], 0.0).then_inc(padded, 1)
            pool.wait_ge(padded, 2)
            pool.memset(ks[64:P, :, :], 0.0).then_inc(padded, 1)
            pool.wait_ge(padded, 3)
            pool.memset(ks[64:65, :, :], 1.0).then_inc(padded, 1)
            pool.wait_ge(padded, 4)
            pool.memset(qs[64:P, :, :], 0.0).then_inc(padded, 1)
            pool.wait_ge(padded, 5)

        @block.vector
        def _(dve):
            dve.sem_inc(low, 3)
            dve.sem_inc(v_used, 1)
            nd.norm(dve)
            dve.wait_ge(loaded, 48)
            with dve.Fori(0, CHUNKS // 2) as i:
                for b in range(2):
                    c = i * 2 + b
                    for n in range(3):
                        r = rows[n]
                        dve.wait_ge(high, 3 + c * 3 + n + 1)
                        dve.tensor_tensor(pieces[0:r, b, n, 1, :], full[0:r, n, :], pieces[0:r, b, n, 0, :],
                                          ALU.subtract).then_inc(low, 1)
                    dve.wait_ge(v_done, c + 1)
                    for g in range(G0):
                        cols = slice(g * D0, (g + 1) * D0)
                        ins = dve.scalar_tensor_tensor(
                            out=v_aug[:, bass.ds(c * CT, CT), g, 0:D0], in0=v_ps[:, :, cols], scalar=1 / W_SCALE,
                            in1=bcast(bv[:, cols].rearrange("p (o d) -> p o d", o=1), [P, CT, D0]), op0=ALU.mult,
                            op1=ALU.add)
                    ins.then_inc(v_used, 1)

        @block.scalar
        def _(act):
            act.sem_inc(high, 3)
            nd.make_pieces(act)
            act.wait_ge(loaded, 48)
            with act.Fori(0, CHUNKS // 2) as i:
                for b in range(2):
                    c = i * 2 + b
                    act.wait_ge(stored[b], (i + 1) * 48)
                    for n in range(3):
                        r = rows[n]
                        bias = bq[:, n:n + 1] if n < 2 else bk[:, 0:1]
                        act.wait_ge(done, c * 3 + n + 1)
                        act.wait_ge(low, c * 3 + n + 1)
                        act.activation(full[0:r, n, :], qk_ps[0:r, n, :], ACT.Identity, bias=bias, scale=1 / W_SCALE)
                        act.activation(pieces[0:r, b, n, 0, :], qk_ps[0:r, n, :], ACT.Identity, bias=bias,
                                       scale=1 / W_SCALE).then_inc(high, 1)

        @block.tensor
        def _(pe):
            nd.turn(pe)
            with pe.Fori(0, CHUNKS // 2) as i:
                for b in range(2):
                    c = i * 2 + b
                    for n in range(3):
                        if n < 2:
                            pe.wait_ge(high, c * 3 + (1, 3)[n])
                        for step, (kt, (pw, px)) in enumerate(product(range(KD), PRODUCT)):
                            ins = pe.matmul(qk_ps[0:rows[n], n, :], w[:, pw, kt, n * P:n * P + rows[n]],
                                            nd.xT[:, px, kt, bass.ds(c * CHUNK, CHUNK)], start=(step == 0),
                                            stop=(step == KD * len(PRODUCT) - 1))
                        ins.then_inc(done, 1)
                    pe.wait_ge(v_used, c + 1)
                    for j in range(CT):
                        for step, (kt, (px, pw)) in enumerate(product(range(KD), PRODUCT)):
                            ins = pe.matmul(v_ps[:, j, :], nd.xT[:, px, kt, bass.ds((c * CT + j) * P, P)],
                                            w[:, pw, kt, V0:V0 + G0 * D0], start=(step == 0),
                                            stop=(step == KD * len(PRODUCT) - 1))
                    ins.then_inc(v_done, 1)


class Attn0Plan:

    units = [(c, kt) for c in range(CHUNKS) for kt in range(CT * c + CT)]
    maxima = [(qt, kc, h) for qt in range(TILES) for kc in range(qt // CT + 1) for h in range(QUAD)]
    UNITS, MAXIMA = len(units), len(maxima)
    LEAD = 84
    LAG = 2
    RING = 4
    BEHIND = 4
    STEPS = UNITS + LAG

    @classmethod
    def maxima_at(cls, u):
        at = [cls.LEAD + v * cls.MAXIMA // cls.STEPS for v in (u, u + 1)]
        return [(n % cls.MAXIMA, n // cls.MAXIMA) for n in range(*at)]

    @classmethod
    def ended_by(cls, u):
        if u < 0:
            return []
        return [(cls.ends_chunk(n), later) for n, later in cls.maxima_at(u) if cls.ends_chunk(n) is not None]

    @classmethod
    def ends_chunk(cls, n):
        c = cls.maxima[n][0] // CT
        last = n + 1 == cls.MAXIMA or cls.maxima[n + 1][0] // CT > c
        return c if last else None


def attn0(nc, k, v_aug, qs, ks, att):
    plan = Attn0Plan
    SCALE = float(D0) ** -0.5
    with ExitStack() as stack:
        m = Core(nc, stack, "attn0_")
        k_now = m.sb("k_now", [P, T], F16)
        v_now = m.sb("v_now", [P, TILES, VW])
        part = m.sb("part", [P, TILES, QUAD, CHUNKS])
        mx = m.sb("mx", [P, P])
        mxT = m.sb("mxT", [QUAD * CT, P], F16)
        prob = m.sb("prob", [P, plan.RING, QUAD, CHUNK])
        oT = m.sb("oT", [P, CHUNK])
        inv = m.sb("inv", [P, CT, QUAD])
        score_ps = m.ps("score_ps", [P, 2, 2, CHUNK])
        max_ps = m.ps("max_ps", [P, 2, CHUNK])
        o_ps = m.ps("o_ps", [P, CHUNK])
        misc_ps = m.ps("misc_ps", [P, CHUNK])
        max_done = m.sem("max_done")
        max_used = m.sem("max_used")
        part_blank = m.sem("part_blank")
        mx_ready = m.sem("mx_ready")
        mx_turned = m.sem("mx_turned")
        mxT_ready = m.sem("mxT_ready")
        row_set = m.sem("row_set")
        now_set = m.sem("now_set")
        scored = m.sem("scored")
        exped = m.sem("exped")
        weighed = m.sem("weighed")
        o_kept = m.sem("o_kept")
        o_turned = m.sem("o_turned")
        o_out = m.sem("o_out")
        inv_ready = m.sem("inv_ready")
        block = stack.enter_context(nc.Block())
        PU, PM = plan.UNITS, plan.MAXIMA

        @block.gpsimd
        def _(pool):
            pool.memset(part[:, :, :, :], NEG).then_inc(part_blank, 1)
            pool.wait_ge(part_blank, 1)
            pool.memset(mx[:, :], 0.0).then_inc(part_blank, 1)
            pool.wait_ge(part_blank, 2)

        @block.sync
        def _(sp):
            sp.sem_inc(row_set, 16 * QUAD)
            def set_row(g, c):
                sp.wait_ge(mxT_ready, g * CHUNKS + c + 1)
                for h in range(QUAD):
                    sp.dma_start(qs[64:65, bass.ds(g * QUAD + h, 1), c * CHUNK:(c + 1) * CHUNK]
                                 .rearrange("o h (t p) -> o (h t) p", p=P), mxT[h * CT:(h + 1) * CT, :]) \
                      .then_inc(row_set, 16)

            with sp.Fori(0, QUADS) as g:
                for c in range(CHUNKS):
                    set_row(g, c)
            sp.wait_ge(row_set, 16 * QUAD * (1 + QUADS * CHUNKS))

        def all_passes(eng, first, one_pass):
            first()
            with eng.Fori(0, QUADS - 1) as g:
                one_pass(g, True)
            one_pass(QUADS - 1, False)

        @block.vector
        def _(dve):
            dve.sem_inc(max_used, 2)
            dve.sem_inc(o_out, 1)
            dve.wait_ge(part_blank, 2)

            def reduce_max(g, n):
                qt, kc, h = plan.maxima[n]
                w = min(CHUNK, (qt + 1) * P - kc * CHUNK)
                tile = g * PM + n
                dve.wait_ge(max_done, tile + 1)
                dve.tensor_reduce(part[:, qt, h, kc:kc + 1], max_ps[:, n % 2, 0:w], AX.X, ALU.max).then_inc(max_used, 1)
                c = plan.ends_chunk(n)
                if c is not None:
                    dve.wait_ge(max_used, 2 + tile + 1)
                    dve.tensor_reduce(mx[:, 0:QUAD * CT].rearrange("p (h t) -> p t h", t=CT),
                                      part[:, CT * c:CT * c + CT, :, :], AX.X, ALU.max, negate=True) \
                       .then_inc(mx_ready, 1)

            def keep_maxima(g, c):
                dve.wait_ge(mx_turned, g * CHUNKS + c + 1)
                dve.wait_ge(row_set, 16 * QUAD * (g * CHUNKS + c + 1))
                dve.tensor_copy(mxT[:, :], misc_ps[0:QUAD * CT, 0:P]).then_inc(mxT_ready, 1)

            def set_keys(g):
                dve.tensor_copy(k_now[:, :], ks[:, bass.ds(g // 2, 1), :].rearrange("p o t -> p (o t)")) \
                   .then_inc(now_set, 1)

            def set_values(g):
                dve.tensor_copy(v_now[:, :, :], v_aug[:, :, bass.ds(g // 2, 1), :].rearrange("p t o w -> p t (o w)")) \
                   .then_inc(now_set, 1)

            def put_out(g, c):
                dve.wait_ge(o_turned, g * CHUNKS + c + 1)
                o = misc_ps[:, :].rearrange("p (t h w) -> p t h w", t=CT, h=QUAD)
                dve.reciprocal(inv[:, :, :], o[:, :, :, D0:D0 + 1].rearrange("p t h o -> p t (h o)")) \
                   .then_inc(inv_ready, 1)
                dve.wait_ge(inv_ready, g * CHUNKS + c + 1)
                dve.tensor_tensor(
                    att[:, CT * c:CT * (c + 1), bass.ds(g * QUAD, QUAD), :], o[:, :, :, 0:D0],
                    bcast(inv[:, :, :].rearrange("p t (h o) -> p t h o", o=1), [P, CT, QUAD, D0]),
                    ALU.mult).then_inc(o_out, 1)

            def first():
                set_keys(0)
                set_values(0)
                for n in range(plan.LEAD):
                    reduce_max(0, n)
                    if n >= plan.BEHIND and plan.ends_chunk(n - plan.BEHIND) is not None:
                        keep_maxima(0, plan.ends_chunk(n - plan.BEHIND))

            def one_pass(g, nxt):
                for u in range(plan.STEPS):
                    c, kt = plan.units[u] if u < PU else (CHUNKS, u - PU)
                    if c > 0 and kt == plan.LAG + 1:
                        put_out(g, c - 1)
                    if nxt and u == PU:
                        dve.wait_ge(scored, (g + 1) * PU * 2)
                        set_keys(g + 1)
                    for n, later in plan.maxima_at(u):
                        if nxt or not later:
                            reduce_max(g + later, n)
                    for ended, later in plan.ended_by(u - 1):
                        if nxt or not later:
                            keep_maxima(g + later, ended)
                if nxt:
                    dve.wait_ge(weighed, plan.RING + (g + 1) * PU)
                    set_values(g + 1)
                put_out(g, CHUNKS - 1)

            all_passes(dve, first, one_pass)

        @block.scalar
        def _(act):
            act.sem_inc(exped, 2)
            act.sem_inc(o_kept, 1)

            def keep_o(g, c):
                act.wait_ge(weighed, plan.RING + g * PU + CT * (c + 1) * (c + 2) // 2)
                act.wait_ge(o_out, g * CHUNKS + c + 1)
                act.activation(oT[:, :], o_ps[:, :], ACT.Copy).then_inc(o_kept, 1)

            with act.Fori(0, QUADS) as g:
                for u, (c, kt) in enumerate(plan.units):
                    off = max(0, kt - CT * c) * P
                    if c > 0 and kt == plan.LAG:
                        keep_o(g, c - 1)
                    act.wait_ge(weighed, g * PU + u + 1)
                    for pair in range(2):
                        act.wait_ge(scored, (g * PU + u) * 2 + pair + 1)
                        act.activation(prob[:, u % plan.RING, 2 * pair:2 * pair + 2, off:CHUNK],
                                       score_ps[:, pair, :, off:CHUNK], ACT.Exp, scale=SCALE).then_inc(exped, 1)
                keep_o(g, CHUNKS - 1)

        @block.tensor
        def _(pe):
            pe.sem_inc(weighed, plan.RING)
            pe.wait_ge(part_blank, 2)

            def max_tile(g, n):
                qt, kc, h = plan.maxima[n]
                w = min(CHUNK, (qt + 1) * P - kc * CHUNK)
                diagonal = kc == qt // CT
                pe.wait_ge(max_used, g * PM + n + 1)
                out = max_ps[:, n % 2, :]
                ins = pe.matmul(out[:, 0:w],
                                qs[:, bass.ds(g * QUAD + h, 1), qt * P:(qt + 1) * P].rearrange("p o t -> p (o t)"),
                                ks[:, bass.ds(g // 2, 1), kc * CHUNK:kc * CHUNK + w].rearrange("p o t -> p (o t)"),
                                start=True, stop=not diagonal)
                if diagonal:
                    ins = pe.matmul(out[:, w - P:w], k.identb[:, :], k.mask_qk[:, :], start=False, stop=True)
                ins.then_inc(max_done, 1)

            def turn_maxima(g, c, outputs):
                pe.wait_ge(mx_ready, g * CHUNKS + c + 1)
                pe.wait_ge(o_out, outputs + 1)
                pe.transpose(misc_ps[:, 0:P], mx[:, :], k.ident[:, :]).then_inc(mx_turned, 1)

            def score(g, u, pair):
                c, kt = plan.units[u]
                off = max(0, kt - CT * c) * P
                if pair == 0 and kt == 0:
                    pe.wait_ge(row_set, 16 * QUAD * (1 + g * CHUNKS + c + 1))
                pe.wait_ge(exped, (g * PU + u) * 2 + pair + 1)
                for h in range(2):
                    head = g * QUAD + 2 * pair + h
                    diagonal = kt >= CT * c
                    ins = pe.matmul(score_ps[:, pair, h, off:CHUNK],
                                    k_now[:, kt * P:(kt + 1) * P],
                                    qs[:, bass.ds(head, 1), c * CHUNK + off:(c + 1) * CHUNK]
                                    .rearrange("p o t -> p (o t)"), start=True, stop=not diagonal)
                    if diagonal:
                        ins = pe.matmul(score_ps[:, pair, h, off:off + P], k.identb[:, :], k.mask_kq[:, :],
                                        start=False, stop=True)
                ins.then_inc(scored, 1)

            def weigh(g, u, pair):
                c, kt = plan.units[u]
                off = max(0, kt - CT * c) * P
                pe.wait_ge(exped, 2 + (g * PU + u) * 2 + pair + 1)
                if u == 0 and pair == 0:
                    pe.wait_ge(now_set, g * 2 + 2)
                if kt == 0 and pair == 0:
                    pe.wait_ge(o_kept, g * CHUNKS + c + 1)
                for h in range(2 * pair, 2 * pair + 2):
                    ins = pe.matmul(o_ps[32 * h:32 * h + 32, off:CHUNK], v_now[:, kt, :],
                                    prob[:, u % plan.RING, h, off:CHUNK],
                                    start=(kt == 0), stop=(kt == CT * c + CT - 1), skip_group_check=True)
                if pair == 1:
                    ins.then_inc(weighed, 1)

            def turn_o(g, c, maxima):
                pe.wait_ge(o_kept, 1 + g * CHUNKS + c + 1)
                pe.wait_ge(mxT_ready, maxima)
                pe.wait_ge(o_out, g * CHUNKS + c + 1)
                for t in range(CT):
                    ins = pe.transpose(misc_ps[:, t * P:(t + 1) * P], oT[:, t * P:(t + 1) * P], k.ident[:, :])
                ins.then_inc(o_turned, 1)

            def first():
                for n in range(plan.LEAD):
                    max_tile(0, n)
                    if n >= plan.BEHIND and plan.ends_chunk(n - plan.BEHIND) is not None:
                        turn_maxima(0, plan.ends_chunk(n - plan.BEHIND), 0)

            def one_pass(g, nxt):
                pe.wait_ge(now_set, g * 2 + 1)
                outputs = 0
                maxima = sum(plan.ends_chunk(n) is not None for n in range(plan.LEAD))
                for u in range(plan.STEPS):
                    c, kt = plan.units[u] if u < PU else (CHUNKS, u - PU)
                    tiles = [t for t in plan.maxima_at(u) if nxt or not t[1]]
                    for step in range(4):
                        if step < 2 and u < PU:
                            score(g, u, step)
                        if step >= 2 and u >= plan.LAG:
                            weigh(g, u - plan.LAG, step - 2)
                        for n, later in tiles[step:step + 1]:
                            max_tile(g + later, n)
                    for ended, later in plan.ended_by(u - 1):
                        if nxt or not later:
                            turn_maxima(g + later, ended, g * CHUNKS + outputs)
                            maxima += 1
                    if c > 0 and kt == plan.LAG:
                        turn_o(g, c - 1, g * CHUNKS + maxima)
                        outputs += 1
                turn_o(g, CHUNKS - 1, g * CHUNKS + maxima)

            all_passes(pe, first, one_pass)


def wo0(nc, k, a, att):
    with ExitStack() as stack:
        m = Core(nc, stack, "wo0_")
        wo = m.sb("wo", [P, KD, D])
        bo = m.sb("bo", [P, D])
        attT = m.sb("attT", [P, 2, KD, CHUNK])
        turned_ps = m.ps("turned_ps", [P, 2, KD, CHUNK])
        out_ps = m.ps("out_ps", [P, 2, CT, D])
        loaded = m.sem("loaded")
        turned = m.sem("turned")
        kept = m.sem("kept")
        biased = m.sem("biased")
        done = m.sem("done")
        used = m.sem("used")
        block = stack.enter_context(nc.Block())

        @block.sync
        def _(sp):
            sp.dma_start(wo[:, :, :], a["wo0"].rearrange("(k p) c -> p k c", p=P)).then_inc(loaded, 16)
            sp.dma_start(bo[:, :], a["bo0"]).then_inc(loaded, 16)
            sp.wait_ge(loaded, 32)

        @block.vector
        def _(dve):
            dve.wait_ge(loaded, 32)
            for c in range(CHUNKS):
                x = k.x[:, c * CT:(c + 1) * CT, :]
                dve.tensor_tensor(x, x, bcast(bo[:, :].rearrange("p (o c) -> p o c", o=1), [P, CT, D]),
                                  ALU.add).then_inc(biased, 1)
            for c in range(CHUNKS):
                x = k.x[:, c * CT:(c + 1) * CT, :]
                dve.wait_ge(biased, c + 1)
                dve.wait_ge(done, c + 1)
                dve.tensor_tensor(x, x, out_ps[:, c % 2, :, :], ALU.add).then_inc(used, 1)
                dve.wait_ge(used, c + 1)
                take_stats(dve, k, c * CT, CT)

        @block.scalar
        def _(act):
            for c in range(CHUNKS):
                if c >= 2:
                    act.wait_ge(done, c - 1)
                for h in range(KD):
                    act.wait_ge(turned, c * KD + h + 1)
                    act.activation(attT[:, c % 2, h, :], turned_ps[:, c % 2, h, :], ACT.Copy).then_inc(kept, 1)

        @block.tensor
        def _(pe):
            def turn(c):
                if c >= 2:
                    pe.wait_ge(kept, (c - 1) * KD)
                for h in range(KD):
                    heads = slice(h * H0 // KD, (h + 1) * H0 // KD)
                    for j in range(CT):
                        ins = pe.transpose(turned_ps[:, c % 2, h, j * P:(j + 1) * P],
                                           att[:, c * CT + j, heads, :].rearrange("p h w -> p (h w)"), k.ident[:, :])
                    ins.then_inc(turned, 1)

            turn(0)
            pe.wait_ge(loaded, 32)
            for c in range(CHUNKS):
                if c + 1 < CHUNKS:
                    turn(c + 1)
                pe.wait_ge(kept, (c + 1) * KD)
                if c >= 2:
                    pe.wait_ge(used, c - 1)
                for j in range(CT):
                    for kt in range(KD):
                        ins = pe.matmul(out_ps[:, c % 2, j, :], attT[:, c % 2, kt, j * P:(j + 1) * P], wo[:, kt, :],
                                        start=(kt == 0), stop=(kt == KD - 1))
                ins.then_inc(done, 1)




def ffn1(nc, k, a, name, w13_pieces, gw_pieces, prefetch=(), last=False):
    with ExitStack() as stack:
        m = Core(nc, stack, name)
        for weights in prefetch:
            weights.open(m)
        w13 = w13_pieces.pieces[:, :, :].rearrange("p e (k x w i) -> p e k x w i", k=KD, x=X1, w=2)
        gw = gw_pieces.pieces[:, :, :].rearrange("p e (k x) -> p e k x", k=KD)
        w2 = m.sb("w2", [P, X1, D])
        gb = m.sb("gb", [P, E1])
        lg = m.sb("lg", [P, TILES, E1])
        el = m.sb("el", [P, TILES, E1])
        prob = m.sb("prob", [P, TILES, E1])
        bias = m.sb("bias", [P, TILES, E1])
        pick = m.sb("pick", [P, TILES, E1])
        chosen = m.sb("chosen", [P, TILES, E1])
        top = m.sb("top", [P, TILES])
        dw = m.sb("dw", [P, TILES, X1])
        act1 = m.sb("act1", [P, 2, CHUNK])
        hid = m.sb("hid", [P, 2, CHUNK])
        lg_ps = m.ps("lg_ps", [P, TILES, E1])
        h_ps = m.ps("h_ps", [P, 2, 2, CHUNK])
        y_ps = m.ps("y_ps", [P, CT, D])
        nd = NormedPieces(m, k, y_ps[:, :, :].rearrange("p (b t) d -> p b (t d)", b=2))
        loaded = m.sem("loaded")
        shared_set = m.sem("shared_set")
        lg_done = m.sem("lg_done")
        lg_ready = m.sem("lg_ready")
        el_ready = m.sem("el_ready")
        dw_ready = m.sem("dw_ready")
        h_done = m.sem("h_done")
        act_ready = m.sem("act_ready")
        hid_ready = m.sem("hid_ready")
        y_done = m.sem("y_done")
        y_used = m.sem("y_used")
        stored = m.sem("stored")
        steps = m.sem("steps")
        block = stack.enter_context(nc.Block())

        @block.sync
        def _(sp):
            sp.dma_start(gb[:, :], a["gate1_b"]).then_inc(loaded, 16)
            sp.dma_start(w2[:, :, :], a["w2"].rearrange("x p d -> p x d")).then_inc(loaded, 16)
            for weights in prefetch:
                weights.load(sp)
            sp.wait_ge(loaded, 32)
            if last:
                for c in range(CHUNKS):
                    at = slice(c * CT, (c + 1) * CT)
                    sp.wait_ge(y_used, CT * (1 + (c + 1) * X1))
                    sp.dma_start(a["out"].rearrange("o (t p) d -> p (o t) d", p=P)[:, at, :], k.x[:, at, :]) \
                      .then_inc(stored, 16)
                sp.wait_ge(stored, 16 * CHUNKS)

        @block.gpsimd
        def _(pool):
            for weights in prefetch:
                weights.split(pool)

        @block.vector
        def _(dve):
            dve.sem_inc(hid_ready, 2)
            dve.sem_inc(y_used, CT)
            dve.memset(dw[:, :, E1:X1], 0.5).then_inc(shared_set, 1)
            dve.wait_ge(shared_set, 1)
            nd.norm(dve)
            dve.wait_ge(loaded, 32)

            def wide(ap):
                return bcast(ap.rearrange("p (c o) -> p c o", o=1), [P, TILES, E1])

            def gating(s):
                dve.wait_ge(lg_done, 1)
                s.link(dve.tensor_reduce(top[:, :], lg_ps[:, :, :], AX.X, ALU.max))
                dve.tensor_tensor(lg[:, :, :], lg_ps[:, :, :], wide(top[:, :]), ALU.subtract).then_inc(lg_ready, 1)
                dve.wait_ge(el_ready, 1)
                s.link(dve.tensor_reduce(top[:, :], el[:, :, :], AX.X, ALU.add))
                s.link(dve.reciprocal(top[:, :], top[:, :]))
                s.link(dve.tensor_tensor(prob[:, :, :], el[:, :, :], wide(top[:, :]), ALU.mult))
                s.link(dve.tensor_tensor(bias[:, :, :], prob[:, :, :], bcast(
                    gb[:, :].rearrange("p (o e) -> p o e", o=1), [P, TILES, E1]), ALU.add))
                for r in range(2):
                    out = (chosen, pick)[r]
                    s.link(dve.tensor_reduce(top[:, :], bias[:, :, :], AX.X, ALU.max))
                    s.link(dve.tensor_tensor(out[:, :, :], bias[:, :, :], wide(top[:, :]), ALU.is_equal))
                    s.link(dve.tensor_tensor(out[:, :, :], out[:, :, :], k.rev[:, :, :], ALU.mult))
                    s.link(dve.tensor_reduce(top[:, :], out[:, :, :], AX.X, ALU.max))
                    s.link(dve.tensor_tensor(out[:, :, :], out[:, :, :], wide(top[:, :]), ALU.is_equal))
                    if r == 0:
                        s.link(dve.scalar_tensor_tensor(out=bias[:, :, :], in0=chosen[:, :, :], scalar=NEG,
                                                        in1=bias[:, :, :], op0=ALU.mult, op1=ALU.add))
                s.link(dve.tensor_tensor(chosen[:, :, :], chosen[:, :, :], pick[:, :, :], ALU.add))
                dve.scalar_tensor_tensor(out=dw[:, :, 0:E1], in0=prob[:, :, :], scalar=0.5, in1=chosen[:, :, :],
                                         op0=ALU.mult, op1=ALU.mult).then_inc(dw_ready, 1)
                dve.wait_ge(dw_ready, 1)

            def add_y(i, turn):
                c, e, q = i * 2 + turn // X1, turn % X1, i * (2 * X1) + turn
                dve.wait_ge(y_done, 2 + q + 1)
                for j in range(CT):
                    x = k.x[:, bass.ds(c * CT + j, 1), :]
                    dve.wait_ge(y_used, (q + 1) * CT)
                    dve.scalar_tensor_tensor(out=x, in0=y_ps[:, j:j + 1, :], 
                                             scalar=dw[:, bass.ds(c * CT + j, 1), e:e + 1], in1=x, op0=ALU.mult,
                                             op1=ALU.add).then_inc(y_used, 1)

                if e == X1 - 1 and not last:
                    dve.wait_ge(y_used, (q + 2) * CT)
                    take_stats(dve, k, c * CT, CT)

            gating(Steps(dve, steps))
            with dve.Fori(0, CHUNKS // 2) as i:
                for turn in range(2 * X1):
                    q = i * (2 * X1) + turn
                    dve.wait_ge(act_ready, 2 + q + 1)
                    dve.wait_ge(y_done, q + 1)
                    dve.scalar_tensor_tensor(out=hid[:, turn % 2, :], in0=h_ps[:, turn % 2, 1, :],
                                             scalar=1 / W_SCALE, in1=act1[:, turn % 2, :], op0=ALU.mult,
                                             op1=ALU.mult).then_inc(hid_ready, 1)
                    if turn > 0:
                        add_y(i, turn - 1)
                add_y(i, 2 * X1 - 1)

        @block.scalar
        def _(act):
            act.sem_inc(act_ready, 2)
            nd.make_pieces(act)
            act.wait_ge(lg_ready, 1)
            act.activation(el[:, :, :], lg[:, :, :], ACT.Exp, scale=1 / W_SCALE).then_inc(el_ready, 1)
            with act.Fori(0, CHUNKS // 2) as i:
                for turn in range(2 * X1):
                    q = i * (2 * X1) + turn
                    act.wait_ge(h_done, q + 1)
                    act.wait_ge(hid_ready, q + 1)
                    act.activation(act1[:, turn % 2, :], h_ps[:, turn % 2, 0, :], ACT.Silu,
                                   scale=1 / W_SCALE).then_inc(act_ready, 1)

        @block.tensor
        def _(pe):
            pe.sem_inc(y_done, 2)
            nd.turn(pe)
            pe.wait_ge(loaded, 32)

            for t in range(TILES):
                for step, (kt, px, pw) in enumerate(product(range(KD), range(2), range(2))):
                    ins = pe.matmul(lg_ps[:, t, :], nd.xT[:, px, kt, t * P:(t + 1) * P], gw[:, pw, kt, :],
                                    start=(step == 0), stop=(step == KD * 4 - 1))
            ins.then_inc(lg_done, 1)

            def first(i, turn):
                c, e = i * 2 + turn // X1, turn % X1
                pe.wait_ge(hid_ready, i * (2 * X1) + turn + 1)
                for n in range(2):
                    for step, (kt, (pw, px)) in enumerate(product(range(KD), PRODUCT)):
                        ins = pe.matmul(h_ps[:, turn % 2, n, :], w13[:, pw, kt, e, n, :],
                                        nd.xT[:, px, kt, bass.ds(c * CHUNK, CHUNK)], start=(step == 0),
                                        stop=(step == KD * len(PRODUCT) - 1))
                ins.then_inc(h_done, 1)

            def second(i, turn):
                e, q = turn % X1, i * (2 * X1) + turn
                pe.wait_ge(hid_ready, 2 + q + 1)
                pe.wait_ge(y_used, (q + 1) * CT)
                for j in range(CT):
                    ins = pe.matmul(y_ps[:, j, :], hid[:, turn % 2, j * P:(j + 1) * P], w2[:, e, :],
                                    start=True, stop=True)
                ins.then_inc(y_done, 1)

            with pe.Fori(0, CHUNKS // 2) as i:
                for turn in range(2 * X1):
                    first(i, turn)
                    if turn > 0:
                        second(i, turn - 1)
                second(i, 2 * X1 - 1)


BANKS1 = QKV1 // CHUNK
ROT = BANKS1 - 1
HPB = CHUNK // D1
PART = CHUNK // 2
PARTS = T // PART


def qkv1(nc, k, a, w_pieces):
    with ExitStack() as stack:
        m = Core(nc, stack, "qkv1_")
        w = w_pieces.pieces[:, :, :].rearrange("p e (k c) -> p e k c", k=KD)
        cos = m.sb("cos", [P, TILES, D1 // 2])
        sin = m.sb("sin", [P, TILES, D1 // 2])
        xc = m.sb("xc", [P, 2, HPB, 2, D1 // 2])
        xs = m.sb("xs", [P, 2, HPB, 2, D1 // 2])
        rot = m.sb("rot", [P, 2, HPB, D1])
        qk = m.sb("qk", [P, 2, ROT * HPB, 2, PART], F16)
        v = m.sb("v", [P, 2, 2, G1 * D1], F16)
        qkv_ps = m.ps("qkv_ps", [P, BANKS1, CHUNK])
        turned_ps = m.ps("rot_ps", [P, 2, CHUNK])
        nd = NormedPieces(m, k, turned_ps)
        loaded = m.sem("loaded")
        done = m.sem("done")
        freed = m.sem("freed")
        scaled = m.sem("scaled")
        rot_ready = m.sem("rot_ready")
        rot_turned = m.sem("rot_turned")
        qk_high = m.sem("qk_high")
        qk_low = m.sem("qk_low")
        v_high = m.sem("v_high")
        v_low = m.sem("v_low")
        stored = [m.sem("stored0"), m.sem("stored1")]
        v_stored = [m.sem("v_stored0"), m.sem("v_stored1")]
        block = stack.enter_context(nc.Block())
        PT = PART // P
        NR = PT * ROT

        @block.sync
        def _(sp):
            for b in range(2):
                sp.sem_inc(stored[b], 32 * ROT)
                sp.sem_inc(v_stored[b], 16)
            sp.dma_start(cos[:, :, :], a["cos"].rearrange("(t p) c -> p t c", p=P)).then_inc(loaded, 16)
            sp.dma_start(sin[:, :, :], a["sin"].rearrange("(t p) c -> p t c", p=P)).then_inc(loaded, 16)

            def store_heads(c, b, r):
                heads = slice(r * HPB, (r + 1) * HPB)
                sp.wait_ge(qk_low, 2 + (c + 1) * NR - (ROT - 1 - r))
                for e in range(2):
                    sp.dma_start(a["qk1_scr"][heads, :, e, bass.ds(c * PART, PART)].rearrange("h p t -> p h t"),
                                 qk[:, b, heads, e, :]).then_inc(stored[b], 16)

            with sp.Fori(0, PARTS // 2) as i:
                for b in range(2):
                    c = i * 2 + b
                    for j in range(PT):
                        if j == PT - 1:
                            for r in range(ROT - 1):
                                store_heads(c, b, r)
                        t = c * PT + j
                        sp.wait_ge(v_low, t + 1)
                        sp.dma_start(a["v1_scr"][bass.ds(t, 1), :, :, :].rearrange("o p e g -> p (o e) g"),
                                     v[:, j % 2, :, :]).then_inc(v_stored[j % 2], 16)
                    store_heads(c, b, ROT - 1)
            for b in range(2):
                sp.wait_ge(stored[b], 32 * ROT * (1 + PARTS // 2))
                sp.wait_ge(v_stored[b], 16 * (1 + TILES // 2))

        def steps():
            LAG = 2
            banks = [(j, n) for j in range(2 * PT) for n in range(BANKS1)]
            behind = [at if at[1] < ROT else None for at in banks]
            return list(zip(banks + [None] * LAG, [None] * LAG + behind))

        @block.vector
        def _(dve):
            dve.sem_inc(freed, BANKS1)
            dve.sem_inc(qk_low, 2)
            nd.norm(dve)
            dve.wait_ge(loaded, 32)
            with dve.Fori(0, PARTS // 2) as i:
                for bank, rotated in steps():
                    if bank is not None and bank[1] < ROT:
                        j, n = bank
                        t, g = i * (2 * PT) + j, j * ROT + n
                        dve.wait_ge(done, t * BANKS1 + n + 1)
                        dve.wait_ge(rot_ready, t * ROT + n + 1)
                        for tab, out in ((cos, xc), (sin, xs)):
                            dve.scalar_tensor_tensor(
                                out=out[:, g % 2, :, :, :].rearrange("p h a w -> p (h a) w"),
                                in0=qkv_ps[:, n, :].rearrange("p (h a w) -> p (h a) w", h=HPB, a=2),
                                scalar=1 / W_SCALE, in1=bcast(tab[:, bass.ds(t, 1), :], [P, 2 * HPB, D1 // 2]),
                                op0=ALU.mult, op1=ALU.mult).then_inc(scaled, 1)
                        dve.wait_ge(scaled, (t * ROT + n + 1) * 2)
                        dve.sem_inc(freed, 1)
                    elif bank is not None:
                        j, n = bank
                        t = i * (2 * PT) + j
                        dve.wait_ge(v_high, t + 1)
                        dve.scalar_tensor_tensor(out=v[:, j % 2, 1, :], in0=qkv_ps[:, n, :], scalar=1 / W_SCALE,
                                                 in1=v[:, j % 2, 0, :], op0=ALU.mult, op1=ALU.subtract) \
                           .then_inc(v_low, 1)
                        dve.wait_ge(v_low, t + 1)
                        dve.sem_inc(freed, 1)
                    if rotated is not None:
                        j, r = rotated
                        t, g = i * (2 * PT) + j, j * ROT + r
                        high, low = (qk[:, j // PT, r * HPB:(r + 1) * HPB, e, j % PT * P:(j % PT + 1) * P]
                                     for e in range(2))
                        dve.wait_ge(qk_high, t * ROT + r + 1)
                        dve.tensor_tensor(low, turned_ps[:, g % 2, :].rearrange("p (h t) -> p h t", h=HPB), high,
                                          ALU.subtract).then_inc(qk_low, 1)

        @block.gpsimd
        def _(pool):
            pool.sem_inc(rot_ready, 2)
            with pool.Fori(0, PARTS // 2) as i:
                for b in range(2):
                    for j in range(PT):
                        t = (i * 2 + b) * PT + j
                        for n in range(ROT):
                            g = j * ROT + n
                            pool.wait_ge(scaled, (t * ROT + n + 1) * 2)
                            pool.wait_ge(rot_turned, t * ROT + n + 1)
                            out = rot[:, g % 2, :, :].rearrange("p h (a w) -> p h a w", a=2)
                            pool.tensor_tensor(out[:, :, 0, :], xc[:, g % 2, :, 0, :], xs[:, g % 2, :, 1, :],
                                               ALU.subtract)
                            pool.tensor_tensor(out[:, :, 1, :], xc[:, g % 2, :, 1, :], xs[:, g % 2, :, 0, :],
                                               ALU.add).then_inc(rot_ready, 1)

        @block.scalar
        def _(act):
            nd.make_pieces(act)
            with act.Fori(0, PARTS // 2) as i:
                for bank, rotated in steps():
                    if bank is not None and bank[1] == ROT:
                        j, n = bank
                        act.wait_ge(done, (i * (2 * PT) + j) * BANKS1 + n + 1)
                        act.wait_ge(v_stored[j % 2], (i * 2 + j // 2) * 16 + 16)
                        act.activation(v[:, j % 2, 0, :], qkv_ps[:, n, :], ACT.Copy, scale=1 / W_SCALE) \
                           .then_inc(v_high, 1)
                    if rotated is not None:
                        j, r = rotated
                        g = j * ROT + r
                        if r == 0 and j % PT == 0:
                            act.wait_ge(stored[j // PT], (i + 1) * 32 * ROT)
                        act.wait_ge(rot_turned, 2 + (i * (2 * PT) + j) * ROT + r + 1)
                        act.activation(qk[:, j // PT, r * HPB:(r + 1) * HPB, 0, j % PT * P:(j % PT + 1) * P],
                                       turned_ps[:, g % 2, :].rearrange("p (h t) -> p h t", h=HPB),
                                       ACT.Copy).then_inc(qk_high, 1)

        @block.tensor
        def _(pe):
            pe.sem_inc(rot_turned, 2)
            nd.turn(pe)
            with pe.Fori(0, PARTS // 2) as i:
                for bank, rotated in steps():
                    if bank is not None:
                        j, n = bank
                        t = i * (2 * PT) + j
                        pe.wait_ge(freed, t * BANKS1 + n + 1)
                        for step, (kt, (px, pw)) in enumerate(product(range(KD), PRODUCT)):
                            ins = pe.matmul(qkv_ps[:, n, :], nd.xT[:, px, kt, bass.ds(t * P, P)],
                                            w[:, pw, kt, n * CHUNK:(n + 1) * CHUNK], start=(step == 0),
                                            stop=(step == KD * len(PRODUCT) - 1))
                        ins.then_inc(done, 1)
                    if rotated is not None:
                        j, r = rotated
                        t, g = i * (2 * PT) + j, j * ROT + r
                        pe.wait_ge(rot_ready, 2 + t * ROT + r + 1)
                        pe.wait_ge(qk_low, t * ROT + r + 1)
                        for h in range(HPB):
                            ins = pe.transpose(turned_ps[:, g % 2, h * P:(h + 1) * P], rot[:, g % 2, h, :],
                                               k.ident[:, :])
                        ins.then_inc(rot_turned, 1)


class Attn1Plan:

    units = [(c, kp) for c in range(CHUNKS) for kp in range(2 * c + 2)]
    maxima = [(qt, kc) for qt in range(TILES) for kc in range(qt // CT + 1)]
    UNITS, MAXIMA, LEAD = len(units), len(maxima), 5
    LAG = 2
    RING = 4

    @classmethod
    def maxima_at(cls, u):
        n, left = u - cls.LEAD, cls.UNITS - cls.LEAD
        return range(n * cls.MAXIMA // left, (n + 1) * cls.MAXIMA // left) if n >= 0 else range(0)

    @staticmethod
    def offset(c, kt):
        return max(0, kt - CT * c) * P

    @classmethod
    def spans(cls, u):
        c, kp = cls.units[u]
        first, second = cls.offset(c, 2 * kp), cls.offset(c, 2 * kp + 1)
        return [(slice(0, 2), first)] if first == second else [(slice(0, 1), first), (slice(1, 2), second)]


def attn1(nc, k, a, prefetch=()):
    plan = Attn1Plan
    SCALE = float(D1) ** -0.5
    PU, PM = plan.UNITS, plan.MAXIMA
    with ExitStack() as stack:
        m = Core(nc, stack, "attn1_")
        for weights in prefetch:
            weights.open(m)
        q = m.sb("q", [P, 2, 2, T], F16)
        kk = m.sb("kk", [P, 2, 2, T], F16)
        v = m.sb("v", [P, 2, TILES, VL + D1], F16)
        part = m.sb("part", [P, TILES, CHUNKS])
        mx = m.sb("mx", [P, 2, TILES])
        diag = m.sb("diag", [P, 2, T], BF16)
        prob = m.sb("prob", [P, 2, 2, CHUNK])
        high = m.sb("high", [P, plan.RING, 2, CHUNK], F16)
        low = m.sb("low", [P, plan.RING, 2, CHUNK], F16)
        inv = m.sb("inv", [P, CT])
        att = m.sb("att", [P, 2, CT, D1])
        score_ps = m.ps("score_ps", [P, 2, 2, CHUNK])
        max_ps = m.ps("max_ps", [P, 2, CHUNK])
        o_ps = m.ps("o_ps", [P, CT, 256])
        loaded = [m.sem("loaded0"), m.sem("loaded1")]
        v_loaded = [m.sem("v_loaded0"), m.sem("v_loaded1")]
        high_in = m.sem("high_in")
        blank = m.sem("blank")
        max_done = m.sem("max_done")
        max_used = m.sem("max_used")
        mx_ready = m.sem("mx_ready")
        diag_ready = m.sem("diag_ready")
        scored = m.sem("scored")
        exped = m.sem("exped")
        low_ready = m.sem("low_ready")
        weighed = m.sem("weighed")
        inv_ready = m.sem("inv_ready")
        o_used = m.sem("o_used")
        stored = [m.sem("stored0"), m.sem("stored1")]
        block = stack.enter_context(nc.Block())

        def all_passes(eng, one_pass, first=None):
            if first:
                first()
            with eng.Fori(0, H1 // 2 - 1) as i:
                for b in range(2):
                    one_pass(i * 2 + b, b, True)
            one_pass(H1 - 2, 0, True)
            one_pass(H1 - 1, 1, False)

        @block.sync
        def _(sp):
            def load(h, b):
                g = h // (H1 // G1)
                sp.dma_start(q[:, b, :, :], a["qk1_scr"][bass.ds(h, 1), :, :, :].rearrange("o p e t -> p (o e) t")) \
                  .then_inc(loaded[b], 16)
                sp.dma_start(kk[:, b, :, :], a["qk1_scr"][bass.ds(g + H1, 1), :, :, :]
                             .rearrange("o p e t -> p (o e) t")).then_inc(loaded[b], 16)
                load_v(g, b)

            def load_v(g, b):
                for e, at in ((0, 0), (1, VL)):
                    sp.dma_start(v[:, b, :, at:at + D1],
                                 a["v1_scr"][:, :, e, bass.ds(g * D1, D1)].rearrange("t p d -> p t d")) \
                      .then_inc(v_loaded[b], 16)

            def one_pass(h, b, nxt):
                if nxt:
                    sp.wait_ge(weighed, plan.RING + h * PU)
                    load(h + 1, 1 - b)
                for c in range(CHUNKS):
                    sp.wait_ge(o_used, 1 + h * CHUNKS + c + 1)
                    sp.dma_start(a["att_scr"][bass.ds(c * CT, CT), :, bass.ds(h * D1, D1)].rearrange("t p d -> p t d"),
                                 att[:, c % 2, :, :]).then_inc(stored[c % 2], 16)

            for b in range(2):
                sp.sem_inc(stored[b], 16)
            for to, head in ((q, 0), (kk, H1)):
                sp.dma_start(to[:, 0, 0, :], a["qk1_scr"][head, :, 0, :]).then_inc(high_in, 16)
            for to, head in ((q, 0), (kk, H1)):
                sp.dma_start(to[:, 0, 1, :], a["qk1_scr"][head, :, 1, :]).then_inc(loaded[0], 16)
            load_v(0, 0)
            for weights in prefetch:
                weights.load(sp)
            all_passes(sp, one_pass)
            for b in range(2):
                sp.wait_ge(stored[b], 16 * (1 + H1 * CHUNKS // 2))

        @block.gpsimd
        def _(pool):
            pool.memset(part[:, :, :], NEG).then_inc(blank, 1)
            pool.wait_ge(blank, 1)
            pool.memset(v[:, :, :, D1:VL], 1.0).then_inc(blank, 1)
            pool.wait_ge(blank, 2)

            def make_diag(h, b):
                if not isinstance(h, int) or h > 0:
                    pool.wait_ge(weighed, plan.RING + (h - 1) * PU)
                for c in range(CHUNKS):
                    pool.wait_ge(mx_ready, h * CHUNKS + c + 1)
                    pool.tensor_tensor(
                        diag[:, b, c * CHUNK:(c + 1) * CHUNK].rearrange("p (t j) -> p t j", t=CT),
                        bcast(k.minusb[:, :].rearrange("p (o j) -> p o j", o=1), [P, CT, P]),
                        bcast(mx[:, b, CT * c:CT * c + CT].rearrange("p (t o) -> p t o", o=1), [P, CT, P]),
                        ALU.mult).then_inc(diag_ready, 1)

            def one_pass(h, b, nxt):
                if nxt:
                    make_diag(h + 1, 1 - b)

            all_passes(pool, one_pass, lambda: make_diag(0, 0))
            for weights in prefetch:
                weights.split(pool)

        @block.vector
        def _(dve):
            dve.sem_inc(max_used, 2)
            dve.sem_inc(low_ready, 2)
            dve.sem_inc(o_used, 1)
            dve.wait_ge(blank, 2)

            def reduce_max(h, b, n):
                qt, kc = plan.maxima[n]
                w = min(CHUNK, (qt + 1) * P - kc * CHUNK)
                tile = h * PM + n
                dve.wait_ge(max_done, tile + 1)
                dve.tensor_reduce(part[:, qt, kc:kc + 1], max_ps[:, n % 2, 0:w], AX.X, ALU.max).then_inc(max_used, 1)
                if kc == qt // CT and qt % CT == CT - 1:
                    c = qt // CT
                    dve.wait_ge(max_used, 2 + tile + 1)
                    dve.tensor_reduce(mx[:, b, CT * c:CT * c + CT], part[:, CT * c:CT * c + CT, :], AX.X, ALU.max) \
                       .then_inc(mx_ready, 1)
                    dve.wait_ge(mx_ready, h * CHUNKS + c + 1)

            def put_out(h, c):
                dve.wait_ge(weighed, plan.RING + h * PU + (c + 1) * (c + 2))
                dve.reciprocal(inv[:, :], o_ps[:, :, D1:VO].rearrange("p t o -> p (t o)")).then_inc(inv_ready, 1)
                dve.wait_ge(inv_ready, h * CHUNKS + c + 1)
                dve.wait_ge(stored[c % 2], (h * 2 + c // 2 + 1) * 16)
                dve.tensor_tensor(att[:, c % 2, :, :], o_ps[:, :, 0:D1],
                                  bcast(inv[:, :].rearrange("p (t o) -> p t o", o=1), [P, CT, D1]), ALU.mult) \
                   .then_inc(o_used, 1)

            def one_pass(h, b, nxt):
                for u, (c, kp) in enumerate(plan.units):
                    if nxt:
                        for n in plan.maxima_at(u):
                            reduce_max(h + 1, 1 - b, n)
                    if c > 0 and kp == plan.LAG - 1:
                        put_out(h, c - 1)
                    unit = h * PU + u
                    dve.wait_ge(exped, 2 + unit + 1)
                    dve.wait_ge(weighed, unit + 1)
                    for s, off in plan.spans(u):
                        ins = dve.tensor_tensor(low[:, u % plan.RING, s, off:CHUNK], prob[:, u % 2, s, off:CHUNK],
                                                high[:, u % plan.RING, s, off:CHUNK], ALU.subtract)
                    ins.then_inc(low_ready, 1)
                put_out(h, CHUNKS - 1)

            def first():
                for n in range(PM):
                    reduce_max(0, 0, n)

            all_passes(dve, one_pass, first)

        @block.scalar
        def _(act):
            act.sem_inc(exped, 2)

            def one_pass(h, b, nxt):
                for u, (c, kp) in enumerate(plan.units):
                    unit = h * PU + u
                    act.wait_ge(scored, unit + 1)
                    act.wait_ge(weighed, unit + 1)
                    act.wait_ge(low_ready, unit + 1)
                    for s, off in plan.spans(u):
                        for out in (high[:, u % plan.RING, s, off:CHUNK], prob[:, u % 2, s, off:CHUNK]):
                            ins = act.activation(out, score_ps[:, u % 2, s, off:CHUNK], ACT.Exp, scale=SCALE)
                    ins.then_inc(exped, 1)

            all_passes(act, one_pass)

        @block.tensor
        def _(pe):
            pe.sem_inc(weighed, plan.RING)
            pe.wait_ge(blank, 2)

            def max_tile(h, b, n):
                qt, kc = plan.maxima[n]
                w = min(CHUNK, (qt + 1) * P - kc * CHUNK)
                diagonal = kc == qt // CT
                pe.wait_ge(max_used, h * PM + n + 1)
                ins = pe.matmul(max_ps[:, n % 2, 0:w], q[:, b, 0, qt * P:(qt + 1) * P],
                                kk[:, b, 0, kc * CHUNK:kc * CHUNK + w], start=True, stop=not diagonal)
                if diagonal:
                    ins = pe.matmul(max_ps[:, n % 2, w - P:w], k.identb[:, :], k.mask_qk[:, :], start=False, stop=True)
                ins.then_inc(max_done, 1)

            def score(h, b, u, s):
                c, kp = plan.units[u]
                unit = h * PU + u
                if s == 0:
                    pe.wait_ge(exped, unit + 1)
                    if kp == 0:
                        pe.wait_ge(diag_ready, h * CHUNKS + c + 1)
                kt = 2 * kp + s
                off = plan.offset(c, kt)
                out = score_ps[:, u % 2, s, off:CHUNK]
                queries = slice(c * CHUNK + off, (c + 1) * CHUNK)
                keys = slice(kt * P, (kt + 1) * P)
                diagonal = kt >= CT * c
                pe.matmul(out, kk[:, b, 0, keys], q[:, b, 0, queries], start=True, stop=False)
                pe.matmul(out, kk[:, b, 0, keys], q[:, b, 1, queries], start=False, stop=False)
                pe.matmul(out, kk[:, b, 1, keys], q[:, b, 0, queries], start=False, stop=False)
                ins = pe.matmul(out, k.onesb[:, :], diag[:, b, queries], start=False, stop=not diagonal)
                if diagonal:
                    ins = pe.matmul(score_ps[:, u % 2, s, off:off + P], k.identb[:, :], k.mask_kq[:, :],
                                    start=False, stop=True)
                if s == 1:
                    ins.then_inc(scored, 1)

            def weigh(h, b, u, s):
                c, kp = plan.units[u]
                if s == 0:
                    pe.wait_ge(low_ready, 2 + h * PU + u + 1)
                    if kp == 0:
                        pe.wait_ge(o_used, h * CHUNKS + c + 1)
                kt = 2 * kp + s
                vh, vl = v[:, b, kt, 0:VO], v[:, b, kt, VL:VL + D1]
                for t in range(plan.offset(c, kt) // P, CT):
                    ph, pl = (p[:, u % plan.RING, s, t * P:(t + 1) * P] for p in (high, low))
                    start = kt == 0 and t % 2 == 0
                    pe.matmul(o_ps[:, t, 0:VO], ph, vh, start=start, stop=False, skip_group_check=True)
                    pe.matmul(o_ps[:, t, 0:D1], ph, vl, start=False, stop=False, skip_group_check=True)
                    ins = pe.matmul(o_ps[:, t, 0:VO], pl, vh, start=False, stop=(kp == 2 * c + 1 and s == 1),
                                    skip_group_check=True)
                if s == 1:
                    ins.then_inc(weighed, 1)

            def one_pass(h, b, nxt):
                pe.wait_ge(v_loaded[b], 32 * (h // 2 + 1))
                for u in range(PU + plan.LAG):
                    if nxt and u == plan.LEAD:
                        pe.wait_ge(loaded[1 - b], 32 * ((h + 1) // 2 + 1))
                    tiles = list(plan.maxima_at(u)) if nxt and u < PU else []
                    parts = [(score, u, s) for s in range(2) if u < PU]
                    parts += [(weigh, u - plan.LAG, s) for s in range(2) if u >= plan.LAG]
                    for part, unit, s in parts:
                        part(h, b, unit, s)
                        if tiles:
                            max_tile(h + 1, 1 - b, tiles.pop(0))
                    for n in tiles:
                        max_tile(h + 1, 1 - b, n)

            def first():
                pe.wait_ge(high_in, 32)
                for n in range(PM):
                    max_tile(0, 0, n)
                pe.wait_ge(loaded[0], 32)

            all_passes(pe, one_pass, first)


def wo1(nc, k, a, wo_pieces):
    HB = H1 // 4
    with ExitStack() as stack:
        m = Core(nc, stack, "wo1_")
        wo = wo_pieces.pieces[:, :, :].rearrange("p e (h c) -> p e h c", h=H1)
        att = m.sb("att", [P, 2, H1, D1])
        attT = m.sb("attT", [P, 2, 2, H1, P], F16)
        turned_ps = m.ps("turned_ps", [P, 4, CHUNK])
        out_ps = m.ps("out_ps", [P, 2, CHUNK])
        att_in = [m.sem("att_in0"), m.sem("att_in1")]
        turned = m.sem("turned")
        high = m.sem("high")
        low = m.sem("low")
        done = m.sem("done")
        used = m.sem("used")
        block = stack.enter_context(nc.Block())

        @block.sync
        def _(sp):
            with sp.Fori(0, TILES // 2) as i:
                for b in range(2):
                    t = i * 2 + b
                    sp.wait_ge(turned, (i + 1) * 8)
                    sp.dma_start(att[:, b, :, :].rearrange("p h d -> p (h d)"),
                                 a["att_scr"][bass.ds(t, 1), :, :].rearrange("o p c -> (o p) c")) \
                      .then_inc(att_in[b], 16)

        @block.scalar
        def _(act):
            with act.Fori(0, TILES // 2) as i:
                for b in range(2):
                    t = i * 2 + b
                    act.wait_ge(used, t + 1)
                    for n in range(4):
                        act.wait_ge(turned, 8 + t * 4 + n + 1)
                        act.activation(attT[:, b, 0, n * HB:(n + 1) * HB, :].rearrange("p h t -> p (h t)"),
                                       turned_ps[:, n, :], ACT.Copy).then_inc(high, 1)

        @block.vector
        def _(dve):
            dve.sem_inc(used, 2)
            dve.sem_inc(low, 4)
            with dve.Fori(0, TILES // 2) as i:
                for b in range(2):
                    t = i * 2 + b
                    for n in range(4):
                        dve.wait_ge(high, t * 4 + n + 1)
                        dve.tensor_tensor(attT[:, b, 1, n * HB:(n + 1) * HB, :].rearrange("p h t -> p (h t)"),
                                          turned_ps[:, n, :],
                                          attT[:, b, 0, n * HB:(n + 1) * HB, :].rearrange("p h t -> p (h t)"),
                                          ALU.subtract).then_inc(low, 1)
                for b in range(2):
                    t = i * 2 + b
                    x = k.x[:, bass.ds(t, 1), :]
                    dve.wait_ge(done, t + 1)
                    dve.scalar_tensor_tensor(out=x, in0=out_ps[:, b:b + 1, 0:D], scalar=1 / W_SCALE, in1=x,
                                             op0=ALU.mult, op1=ALU.add).then_inc(used, 1)
                    dve.wait_ge(used, 2 + t + 1)
                    take_stats(dve, k, t)

        @block.tensor
        def _(pe):
            pe.sem_inc(turned, 8)

            def turn(i, b):
                t = i * 2 + b
                pe.wait_ge(att_in[b], i * 16 + 16)
                for n in range(4):
                    pe.wait_ge(low, t * 4 + n + 1)
                    for h in range(HB):
                        ins = pe.transpose(turned_ps[:, n, h * P:(h + 1) * P], att[:, b, n * HB + h, :],
                                           k.ident[:, :])
                    ins.then_inc(turned, 1)

            def multiply(i, b):
                t = i * 2 + b
                pe.wait_ge(low, 4 + (t + 1) * 4)
                pe.wait_ge(used, t + 1)
                for step, (h, (px, pw)) in enumerate(product(range(H1), PRODUCT)):
                    ins = pe.matmul(out_ps[:, b, 0:D], attT[:, b, px, h, :], wo[:, pw, h, :], start=(step == 0),
                                    stop=(step == H1 * len(PRODUCT) - 1))
                ins.then_inc(done, 1)

            with pe.Fori(0, TILES // 2) as i:
                for b in range(2):
                    turn(i, b)
                for b in range(2):
                    multiply(i, b)


def program(nc, a):
    a["q0_scr"] = nc.dram_tensor("q0_scr", (2, P, 2, T), F16, kind="Internal").ap()
    a["k0_scr"] = nc.dram_tensor("k0_scr", (G0 * D0, 2, T), F16, kind="Internal").ap()
    a["qk1_scr"] = nc.dram_tensor("qk1_scr", (H1 + G1, D1, 2, T), F16, kind="Internal").ap()
    a["v1_scr"] = nc.dram_tensor("v1_scr", (TILES, P, 2, G1 * D1), F16, kind="Internal").ap()
    a["att_scr"] = nc.dram_tensor("att_scr", (TILES, P, H1 * D1), F32, kind="Internal").ap()
    with ExitStack() as stack:
        k = Core(nc, stack)
        k.x = k.sb("x", [P, TILES, D])
        k.bn = k.sb("bn", [P, TILES, 6])
        k.rstd = k.sb("rstd", [P, TILES])
        k.shift = k.sb("shift", [P, TILES])
        k.ident = k.sb("ident", [P, P])
        k.identb = k.sb("identb", [P, P], BF16)
        k.minusb = k.sb("minusb", [P, P], BF16)
        k.mask_qk = k.sb("mask_qk", [P, P], BF16)
        k.mask_kq = k.sb("mask_kq", [P, P], BF16)
        k.ones = k.sb("ones", [P, P])
        k.onesb = k.sb("onesb", [P, P], BF16)
        k.eps = k.sb("eps", [P, 1])
        k.rev = k.sb("rev", [P, TILES, N0])
        setup(nc, k, a)
        wqkv0 = Weights(k, "wqkv0", a["wqkv0"].rearrange("(k p) c -> p k c", p=P), KD * QKV0)
        ffn0(nc, k, a, "f1_", (wqkv0,))
        with ExitStack() as inner:
            m = Core(nc, inner, "a0_")
            v_aug = m.sb("v_aug", [P, TILES, G0, VW])
            att = m.sb("att", [P, TILES, H0, D0])
            qs = m.sb("qs", [P, H0, T], F16)
            ks = m.sb("ks", [P, G0, T], F16)
            qkv0(nc, k, a, wqkv0, v_aug, qs, ks)
            attn0(nc, k, v_aug, qs, ks, att)
            wo0(nc, k, a, att)
        gw = Weights(k, "gw", a["gate1_w"].rearrange("(k p) c -> p k c", p=P), KD * E1)
        w13 = Weights(k, "w13", a["w13"].rearrange("(k p) c -> p k c", p=P), KD * X1 * 2 * I1)
        wqkv = Weights(k, "wqkv", a["wqkv1"].rearrange("(k p) c -> p k c", p=P), KD * QKV1)
        wo = Weights(k, "wo", a["wo1"].rearrange("(h p) c -> p h c", p=P), H1 * D)
        ffn0(nc, k, a, "f3_", (gw, w13))
        ffn1(nc, k, a, "f4_", w13, gw, (wqkv,))
        qkv1(nc, k, a, wqkv)
        attn1(nc, k, a, (wo,))
        wo1(nc, k, a, wo)
        ffn1(nc, k, a, "f6_", w13, gw, last=True)


def laid_out(inputs):
    import numpy as np

    i = {n: np.asarray(v) for n, v in inputs.items()}
    c = np.ascontiguousarray

    def on_all(row):
        return c(np.broadcast_to(row[None, :], (P, row.shape[0])))

    def columns(w):
        return np.transpose(w, (1, 0, 2)).reshape(D, -1)

    smd = i["L0_ffn_select_mean_diff"].T
    w1, w2, w3 = (np.concatenate([i[f"L1_ffn_W{n}"], i[f"L1_ffn_Ws{n}"][None]], 0) for n in (1, 2, 3))
    freqs = np.float32(1.0) / np.power(np.float32(10000.0), np.arange(0, D1, 2, dtype=np.float32) / np.float32(D1))
    angle = np.arange(T, dtype=np.float32)[:, None] * freqs[None, :]
    cos, sin = np.cos(angle), np.sin(angle)
    return {
        "x": i["L0_attn_x"],
        "ffn0_w": c(np.concatenate([columns(i["L0_ffn_select_weight"]), columns(i["L0_ffn_lora_update"]), smd], 1)),
        "ffn0_other": c(np.concatenate([np.repeat(smd, S0, 1), np.repeat(i["L0_ffn_debias_w"].T, S0, 1), smd], 1)),
        "ffn0_w2": c(np.concatenate([np.transpose(i["L0_ffn_lora_degen"], (0, 2, 1)).reshape(-1, D),
                                     i["L0_ffn_bias_w"]], 0)),
        "ffn0_center": on_all(i["L0_ffn_imp_center"]),
        "ffn0_slope": on_all(i["L0_ffn_imp_slope"]),
        "wqkv0": c(np.concatenate([i["L0_attn_Wq"], i["L0_attn_Wk"], i["L0_attn_Wv"]], 1)), "wo0": i["L0_attn_Wo"],
        "bq0": c(i["L0_attn_bq"].reshape(2, P).T), "bk0": i["L0_attn_bk"], "bv0": on_all(i["L0_attn_bv"]),
        "bo0": on_all(i["L0_attn_bo"]),
        "gate1_w": c(i["L1_ffn_gate_w"].T), "gate1_b": on_all(i["L1_ffn_gate_b"]),
        "w13": c(np.stack([w1, w3], 1).reshape(X1 * 2 * I1, D).T), "w2": c(np.transpose(w2, (0, 2, 1))),
        "wqkv1": i["L1_attn_Wqkv"], "wo1": i["L1_attn_Wo"], "cos": cos, "sin": sin,
    }


def kernel(**inputs):
    import concourse.bacc as bacc
    from concourse.bass_utils import run_bass_kernel_spmd

    nc = bacc.Bacc("TRN2", target_bir_lowering=False, num_devices=1)
    arrays, a = {}, {}
    for name, value in laid_out(inputs).items():
        arrays["in_" + name] = value
        a[name] = nc.dram_tensor("in_" + name, value.shape, mybir.dt.from_np(value.dtype), kind="ExternalInput").ap()
    a["out"] = nc.dram_tensor("out", (1, T, D), F32, kind="ExternalOutput").ap()
    program(nc, a)
    return run_bass_kernel_spmd(nc, [arrays], core_ids=[0]).results[0]["out"]
```
